# Optimizing a Trainium2 kernel written in Bass

```python
import numpy as np
import jax
import jax.numpy as jnp

def _softmax(x, axis=-1):
    return jax.nn.softmax(x, axis=axis)

def _gelu(x):
    return jax.nn.gelu(x, approximate=True)

def _silu(x):
    return jax.nn.silu(x)

def _sigmoid(x):
    return jax.nn.sigmoid(x)

def _layernorm(x, axis=-1, eps=1e-05):
    m = jnp.mean(x, axis=axis, keepdims=True)
    v = jnp.var(x, axis=axis, keepdims=True)
    return (x - m) / jnp.sqrt(v + eps)

def _scatter_add(tgt, idx, src, axis=0):
    return tgt.at[idx].add(src)

def _segment_sum(src, seg, n):
    return jax.ops.segment_sum(src, seg, n)
kernel_name = 'mk_conv_preact_d2_conv_nchw768_r2_ae757d'

def setup_inputs(seed: int=0):
    np.random.seed(seed)
    _w = jnp.asarray

    def _rec_inputs():
        import jax
        import jax.numpy as jnp
        _gk = jax.random.key(seed)
        x = -0.0001538 + 1 * jax.random.normal(jax.random.fold_in(_gk, 1), (8, 384, 32, 32), jnp.float32)
        return x
    x = _rec_inputs()

    def _L0_conv_setup():
        import jax, jax.numpy as jnp
        import numpy as np
        DIM = 384
        NUM_HEADS = 8
        HEAD_DIM = DIM // NUM_HEADS
        SCALE = HEAD_DIM ** (-0.5)
        key = jax.random.key(seed)
        k1, k2, k3, k4 = jax.random.split(key, 4)
        B, C, H, W = (8, DIM, 32, 32)
        x = jax.random.normal(k1, (B, C, H, W), dtype=jnp.float32)
        w_qkv = jax.random.normal(k2, (3 * DIM, DIM), dtype=jnp.float32) * DIM ** (-0.5)
        w_proj = jax.random.normal(k3, (DIM, DIM), dtype=jnp.float32) * DIM ** (-0.5)
        b_proj = jax.random.normal(k4, (DIM,), dtype=jnp.float32) * 0.02
        return {'x': x, 'w_qkv': w_qkv, 'w_proj': w_proj, 'b_proj': b_proj}
    _L0_conv_all = _L0_conv_setup()
    _L0_conv_in = {k: v for k, v in _L0_conv_all.items() if k in ('w_qkv', 'w_proj', 'b_proj')}
    del _L0_conv_all

    def _L1_conv_setup():
        import jax, jax.numpy as jnp
        import numpy as np
        B, C, H, W = (8, 384, 32, 32)
        CO, KS = (384, 3)

        def _conv(x, w, b):
            y = jax.lax.conv_general_dilated(x, w, (1, 1), [(1, 1), (1, 1)], dimension_numbers=('NCHW', 'OIHW', 'NCHW'))
            return y + b[None, :, None, None]

        def _deform_conv(x, offset, mask, w, b):
            b_, c_, h_, w_ = x.shape
            co, _, kh, kw = w.shape
            K = kh * kw
            off = offset.reshape(b_, K, 2, h_, w_)
            ky = (jnp.arange(K) // kw).astype(x.dtype)
            kx = (jnp.arange(K) % kw).astype(x.dtype)
            py = off[:, :, 0] + (jnp.arange(h_, dtype=x.dtype) - 1.0)[None, None, :, None] + ky[None, :, None, None]
            px = off[:, :, 1] + (jnp.arange(w_, dtype=x.dtype) - 1.0)[None, None, None, :] + kx[None, :, None, None]
            y0 = jnp.floor(py)
            x0 = jnp.floor(px)
            wy1 = py - y0
            wx1 = px - x0
            y0i = y0.astype(jnp.int32)
            x0i = x0.astype(jnp.int32)

            def corner(yi, xi, wt):
                valid = (yi >= 0) & (yi < h_) & (xi >= 0) & (xi < w_)
                yc = jnp.clip(yi, 0, h_ - 1)
                xc = jnp.clip(xi, 0, w_ - 1)
                g = jax.vmap(lambda im, yy, xx: im[:, yy, xx])(x, yc, xc)
                return g * (wt * valid)[:, None]
            p = corner(y0i, x0i, (1.0 - wy1) * (1.0 - wx1) * mask) + corner(y0i, x0i + 1, (1.0 - wy1) * wx1 * mask) + corner(y0i + 1, x0i, wy1 * (1.0 - wx1) * mask) + corner(y0i + 1, x0i + 1, wy1 * wx1 * mask)
            out = jnp.einsum('bckhw,ock->bohw', p, w.reshape(co, c_, K))
            return out + b[None, :, None, None]
        key = jax.random.key(seed)
        ks = jax.random.split(key, 6)
        x = jax.random.normal(ks[0], (B, C, H, W), jnp.float32)
        proj_w = jax.random.normal(ks[1], (CO, C, KS, KS), jnp.float32) * 0.02
        proj_b = jnp.zeros((CO,), jnp.float32)
        off_w = jax.random.normal(ks[2], (2 * KS * KS, C, KS, KS), jnp.float32) * 0.01
        off_b = jax.random.normal(ks[3], (2 * KS * KS,), jnp.float32) * 0.01
        mask_w = jax.random.normal(ks[4], (KS * KS, C, KS, KS), jnp.float32) * 0.01
        mask_b = jax.random.normal(ks[5], (KS * KS,), jnp.float32) * 0.01
        gamma = jnp.ones((CO,), jnp.float32)
        beta = jnp.zeros((CO,), jnp.float32)
        return {'x': x, 'proj_w': proj_w, 'proj_b': proj_b, 'off_w': off_w, 'off_b': off_b, 'mask_w': mask_w, 'mask_b': mask_b, 'gamma': gamma, 'beta': beta}
    _L1_conv_all = _L1_conv_setup()
    _L1_conv_in = {k: v for k, v in _L1_conv_all.items() if k in ('proj_w', 'proj_b', 'off_w', 'off_b', 'mask_w', 'mask_b', 'gamma', 'beta')}
    del _L1_conv_all
    return {'x': x, 'L0_conv_w_qkv': _L0_conv_in['w_qkv'], 'L0_conv_w_proj': _L0_conv_in['w_proj'], 'L0_conv_b_proj': _L0_conv_in['b_proj'], 'L1_conv_proj_w': _L1_conv_in['proj_w'], 'L1_conv_proj_b': _L1_conv_in['proj_b'], 'L1_conv_off_w': _L1_conv_in['off_w'], 'L1_conv_off_b': _L1_conv_in['off_b'], 'L1_conv_mask_w': _L1_conv_in['mask_w'], 'L1_conv_mask_b': _L1_conv_in['mask_b'], 'L1_conv_gamma': _L1_conv_in['gamma'], 'L1_conv_beta': _L1_conv_in['beta']}

def reference(x, L0_conv_w_qkv, L0_conv_w_proj, L0_conv_b_proj, L1_conv_proj_w, L1_conv_proj_b, L1_conv_off_w, L1_conv_off_b, L1_conv_mask_w, L1_conv_mask_b, L1_conv_gamma, L1_conv_beta):
    import jax
    import jax.numpy as jnp

    def _L0_conv_ref(x, w_qkv, w_proj, b_proj):
        import jax, jax.numpy as jnp
        import numpy as np
        DIM = 384
        NUM_HEADS = 8
        HEAD_DIM = DIM // NUM_HEADS
        SCALE = HEAD_DIM ** (-0.5)
        B, C, H, W = x.shape
        N = H * W
        nh, hd = (NUM_HEADS, HEAD_DIM)
        tokens = x.reshape(B, C, N).transpose(0, 2, 1)
        qkv = tokens @ w_qkv.T
        qkv = qkv.reshape(B, N, 3, nh, hd).transpose(2, 0, 3, 1, 4)
        q, k, v = (qkv[0], qkv[1], qkv[2])
        attn = jnp.einsum('bhnd,bhmd->bhnm', q, k) * SCALE
        attn = jax.nn.softmax(attn, axis=-1)
        out = jnp.einsum('bhnm,bhmd->bhnd', attn, v)
        out = out.transpose(0, 2, 1, 3).reshape(B, N, C)
        out = out @ w_proj.T + b_proj
        return out.transpose(0, 2, 1).reshape(B, C, H, W)

    def _L1_conv_ref(x, proj_w, proj_b, off_w, off_b, mask_w, mask_b, gamma, beta):
        import jax, jax.numpy as jnp
        import numpy as np
        B, C, H, W = (8, 384, 32, 32)
        CO, KS = (384, 3)

        def _conv(x, w, b):
            y = jax.lax.conv_general_dilated(x, w, (1, 1), [(1, 1), (1, 1)], dimension_numbers=('NCHW', 'OIHW', 'NCHW'))
            return y + b[None, :, None, None]

        def _deform_conv(x, offset, mask, w, b):
            b_, c_, h_, w_ = x.shape
            co, _, kh, kw = w.shape
            K = kh * kw
            off = offset.reshape(b_, K, 2, h_, w_)
            ky = (jnp.arange(K) // kw).astype(x.dtype)
            kx = (jnp.arange(K) % kw).astype(x.dtype)
            py = off[:, :, 0] + (jnp.arange(h_, dtype=x.dtype) - 1.0)[None, None, :, None] + ky[None, :, None, None]
            px = off[:, :, 1] + (jnp.arange(w_, dtype=x.dtype) - 1.0)[None, None, None, :] + kx[None, :, None, None]
            y0 = jnp.floor(py)
            x0 = jnp.floor(px)
            wy1 = py - y0
            wx1 = px - x0
            y0i = y0.astype(jnp.int32)
            x0i = x0.astype(jnp.int32)

            def corner(yi, xi, wt):
                valid = (yi >= 0) & (yi < h_) & (xi >= 0) & (xi < w_)
                yc = jnp.clip(yi, 0, h_ - 1)
                xc = jnp.clip(xi, 0, w_ - 1)
                g = jax.vmap(lambda im, yy, xx: im[:, yy, xx])(x, yc, xc)
                return g * (wt * valid)[:, None]
            p = corner(y0i, x0i, (1.0 - wy1) * (1.0 - wx1) * mask) + corner(y0i, x0i + 1, (1.0 - wy1) * wx1 * mask) + corner(y0i + 1, x0i, wy1 * (1.0 - wx1) * mask) + corner(y0i + 1, x0i + 1, wy1 * wx1 * mask)
            out = jnp.einsum('bckhw,ock->bohw', p, w.reshape(co, c_, K))
            return out + b[None, :, None, None]
        h, w = (x.shape[-2], x.shape[-1])
        max_off = float(min(h, w) // 4)
        offset = jnp.clip(_conv(x, off_w, off_b), -max_off, max_off)
        mask = 2.0 * jax.nn.sigmoid(_conv(x, mask_w, mask_b))
        y = _deform_conv(x, offset, mask, proj_w, proj_b)
        mean = y.mean(axis=(0, 2, 3))
        var = y.var(axis=(0, 2, 3))
        yn = (y - mean[None, :, None, None]) * jax.lax.rsqrt(var + 1e-05)[None, :, None, None]
        yn = yn * gamma[None, :, None, None] + beta[None, :, None, None]
        return jax.nn.gelu(yn, approximate=False)

    def _gn(v, G=32, eps=1e-05):
        B_, C_, H_, W_ = v.shape
        g = v.reshape(B_, G, C_ // G, H_, W_)
        m = jnp.mean(g, axis=(2, 3, 4), keepdims=True)
        s = jnp.var(g, axis=(2, 3, 4), keepdims=True)
        return ((g - m) / jnp.sqrt(s + eps)).reshape(v.shape)

    def _ln_c(v, eps=1e-06):
        m = jnp.mean(v, axis=1, keepdims=True)
        s = jnp.var(v, axis=1, keepdims=True)
        return (v - m) / jnp.sqrt(s + eps)

    def _ln_t(v, eps=1e-05):
        m = jnp.mean(v, axis=-1, keepdims=True)
        s = jnp.var(v, axis=-1, keepdims=True)
        return (v - m) / jnp.sqrt(s + eps)

    def _to_tokens(v):
        B_, C_, H_, W_ = v.shape
        return v.reshape(B_, C_, H_ * W_).transpose(0, 2, 1)

    def _from_tokens(t, like):
        B_, C_, H_, W_ = like.shape
        return t.transpose(0, 2, 1).reshape(B_, C_, H_, W_)
    x = x + _L0_conv_ref(_gn(x), L0_conv_w_qkv, L0_conv_w_proj, L0_conv_b_proj)
    x = x + _L1_conv_ref(_gn(x), L1_conv_proj_w, L1_conv_proj_b, L1_conv_off_w, L1_conv_off_b, L1_conv_mask_w, L1_conv_mask_b, L1_conv_gamma, L1_conv_beta)
    return x

_drawn_inputs = setup_inputs


def setup_inputs(seed=0):
    import zlib

    import numpy as np

    out = dict(_drawn_inputs(seed))
    spreads = {'L1_conv_proj_b': (0.0, 0.8), 'L1_conv_gamma': (1.0, 0.2), 'L1_conv_beta': (0.0, 0.1)}
    factors = {'L0_conv_b_proj': 2.715, 'L1_conv_off_b': 3.239}
    for name, (base, spread) in spreads.items():
        noise = np.random.default_rng([zlib.crc32(name.encode()), seed]).standard_normal(out[name].shape)
        drawn = base * np.exp(spread * noise) if base else spread * noise
        out[name] = jnp.asarray(drawn.astype(out[name].dtype))
    for name, factor in factors.items():
        out[name] = (out[name] * factor).astype(out[name].dtype)
    return out
```

```python
import concourse.bass as bass
from concourse import mybir
from contextlib import ExitStack
import numpy as np

BATCH, CH, HW, PIX = 8, 384, 32, 1024
PART = 128
CT = CH // PART
HEADS, HD = 8, 48
PAIRS = HEADS // 2
HEAD_B = 64
PAIR_ROWS = HEAD_B + HD
GN_GROUPS = 32
GN_EPS, BN_EPS = 1e-5, 1e-5
TAPS = 9
MAX_OFF = HW // 4
OFF_CH = 3 * TAPS
ROWS = OFF_CH + 1
LO_ROW = 32
HALF = 512
QT = PIX // PART
TILE_ROWS = HW // QT
VCOL = 2 * HD + 1
SCALE = HD ** -0.5
W_SCALE = 256.0
W_UN = 1.0 / W_SCALE
MAX_ROW, MAX_UNIT = HD, 16.0
PAD = HW + 2
MCOLS = (TILE_ROWS + 2 * MAX_OFF) * HW


def tap_segments(j, ky):
    first = max(0, TILE_ROWS * j + 1 - ky - MAX_OFF)
    last = min(HW - 1, TILE_ROWS * j + TILE_ROWS + MAX_OFF - ky)
    lo, hi = first * HW, (last + 1) * HW
    segs = []
    if lo < HALF:
        segs.append((lo, min(hi, HALF)))
    if hi > HALF:
        segs.append((max(lo, HALF), hi))
    return segs


def chunk_schedule():
    pre = [("gn", 0, "D")]
    pre += [(("v", n), 0, "AD") for n in range(QT)]

    def pair_prep(i):
        out = [(("qk", i, w, h), 0, "AD") for w in range(2) for h in range(2)]
        out += [(("max", i, n), 0, "D") for n in range(4 * QT)]
        return out + [(("maxT", i), 0, "A")]

    for i in range(PAIRS):
        pre += pair_prep(i)
    pre += [(("oT", t, h), 0, "AD") for t in range(CT) for h in range(2)]
    pre += [(("proj", t, h), 0, "D") for t in range(CT) for h in range(2)]
    pre += [("gn2", 0, "D")]
    pre += [(("conv", h), 0, "A") for h in range(2)]
    pre += [(("comb", h), 0, "D") for h in range(2)]
    prep = [(("pos", h), "A") for h in range(2)] + [(("mask", h), "D") for h in range(2)] \
        + [(("hx", h), "A") for h in range(2)]
    pre += [(("pre",) + n, 0, r) for n, r in prep]
    tail = [(("next", "hy", 0), 0, "D"), (("next", "z"), 0, "AD")]
    pre += tail
    loop = []
    for ky in range(3):
        nky = (ky + 1) % 3
        for j in range(QT):
            last = j == QT - 1
            hj, hky = (0, nky) if last else (j + 1, ky)
            for n, _ in enumerate(tap_segments(hj, hky)):
                loop.append((("hy", ky, j, n), 0, "D"))
            loop.append((("z", ky, j), 0, "AD"))
            for n, r in PREP_AT.get(j, []):
                loop.append((("prep", ky) + n, 0, r))
    return pre, loop


PREP_AT = {0: [(("pos", 0), "A")], 1: [(("pos", 1), "A")], 2: [(("mask", 0), "D")], 3: [(("mask", 1), "D")],
           4: [(("hx", 0), "A")], 5: [(("hx", 1), "A")]}
PRE, LOOP = chunk_schedule()
if len(PRE) % 2:
    PRE = [("skip", 0, "")] + PRE
if len(LOOP) % 2:
    raise ValueError("loop's chunks must pair up")
INDEX = {n: g for g, (n, _, _) in enumerate(PRE)}
LINDEX = {n: g for g, (n, _, _) in enumerate(LOOP)}
NPRE, NLOOP = len(PRE), len(LOOP)
KX = 3


def reads(table, upto, who):
    return sum(who in r for _, _, r in table[:upto])


PRE_A, PRE_D = reads(PRE, NPRE, "A"), reads(PRE, NPRE, "D")
LOOP_A, LOOP_D = reads(LOOP, NLOOP, "A"), reads(LOOP, NLOOP, "D")
NSKIP = sum(n == "skip" for n, _, _ in PRE)
PER_FULL = NPRE - NSKIP + KX * NLOOP
PER_A, PER_D = PRE_A + KX * LOOP_A, PRE_D + KX * LOOP_D
STEPS = HEADS * QT
TAP_STEPS = TAPS * QT
POOL_STEPS = [s for s in range(STEPS) if s % 2 == 1]
DVE_STEPS = [s for s in range(STEPS) if s % 2 == 0]
NEXT_AT = [[] for _ in range(2 * QT)]
for _n in range(4):
    NEXT_AT[_n // 2].append(("qk", _n // 2, _n % 2))
for _n in range(4 * QT):
    NEXT_AT[2 + _n * 12 // (4 * QT)].append(("max", _n))
NEXT_AT[14] = [("maxT",)]


def next_chunks(i, s16):
    if i + 1 >= PAIRS:
        return []
    return [(n[0], i + 1) + n[1:] for n in NEXT_AT[s16]]


DVE_LINKS = 60
PRE_SEGS = len(tap_segments(0, 0))
LOOP_SEGS = sum(n[0] == "hy" for n, _, _ in LOOP)
PER_SEGS = PRE_SEGS + KX * LOOP_SEGS
PER_SAMPLED = TAP_STEPS + 1


def build(nc, x, wqk, wv, wp, wd, wc, bias_p, bias_c, bias_d, gamma, beta, c16, c32, out, x1_d, y_d):
    fp32, fp16, bf16 = mybir.dt.float32, mybir.dt.float16, mybir.dt.bfloat16
    ALU, ACT, AX = mybir.AluOpType, mybir.ActivationFunctionType, mybir.AxisListType
    ctx = ExitStack()
    with ctx:
        def sb(name, shape, dt):
            return ctx.enter_context(nc.sbuf_tensor(name, shape, dt))

        def sem(name):
            return ctx.enter_context(nc.semaphore(name))

        X1 = sb("X1", [128, CT, PIX], fp32)
        XN = sb("XN", [128, CT, PIX], fp32)
        XHL = sb("XHL", [128, 2, CT, PIX], fp16)
        XP = sb("XP", [128, 2, CT, PAD, PAD], fp16)
        QS = sb("QS", [128, 2, 2, PIX], fp16)
        KS = sb("KS", [128, 2, 2, PIX], fp16)
        KL = sb("KL", [128, 2, 2, PIX], fp16)
        VS = sb("VS", [128, QT, HEADS, VCOL + 1], fp16)
        P32 = sb("P32", [128, 3, PIX], fp32)
        PL = sb("PL", [128, 3, PIX], fp16)
        TAPW = CT * CH
        WALL = sb("WALL", [128, (2 * TAPS + 2) * TAPW], fp16)
        WQK = sb("WQK", [128, 2, CT, 2 * PAIRS, PAIR_ROWS], fp16)
        WP = sb("WP", [128, 2, CT, CH], fp16)
        WC = sb("WC", [128, CT * TAPS, 2 * OFF_CH], fp16)
        C16 = sb("C16", [128, 29 * 128 + PIX], fp16)
        C32 = sb("C32", [128, 128 + 128 + ROWS + 8], fp32)
        BIAS = sb("BIAS", [128, 4, CT], fp32)
        CBIAS = sb("CBIAS", [128, 1], fp32)
        MXP = sb("MXP", [128, 2 * QT, 2], fp32)
        MX = sb("MX", [128, 2 * QT], fp32)
        MR = sb("MR", [2 * QT, 128], fp16)
        OLO = sb("OLO", [128, 2, 4, HD], fp32)
        OSUM = sb("OSUM", [128, 2, 4, HD], fp32)
        ORS = sb("ORS", [128, 2, 4], fp32)
        ST6 = sb("ST6", [128, 6, 6], fp32)
        MV = sb("MV", [128, 2], fp32)
        GM = sb("GM", [128, 8], fp32)
        BST = sb("BST", [128, CT, 2 * BATCH, 6], fp32)
        BMV = sb("BMV", [128, CT, 2], fp32)
        BSC = sb("BSC", [128, 4, CT], fp32)
        CV = P32[:, 0, :]
        POSM = P32[:, 1, :]
        PTMP = P32[:, 2, :]
        POSS = sb("POSS", [128, PIX], fp16)
        TV = P32
        H16 = PL[:, 0, :]
        HL = sb("HL", [128, 3, PIX], fp16)
        HX = VS[:, :, :, :].rearrange("p a h c -> p (a h c)")[:, 0:6 * PIX].bitcast(fp32).rearrange("p (k n) -> p k n", k=3)
        M32 = sb("M32", [128, 2, MCOLS], fp32)
        MHL = sb("MHL", [128, 2, 2, MCOLS], fp16)
        ZHL = sb("ZHL", [128, 2, 2, CH], fp16)

        WDH, WDL, WVO = 0, TAPS * TAPW, 2 * TAPS * TAPW
        SELP, SELM, SELY, SELX, BASE = 0, 1280, 2560, 3584, 3712
        IDENT, GMAT, CMB, COL = C32[:, 0:128], C32[:, 128:256], C32[:, 256:256 + ROWS], 256 + ROWS
        IS_POS, TWO_MASK, NEG_POS, NEG_LO, MHALF = [C32[:, COL + n:COL + n + 1] for n in range(5)]

        G = [ctx.enter_context(nc.psum_tensor(f"G{n}", [128, HALF], fp32)) for n in range(2)]
        R6 = ctx.enter_context(nc.psum_tensor("R6", [128, 6, HALF], fp32))
        ST = [R6[:, 2 * n:2 * n + 2, :].rearrange("p a n -> p (a n)") for n in range(2)]
        O = [R6[:, 4 + n, 0:4 * VCOL] for n in range(2)]

        consts_in = sem("consts_in")
        maxunit_in = sem("maxunit_in")
        stage_in = [sem(f"stage_in{n}") for n in range(2)]
        cleared = sem("cleared")
        ones_ready = sem("ones_ready")
        w_high = sem("w_high")
        w_low = sem("w_low")
        x_in = sem("x_in")
        chunk_full = sem("chunk_full")
        act_read = sem("act_read")
        dve_read = sem("dve_read")
        gn_stats = sem("gn_stats")
        gn_var = sem("gn_var")
        gn_rstd = sem("gn_rstd")
        gn_shift = sem("gn_shift")
        xn_ready = sem("xn_ready")
        x_split = sem("x_split")
        x_biased = sem("x_biased")
        xph_ready = sem("xph_ready")
        xpl_ready = sem("xpl_ready")
        max_ready = sem("max_ready")
        maxrow_in = sem("maxrow_in")
        scores_full = sem("scores_full")
        p_exp = sem("p_exp")
        p_low_dve = sem("p_low_dve")
        p_low_pool = sem("p_low_pool")
        pv_done = sem("pv_done")
        o_low = sem("o_low")
        o_norm = sem("o_norm")
        x1_out = sem("x1_out")
        z_exp = sem("z_exp")
        pos_ready = sem("pos_ready")
        hat_ready = sem("hat_ready")
        hl_ready = sem("hl_ready")
        m_high = sem("m_high")
        m_low = sem("m_low")
        sampled = sem("sampled")
        y_ready = sem("y_ready")
        y_stats = sem("y_stats")
        y_out = sem("y_out")
        dve_chain = sem("dve_chain")
        bn_var = sem("bn_var")
        bn_rstd = sem("bn_rstd")
        bn_ready = sem("bn_ready")
        yf_in = [sem(f"yf_in{n}") for n in range(3)]
        xf_in = [sem(f"xf_in{n}") for n in range(3)]
        gelu_done = sem("gelu_done")
        added = sem("added")
        out_done = [sem(f"out_done{n}") for n in range(3)]

        stage = [X1[:, :, :].rearrange("p t n -> p (t n)"), XN[:, :, :].rearrange("p t n -> p (t n)")]
        pieces = []
        for t in range(CT):
            n = 2 * PAIRS * 2 * HD
            dst = [[WQK[:, hl, t, :, half * HEAD_B:half * HEAD_B + HD] for hl in range(2)] for half in range(2)]
            pieces.append((wqk[:, t * n:(t + 1) * n], n, dst))
        pieces.append((wv, TAPW, [[WALL[:, WVO + hl * TAPW:WVO + (hl + 1) * TAPW] for hl in range(2)]]))
        pieces.append((wp, TAPW, [[WP[:, hl, :, :].rearrange("p t n -> p (t n)") for hl in range(2)]]))
        pieces.append((wc, CT * TAPS * OFF_CH, [[WC[:, :, hl * OFF_CH:(hl + 1) * OFF_CH] for hl in range(2)]]))
        for n in range(TAPS // 1):
            pieces.append((wd[:, n * TAPW:(n + 1) * TAPW], TAPW,
                           [[WALL[:, o + n * TAPW:o + (n + 1) * TAPW] for o in (WDH, WDL)]]))

        def staged(n, k):
            src, cols, dst = pieces[n]
            s = stage[n % 2][:, 0:cols]
            if len(dst) == 2:
                return s.rearrange("p (m a d) -> p m a d", a=2, d=HD)[:, :, k, :]
            if dst[0][0].shape[1:] != s.shape[1:]:
                return s.rearrange("p (m d) -> p m d", d=OFF_CH)
            return s

        NP = len(pieces)
        ring = [X1[:, :, :].rearrange("p t n -> p (t n)"), XN[:, :, :].rearrange("p t n -> p (t n)"),
                XHL[:, :, :, :].rearrange("p a t n -> p (a t n)").bitcast(fp32)]

        def YF(n):
            return WALL[:, (n % 3) * 2 * CT * PIX:(n % 3 + 1) * 2 * CT * PIX].bitcast(fp32)

        def XF(n):
            return ring[n % 3]

        ON = XN[:, :, :].rearrange("p t n -> p (t n)").rearrange("p (q c) -> p q c", q=QT)

        def high_view(s):
            return P32[:, s % 3, :].bitcast(bf16).rearrange("p (n two) -> p n two", two=2)[:, :, 1]

        def full_at(name, b):
            return b * PER_FULL + (INDEX[name] + 1 - NSKIP)

        def act_at(name, b):
            return b * PER_A + reads(PRE, INDEX[name] + 1, "A")

        def dve_at(name, b):
            return b * PER_D + reads(PRE, INDEX[name] + 1, "D")

        block = ctx.enter_context(nc.Block())

        @block.sync
        def _(sp):
            sp.dma_start(C16[:, :], c16).then_inc(consts_in, 16)
            sp.dma_start(C32[:, :], c32).then_inc(consts_in, 16)
            for n, a in enumerate((bias_p, bias_d, gamma, beta)):
                sp.dma_start(BIAS[:, n, :], a).then_inc(consts_in, 16)
            sp.wait_ge(cleared, 1)
            sp.dma_start(CBIAS[0:OFF_CH, :], bias_c).then_inc(consts_in, 16)
            for pp in range(2):
                for hd in range(2):
                    sp.dma_start(KL[MAX_ROW:MAX_ROW + 1, pp, hd, :],
                                 c16[127:128, BASE:BASE + PIX]).then_inc(maxunit_in, 16)
            for n in range(NP):
                if n >= 2:
                    sp.wait_ge(w_low, n - 1)
                sp.dma_start(stage[n % 2][:, 0:pieces[n][1]], pieces[n][0]).then_inc(stage_in[n % 2], 16)
            sp.wait_ge(w_low, NP)

            def load_x(b):
                sp.dma_start(X1[:, :, :].rearrange("p t n -> p (t n)"),
                             x[bass.ds(b, 1), :, :].rearrange("a p n -> (a p) n")).then_inc(x_in, 16)

            def batch(b):
                for i in range(PAIRS):
                    sp.wait_ge(act_read, act_at(("maxT", i), b))
                    for hd in range(2):
                        sp.dma_start(QS[MAX_ROW:MAX_ROW + 1, i % 2, hd, :],
                                     MR[hd * QT:(hd + 1) * QT, :]).then_inc(maxrow_in, 16)
                sp.wait_ge(dve_read, dve_at(("proj", CT - 1, 1), b))
                sp.dma_start(x1_d[bass.ds(b, 1), :, :].rearrange("a p n -> (a p) n"),
                             X1[:, :, :].rearrange("p t n -> p (t n)")).then_inc(x1_out, 16)
                sp.wait_ge(xn_ready, b * 6 + 6)
                sp.wait_ge(x1_out, b * 16 + 16)

            load_x(0)
            if BATCH > 1:
                with sp.Fori(0, BATCH - 1) as b:
                    batch(b)
                    load_x(b + 1)
            batch(BATCH - 1)
            sp.wait_ge(y_out, BATCH * 16)
            sp.wait_ge(y_stats, BATCH)
            for n in range(BATCH):
                if n >= 3:
                    sp.wait_ge(out_done[n % 3], 16 * (n // 3))
                sp.dma_start(YF(n), y_d[n, :, :]).then_inc(yf_in[n % 3], 16)
                sp.dma_start(XF(n), x1_d[n, :, :]).then_inc(xf_in[n % 3], 16)

        @block.gpsimd
        def _(pool):
            for t in (QS, KS, KL):
                pool.memset(t[:, :, :, :].rearrange("p a b n -> p (a b n)"), 0.0)
            pool.memset(XP[:, :, :, :, :].rearrange("p a t h w -> p (a t h w)"), 0.0)
            pool.memset(WQK[:, :, :, :, :].rearrange("p a t m n -> p (a t m n)"), 0.0)
            pool.memset(POSS[:, :], 0.0)
            pool.memset(CBIAS[:, :], 0.0).then_inc(cleared, 1)
            with pool.Fori(0, BATCH) as b:
                for g in range(2):
                    pool.wait_ge(gn_var, b * 2 + g + 1)
                    if g == 0:
                        pool.wait_ge(consts_in, 16 * 7)
                    pool.tensor_tensor(GM[:, 4:5], GM[:, 3:4], MHALF, ALU.pow).then_inc(gn_rstd, 1)
                    if g == 0:
                        pool.memset(VS[:, :, :, 2 * HD:2 * HD + 1], 1.0).then_inc(ones_ready, 1)
                        for t in range(CT):
                            pool.wait_ge(xn_ready, b * 6 + t + 1)
                            pool.tensor_tensor(X1[:, t, :], X1[:, t, :], BIAS[:, 0, t:t + 1].to_broadcast([128, PIX]),
                                               ALU.add).then_inc(x_biased, 1)
                        for s in POOL_STEPS:
                            pool.wait_ge(p_exp, b * STEPS + s + 1)
                            pool.tensor_tensor(PL[:, s % 3, :], P32[:, s % 3, :], high_view(s),
                                               ALU.subtract).then_inc(p_low_pool, 1)
                    else:
                        for t in range(CT):
                            pool.wait_ge(x_split, b * 6 + 3 + t + 1)
                            image = (lambda a: a.rearrange("p (h w) -> p h w", w=HW))
                            pool.tensor_tensor(XP[:, 1, t, 1:HW + 1, 1:HW + 1], image(XN[:, t, :]),
                                               image(XHL[:, 0, t, :]), ALU.subtract).then_inc(xpl_ready, 1)
            pool.wait_ge(bn_var, 1)
            for t in range(CT):
                last = pool.tensor_tensor(BSC[:, 1, t:t + 1], BSC[:, 0, t:t + 1], MHALF, ALU.pow)
            last.then_inc(bn_rstd, 1)
            for n in range(BATCH):
                pool.wait_ge(added, n + 1)
                pool.dma_start(out[n, :, :], YF(n)).then_inc(out_done[n % 3], 16)
            for n in range(3):
                pool.wait_ge(out_done[n], 16 * len(range(n, BATCH, 3)))

        @block.scalar
        def _(act):
            act.wait_ge(cleared, 1)
            for n in range(NP):
                act.wait_ge(stage_in[n % 2], 16 * (n // 2 + 1))
                for k, (hi, lo) in enumerate(pieces[n][2]):
                    last = act.activation(hi, staged(n, k), ACT.Copy, scale=W_SCALE)
                last.then_inc(w_high, 1)
            act.wait_ge(consts_in, 16 * 7)

            with act.Fori(0, BATCH) as b:

                def chunk(name):
                    act.wait_ge(chunk_full, full_at(name, b))
                    return G[INDEX[name] % 2]

                def norm(g):
                    act.wait_ge(gn_shift, b * 2 + g + 1)
                    for t in range(CT):
                        act.activation(XN[:, t, :], X1[:, t, :], ACT.Identity, bias=GM[:, 5:6],
                                       scale=GM[:, 4:5]).then_inc(xn_ready, 1)
                    if g == 1:
                        for t in range(CT):
                            act.wait_ge(xn_ready, b * 6 + 3 + t + 1)
                            act.activation(XP[:, 0, t, 1:HW + 1, 1:HW + 1],
                                           XN[:, t, :].rearrange("p (h w) -> p h w", w=HW),
                                           ACT.Copy).then_inc(xph_ready, 1)

                def extra(name):
                    if name[0] == "qk":
                        _, i, w, h = name
                        ps = chunk(name)
                        cols = slice(h * HALF, (h + 1) * HALF)
                        dst = (QS, KS)[w]
                        for hd in range(2):
                            r = hd * HEAD_B
                            for o in ((r,), (r, HEAD_B - r))[w]:
                                last = act.activation(dst[o:o + HD, i % 2, hd, cols], ps[r:r + HD, :],
                                                      ACT.Copy, scale=W_UN)
                        last.then_inc(act_read, 1)
                    if name[0] == "maxT":
                        ps = chunk(name)
                        if name[1] > 0:
                            act.wait_ge(maxrow_in, b * 32 * PAIRS + 32 * name[1])
                        act.activation(MR[:, :], ps[0:2 * QT, 0:128], ACT.Copy,
                                       scale=-1.0 / MAX_UNIT).then_inc(act_read, 1)

                norm(0)
                for n in range(QT):
                    ps = chunk(("v", n))
                    act.activation(VS[:, n, :, HD:2 * HD], ps[:, 0:CH].rearrange("p (h d) -> p h d", d=HD),
                                   ACT.Copy, scale=W_UN).then_inc(act_read, 1)
                for name in [("qk", 0, w, h) for w in range(2) for h in range(2)] + [("maxT", 0)]:
                    extra(name)

                for s in range(STEPS + 2):
                    i, s16 = divmod(s, 2 * QT)
                    if s < STEPS:
                        act.wait_ge(scores_full, b * STEPS + s + 1)
                        if s >= 3:
                            act.wait_ge(pv_done, b * STEPS + s - 2)
                        act.activation(P32[:, s % 3, :], ST[s % 2], ACT.Exp, scale=SCALE).then_inc(p_exp, 1)
                        for name in next_chunks(i, s16):
                            extra(name)
                    if s >= 2 and (s - 2) % QT == QT - 1:
                        act.wait_ge(pv_done, b * STEPS + s - 1)
                        for k in range(2):
                            act.activation(OLO[:, k, :, :], O[k].rearrange("p (q d) -> p q d", d=VCOL)[:, :, 0:HD],
                                           ACT.Copy).then_inc(o_low, 1)
                for t in range(CT):
                    for h in range(2):
                        ps = chunk(("oT", t, h))
                        act.activation(XHL[:, 0, t, h * HALF:(h + 1) * HALF], ps[:, :], ACT.Copy).then_inc(act_read, 1)
                norm(1)
                for h in range(2):
                    ps = chunk(("conv", h))
                    for r in (0, HEAD_B):
                        last = act.activation(CV[r:r + 2 * OFF_CH, h * HALF:(h + 1) * HALF],
                                              ps[r:r + 2 * OFF_CH, :], ACT.Copy)
                    last.then_inc(act_read, 1)
                for h in range(2):
                    act.wait_ge(dve_read, dve_at(("comb", h), b))
                    act.activation(PTMP[0:ROWS, h * HALF:(h + 1) * HALF], POSM[0:ROWS, h * HALF:(h + 1) * HALF],
                                   ACT.Exp, scale=-1.0).then_inc(z_exp, 1)

                def hats(ps, h, read_count):
                    d, v = TV[:, 0, h * HALF:(h + 1) * HALF], TV[:, 1, h * HALF:(h + 1) * HALF]
                    act.activation(d, ps[:, :], ACT.Abs, bias=NEG_POS).then_inc(act_read, 1)
                    act.wait_ge(act_read, read_count)
                    act.activation(v, d, ACT.Relu, bias=1.0, scale=-1.0).then_inc(hat_ready, 1)

                for h in range(2):
                    hats(chunk(("pre", "pos", h)), h, act_at(("pre", "pos", h), b))
                for h in range(2):
                    act.activation(HX[:, 0, h * HALF:(h + 1) * HALF], chunk(("pre", "hx", h))[:, :],
                                   ACT.Copy).then_inc(act_read, 1)
                for n, (lo, hi) in enumerate(tap_segments(0, 0)):
                    act.wait_ge(dve_read, dve_at(("next", "hy", n), b))
                    act.activation(MHL[:, 0, 0, 0:hi - lo], M32[:, 0, 0:hi - lo], ACT.Copy).then_inc(m_high, 1)
                act.activation(ZHL[:, 0, 0, :], chunk(("next", "z"))[:, 0:CH], ACT.Copy, scale=W_UN).then_inc(act_read, 1)

                with act.Fori(0, KX) as kx:
                    base_full = act.snap(b * PER_FULL + kx * NLOOP + (NPRE - NSKIP))
                    base_a = act.snap(b * PER_A + kx * LOOP_A + PRE_A)
                    base_d = act.snap(b * PER_D + kx * LOOP_D + PRE_D)
                    base_s = act.snap(b * PER_SAMPLED + kx * (3 * QT) + 1)
                    base_hl = act.snap(b * (2 * (TAPS + 1)) + kx * 6)
                    seg = 0
                    for ky in range(3):
                        nky = (ky + 1) % 3
                        for j in range(QT):
                            last = j == QT - 1
                            nj, hky = (0, nky) if last else (j + 1, ky)
                            buf = nj % 2
                            segs = tap_segments(nj, hky)
                            act.wait_ge(sampled, base_s + (ky * QT + j))
                            for n, (lo, hi) in enumerate(segs):
                                o = lo - segs[0][0]
                                act.wait_ge(dve_read, base_d + reads(LOOP, LINDEX[("hy", ky, j, n)] + 1, "D"))
                                act.activation(MHL[:, buf, 0, o:o + hi - lo], M32[:, buf, o:o + hi - lo],
                                               ACT.Copy).then_inc(m_high, 1)
                            g = LINDEX[("z", ky, j)]
                            act.wait_ge(chunk_full, base_full + (g + 1))
                            act.activation(ZHL[:, buf, 0, :], G[(NPRE + g) % 2][:, 0:CH], ACT.Copy,
                                           scale=W_UN).then_inc(act_read, 1)
                            for (kind, h), who in PREP_AT.get(j, []):
                                if who != "A":
                                    continue
                                g = LINDEX[("prep", ky, kind, h)]
                                act.wait_ge(chunk_full, base_full + (g + 1))
                                ps = G[(NPRE + g) % 2]
                                if kind == "pos":
                                    if h == 0:
                                        act.wait_ge(hl_ready, base_hl + (2 * ky + 2))
                                    hats(ps, h, base_a + reads(LOOP, g + 1, "A"))
                                else:
                                    act.activation(HX[:, nky, h * HALF:(h + 1) * HALF], ps[:, :],
                                                   ACT.Copy).then_inc(act_read, 1)

                act.wait_ge(sampled, b * PER_SAMPLED + PER_SAMPLED)
                for t in range(CT):
                    for h in range(2):
                        act.activation(XN[:, t, h * HALF:(h + 1) * HALF], R6[:, 2 * t + h, :], ACT.Identity,
                                       bias=BIAS[:, 1, t:t + 1]).then_inc(y_ready, 1)
                act.wait_ge(y_ready, b * 6 + 6)
                act.dma_start(y_d[bass.ds(b, 1), :, :].rearrange("a p n -> (a p) n"),
                              XN[:, :, :].rearrange("p t n -> p (t n)")).then_inc(y_out, 16)
                act.wait_ge(y_out, b * 16 + 16)
            act.wait_ge(bn_ready, 1)
            for n in range(BATCH):
                act.wait_ge(yf_in[n % 3], 16 * (n // 3 + 1))
                for t in range(CT):
                    y = YF(n)[:, t * PIX:(t + 1) * PIX]
                    act.activation(y, y, ACT.Gelu, bias=BSC[:, 3, t:t + 1], scale=BSC[:, 2, t:t + 1]).then_inc(gelu_done, 1)

        @block.vector
        def _(dve):
            dve.wait_ge(cleared, 1)
            for n in range(NP):
                dve.wait_ge(w_high, n + 1)
                for k, (hi, lo) in enumerate(pieces[n][2]):
                    last = dve.scalar_tensor_tensor(lo, staged(n, k), W_SCALE, hi, ALU.mult, ALU.subtract)
                last.then_inc(w_low, 1)
            dve.wait_ge(consts_in, 16 * 7)

            with dve.Fori(0, BATCH) as b:
                links = [0]

                def link(ins):
                    links[0] += 1
                    ins.then_inc(dve_chain, 1)
                    dve.wait_ge(dve_chain, b * DVE_LINKS + links[0])

                def chunk(name):
                    dve.wait_ge(chunk_full, full_at(name, b))
                    return G[INDEX[name] % 2]

                def norm(g):
                    for n in range(6):
                        t, h = divmod(n, 2)
                        last = dve.bn_stats(ST6[:, n, :], X1[:, t, h * HALF:(h + 1) * HALF])
                    link(last)
                    dve.memset(GM[:, 6:7], 0.0)
                    link(dve.bn_aggr(MV[:, :], ST6[:, :, :].rearrange("p a s -> p (a s)")))
                    dve.scalar_tensor_tensor(MV[:, 1:2], MV[:, 0:1], MV[:, 0:1], MV[:, 1:2],
                                             ALU.mult, ALU.add).then_inc(gn_stats, 1)
                    name = ("gn", "gn2")[g]
                    dve.tensor_copy(GM[:, 0:2], chunk(name)[:, 0:2]).then_inc(dve_read, 1)
                    dve.wait_ge(dve_read, dve_at(name, b))
                    link(dve.scalar_tensor_tensor(GM[:, 2:3], GM[:, 0:1], GM[:, 0:1], GM[:, 1:2],
                                                  ALU.mult, ALU.subtract))
                    dve.tensor_scalar(GM[:, 3:4], GM[:, 2:3], -1.0, GN_EPS, ALU.mult, ALU.add).then_inc(gn_var, 1)
                    dve.wait_ge(gn_rstd, b * 2 + g + 1)
                    dve.scalar_tensor_tensor(GM[:, 5:6], GM[:, 0:1], -1.0, GM[:, 4:5],
                                             ALU.mult, ALU.mult).then_inc(gn_shift, 1)
                    for t in range(CT):
                        dve.wait_ge(xn_ready, b * 6 + 3 * g + t + 1)
                        link(dve.tensor_copy(XHL[:, 0, t, :], XN[:, t, :]))
                        dve.tensor_tensor(XHL[:, 1, t, :], XN[:, t, :], XHL[:, 0, t, :],
                                          ALU.subtract).then_inc(x_split, 1)

                def extra(name):
                    ps = chunk(name) if name[0] != "maxT" else None
                    if name[0] == "qk":
                        _, i, w, h = name
                        cols = slice(h * HALF, (h + 1) * HALF)
                        dve.wait_ge(act_read, act_at(name, b))
                        for hd in range(2):
                            r = hd * HEAD_B
                            o = (HEAD_B - r, r)[w]
                            high, low = (QS, KS)[w], (QS, KL)[w]
                            last = dve.scalar_tensor_tensor(low[o:o + HD, i % 2, hd, cols], ps[r:r + HD, :], W_UN,
                                                            high[r:r + HD, i % 2, hd, cols], ALU.mult, ALU.subtract)
                        last.then_inc(dve_read, 1)
                    if name[0] == "max":
                        n = name[2]
                        dve.reduce_max(MXP[:, n // 2, n % 2:n % 2 + 1], ps[:, :], AX.X).then_inc(dve_read, 1)
                        if n == 4 * QT - 1:
                            dve.wait_ge(dve_read, dve_at(name, b))
                            dve.reduce_max(MX[:, :], MXP[:, :, :], AX.X).then_inc(max_ready, 1)

                dve.wait_ge(x_in, b * 16 + 16)
                norm(0)
                for n in range(QT):
                    ps = chunk(("v", n))
                    dve.wait_ge(act_read, act_at(("v", n), b))
                    dve.scalar_tensor_tensor(VS[:, n, :, 0:HD], ps[:, 0:CH].rearrange("p (h d) -> p h d", d=HD), W_UN,
                                             VS[:, n, :, HD:2 * HD], ALU.mult, ALU.subtract).then_inc(dve_read, 1)
                for name, _, _ in PRE[INDEX[("qk", 0, 0, 0)]:INDEX[("maxT", 0)]]:
                    extra(name)

                for s in range(STEPS + 2):
                    i, s16 = divmod(s, 2 * QT)
                    if s < STEPS:
                        for name in next_chunks(i, s16):
                            extra(name)
                    if s in DVE_STEPS:
                        dve.wait_ge(p_exp, b * STEPS + s + 1)
                        dve.tensor_tensor(PL[:, s % 3, :], P32[:, s % 3, :], high_view(s),
                                          ALU.subtract).then_inc(p_low_dve, 1)
                    if s >= 2 and (s - 2) % QT == QT - 1:
                        head = (s - 2) // QT
                        for k in range(2):
                            ov = O[k].rearrange("p (q d) -> p q d", d=VCOL)
                            dve.wait_ge(o_low, b * 2 * HEADS + 2 * head + k + 1)
                            dve.reciprocal(ORS[:, k, :], ov[:, :, 2 * HD])
                            link(dve.tensor_tensor(OSUM[:, k, :, :], ov[:, :, HD:2 * HD], OLO[:, k, :, :], ALU.add))
                            dve.tensor_tensor(ON[:, 4 * k:4 * k + 4, head * HD:(head + 1) * HD], OSUM[:, k, :, :],
                                              ORS[:, k, :].unsqueeze(2).to_broadcast([128, 4, HD]),
                                              ALU.mult).then_inc(o_norm, 1)
                for t in range(CT):
                    for h in range(2):
                        ps = chunk(("oT", t, h))
                        dve.wait_ge(act_read, act_at(("oT", t, h), b))
                        dve.tensor_tensor(XHL[:, 1, t, h * HALF:(h + 1) * HALF], ps[:, :],
                                          XHL[:, 0, t, h * HALF:(h + 1) * HALF], ALU.subtract).then_inc(dve_read, 1)
                dve.wait_ge(x_biased, b * 3 + 3)
                for t in range(CT):
                    for h in range(2):
                        cols = slice(h * HALF, (h + 1) * HALF)
                        dve.scalar_tensor_tensor(X1[:, t, cols], chunk(("proj", t, h))[:, :], W_UN, X1[:, t, cols],
                                                 ALU.mult, ALU.add).then_inc(dve_read, 1)
                dve.wait_ge(dve_read, dve_at(("proj", CT - 1, 1), b))
                norm(1)

                for h in range(2):
                    cols = slice(h * HALF, (h + 1) * HALF)
                    dve.tensor_scalar(POSM[0:ROWS, cols], chunk(("comb", h))[0:ROWS, :], CBIAS[0:ROWS, :], -80.0,
                                      ALU.add, ALU.max).then_inc(dve_read, 1)
                for h in range(2):
                    cols = slice(h * HALF, (h + 1) * HALF)
                    dve.wait_ge(dve_read, dve_at(("comb", h), b))
                    link(dve.tensor_scalar(CV[0:ROWS, cols], POSM[0:ROWS, cols], -float(MAX_OFF), float(MAX_OFF),
                                           ALU.max, ALU.min))
                    link(dve.scalar_tensor_tensor(CV[0:ROWS, cols], CV[0:ROWS, cols], IS_POS[0:ROWS, :],
                                                  C16[0:ROWS, BASE + h * HALF:BASE + (h + 1) * HALF], ALU.mult, ALU.add))
                    dve.wait_ge(z_exp, b * 2 + h + 1)
                    link(dve.tensor_scalar_add(PTMP[0:ROWS, cols], PTMP[0:ROWS, cols], 1.0))
                    link(dve.reciprocal(PTMP[0:ROWS, cols], PTMP[0:ROWS, cols]))
                    link(dve.scalar_tensor_tensor(POSM[0:ROWS, cols], PTMP[0:ROWS, cols], TWO_MASK[0:ROWS, :],
                                                  CV[0:ROWS, cols], ALU.mult, ALU.add))
                    link(dve.tensor_copy(POSS[0:ROWS, cols], POSM[0:ROWS, cols]))
                    dve.tensor_tensor(POSS[LO_ROW:LO_ROW + ROWS, cols], POSM[0:ROWS, cols], POSS[0:ROWS, cols],
                                      ALU.subtract).then_inc(pos_ready, 1)

                def hat_halves(ps, h, buf, read_count, hat_count, wait_link):
                    cols = slice(h * HALF, (h + 1) * HALF)
                    v = TV[:, 1, cols]
                    dve.wait_ge(hat_ready, hat_count)
                    dve.tensor_tensor(v, ps[:, :], v, ALU.mult).then_inc(dve_read, 1)
                    dve.wait_ge(dve_read, read_count)
                    wait_link(dve.tensor_copy(H16[:, cols], v))
                    dve.scalar_tensor_tensor(HL[:, buf, cols], H16[:, cols], NEG_LO, v,
                                             ALU.mult, ALU.add).then_inc(hl_ready, 1)

                hats_b = 2 * (TAPS + 1)
                for h in range(2):
                    name = ("pre", "mask", h)
                    hat_halves(chunk(name), h, 0, dve_at(name, b), b * hats_b + h + 1, link)
                dve.wait_ge(act_read, act_at(("pre", "hx", 1), b))
                for n, (lo, hi) in enumerate(tap_segments(0, 0)):
                    name = ("next", "hy", n)
                    dve.tensor_tensor(M32[:, 0, 0:hi - lo], chunk(name)[:, 0:hi - lo], HX[:, 0, lo:hi],
                                      ALU.mult).then_inc(dve_read, 1)
                    dve.wait_ge(m_high, b * PER_SEGS + n + 1)
                    dve.tensor_tensor(MHL[:, 0, 1, 0:hi - lo], M32[:, 0, 0:hi - lo], MHL[:, 0, 0, 0:hi - lo],
                                      ALU.subtract).then_inc(m_low, 1)
                dve.wait_ge(act_read, act_at(("next", "z"), b))
                dve.scalar_tensor_tensor(ZHL[:, 0, 1, :], G[INDEX[("next", "z")] % 2][:, 0:CH], W_UN, ZHL[:, 0, 0, :],
                                         ALU.mult, ALU.subtract).then_inc(dve_read, 1)
                if links[0] != DVE_LINKS - 6 * KX:
                    raise ValueError(f"DVE_LINKS {links[0] + 6 * KX}")

                with dve.Fori(0, KX) as kx:
                    base_full = dve.snap(b * PER_FULL + kx * NLOOP + (NPRE - NSKIP))
                    base_a = dve.snap(b * PER_A + kx * LOOP_A + PRE_A)
                    base_d = dve.snap(b * PER_D + kx * LOOP_D + PRE_D)
                    base_seg = dve.snap(b * PER_SEGS + kx * LOOP_SEGS + PRE_SEGS)
                    base_hat = dve.snap(b * hats_b + kx * 6 + 2)
                    base_link = dve.snap(b * DVE_LINKS + kx * 6 + (DVE_LINKS - 6 * KX))
                    kx_links = [0]

                    def kx_link(ins):
                        kx_links[0] += 1
                        ins.then_inc(dve_chain, 1)
                        dve.wait_ge(dve_chain, base_link + kx_links[0])

                    seg = 0
                    for ky in range(3):
                        nky = (ky + 1) % 3
                        for j in range(QT):
                            last = j == QT - 1
                            nj, hky = (0, nky) if last else (j + 1, ky)
                            buf = nj % 2
                            segs = tap_segments(nj, hky)
                            if last:
                                dve.wait_ge(act_read, base_a + reads(LOOP, LINDEX[("prep", ky, "hx", 1)] + 1, "A"))
                            for n, (lo, hi) in enumerate(segs):
                                o = lo - segs[0][0]
                                g = LINDEX[("hy", ky, j, n)]
                                dve.wait_ge(chunk_full, base_full + (g + 1))
                                dve.tensor_tensor(M32[:, buf, o:o + hi - lo], G[(NPRE + g) % 2][:, 0:hi - lo],
                                                  HX[:, hky, lo:hi], ALU.mult).then_inc(dve_read, 1)
                            for n, (lo, hi) in enumerate(segs):
                                o = lo - segs[0][0]
                                seg += 1
                                dve.wait_ge(m_high, base_seg + seg)
                                dve.tensor_tensor(MHL[:, buf, 1, o:o + hi - lo], M32[:, buf, o:o + hi - lo],
                                                  MHL[:, buf, 0, o:o + hi - lo], ALU.subtract).then_inc(m_low, 1)
                            g = LINDEX[("z", ky, j)]
                            dve.wait_ge(act_read, base_a + reads(LOOP, g + 1, "A"))
                            dve.scalar_tensor_tensor(ZHL[:, buf, 1, :], G[(NPRE + g) % 2][:, 0:CH], W_UN,
                                                     ZHL[:, buf, 0, :], ALU.mult, ALU.subtract).then_inc(dve_read, 1)
                            for (kind, h), who in PREP_AT.get(j, []):
                                if who != "D":
                                    continue
                                g = LINDEX[("prep", ky, kind, h)]
                                dve.wait_ge(chunk_full, base_full + (g + 1))
                                hat_halves(G[(NPRE + g) % 2], h, nky, base_d + reads(LOOP, g + 1, "D"),
                                           base_hat + (2 * ky + h + 1), kx_link)
                    if kx_links[0] != 6 or seg != LOOP_SEGS:
                        raise ValueError(f"links per kx {kx_links[0]}")

                for t in range(CT):
                    for h in range(2):
                        dve.wait_ge(y_ready, b * 6 + (2 * t + h + 1))
                        last = dve.bn_stats(BST[:, t, bass.ds(b * 2 + h, 1), :].rearrange("p a s -> p (a s)"),
                                            XN[:, t, h * HALF:(h + 1) * HALF])
                last.then_inc(y_stats, 1)

            dve.wait_ge(y_stats, BATCH)
            n_links = [BATCH * DVE_LINKS]

            def end_link(ins):
                n_links[0] += 1
                ins.then_inc(dve_chain, 1)
                dve.wait_ge(dve_chain, n_links[0])

            for t in range(CT):
                last = dve.bn_aggr(BMV[:, t, :], BST[:, t, :, :].rearrange("p a s -> p (a s)"))
            end_link(last)
            dve.tensor_scalar_add(BSC[:, 0, :], BMV[:, :, 1], BN_EPS).then_inc(bn_var, 1)
            dve.wait_ge(bn_rstd, 1)
            end_link(dve.tensor_tensor(BSC[:, 2, :], BSC[:, 1, :], BIAS[:, 2, :], ALU.mult))
            end_link(dve.tensor_tensor(BSC[:, 0, :], BMV[:, :, 0], BSC[:, 2, :], ALU.mult))
            dve.tensor_tensor(BSC[:, 3, :], BIAS[:, 3, :], BSC[:, 0, :], ALU.subtract).then_inc(bn_ready, 1)
            for n in range(BATCH):
                dve.wait_ge(xf_in[n % 3], 16 * (n // 3 + 1))
                for t in range(CT):
                    y = YF(n)[:, t * PIX:(t + 1) * PIX]
                    dve.wait_ge(gelu_done, n * CT + t + 1)
                    last = dve.tensor_tensor(y, y, XF(n)[:, t * PIX:(t + 1) * PIX], ALU.add)
                last.then_inc(added, 1)

        @block.tensor
        def _(pe):
            pe.wait_ge(w_low, NP)
            pe.wait_ge(consts_in, 16 * 7)
            pe.wait_ge(maxunit_in, 16 * 4)
            with pe.Fori(0, BATCH) as b:

                def bank(name):
                    g = INDEX[name]
                    if g >= 2:
                        who = PRE[g - 2][2]
                        if "A" in who:
                            pe.wait_ge(act_read, b * PER_A + reads(PRE, g - 1, "A"))
                        if "D" in who:
                            pe.wait_ge(dve_read, b * PER_D + reads(PRE, g - 1, "D"))
                    return G[g % 2]

                def products(out, operands):
                    for n, (l, r) in enumerate(operands):
                        last = pe.matmul(out, l, r, start=(n == 0), stop=(n == len(operands) - 1))
                    return last

                def norm(g):
                    pe.wait_ge(gn_stats, b * 2 + g + 1)
                    out = bank(("gn", "gn2")[g])
                    pe.matmul(out[:, 0:2], GMAT, MV[:, :], start=True, stop=True).then_inc(chunk_full, 1)

                def extra(name):
                    if name[0] == "qk":
                        _, i, w, h = name
                        cols = slice(h * HALF, (h + 1) * HALF)
                        out = bank(name)
                        products(out[0:PAIR_ROWS, :],
                                 [(WQK[:, wp_, t, 2 * i + w, :], XHL[:, xp_, t, cols])
                                  for t in range(CT) for wp_, xp_ in ((0, 0), (0, 1), (1, 0))]).then_inc(chunk_full, 1)
                    if name[0] == "max":
                        _, i, n = name
                        hd, q, h = n // (2 * QT), n // 2 % QT, n % 2
                        if n == 0:
                            pe.wait_ge(dve_read, dve_at(("qk", i, 1, 1), b))
                        out = bank(name)
                        pe.matmul(out[:, :], QS[0:PAIR_ROWS, i % 2, hd, q * 128:(q + 1) * 128],
                                  KS[0:PAIR_ROWS, i % 2, hd, h * HALF:(h + 1) * HALF],
                                  start=True, stop=True).then_inc(chunk_full, 1)
                    if name[0] == "maxT":
                        pe.wait_ge(max_ready, b * PAIRS + name[1] + 1)
                        out = bank(name)
                        pe.transpose(out[0:2 * QT, 0:128], MX[:, :], IDENT).then_inc(chunk_full, 1)

                norm(0)
                for n in range(QT):
                    if n == 0:
                        pe.wait_ge(x_split, b * 6 + 3)
                    out = bank(("v", n))
                    wv_ = [WALL[:, WVO + a * TAPW:WVO + (a + 1) * TAPW].rearrange("p (t c) -> p t c", t=CT) for a in range(2)]
                    products(out[:, 0:CH], [(XHL[:, xp_, t, n * 128:(n + 1) * 128], wv_[wp_][:, t, :])
                                            for t in range(CT) for xp_, wp_ in ((0, 0), (0, 1), (1, 0))]).then_inc(chunk_full, 1)
                for name, _, _ in PRE[INDEX[("qk", 0, 0, 0)]:INDEX[("maxT", 0)] + 1]:
                    extra(name)

                def pv(s, first, count):
                    head, kt = divmod(s, QT)
                    if first == 0:
                        pv_waits(s, head, kt)
                    for q in range(first, first + count):
                        ov = O[q // 4].rearrange("p (q d) -> p q d", d=VCOL)[:, q % 4, :]
                        pe.matmul(ov, high_view(s)[:, q * 128:(q + 1) * 128], VS[:, kt, head, 0:VCOL],
                                  start=(kt == 0 and q % 4 == 0), stop=False, skip_group_check=True)
                        last = pe.matmul(ov[:, HD:VCOL], PL[:, s % 3, q * 128:(q + 1) * 128],
                                         VS[:, kt, head, HD:VCOL], start=False, stop=(kt == QT - 1),
                                         skip_group_check=True)
                    if first + count == QT:
                        last.then_inc(pv_done, 1)

                def pv_waits(s, head, kt):
                    if s in POOL_STEPS:
                        pe.wait_ge(p_low_pool, b * len(POOL_STEPS) + POOL_STEPS.index(s) + 1)
                    else:
                        pe.wait_ge(p_low_dve, b * len(DVE_STEPS) + DVE_STEPS.index(s) + 1)
                    if s == 0:
                        pe.wait_ge(ones_ready, b + 1)
                    if kt == 0 and head > 0:
                        pe.wait_ge(o_norm, b * 2 * HEADS + 2 * head)

                for s in range(STEPS + 2):
                    i, s16 = divmod(s, 2 * QT)
                    chunks = []
                    if s < STEPS:
                        hd, kt = divmod(s16, QT)
                        chunks = next_chunks(i, s16)
                        if s16 == 0:
                            pe.wait_ge(maxrow_in, b * 32 * PAIRS + 32 * (i + 1))
                        if s >= 2:
                            pe.wait_ge(p_exp, b * STEPS + s - 1)
                        for h in range(2):
                            if h == 1 and chunks and chunks[0][0] == "max":
                                extra(chunks.pop(0))
                            cols = slice(h * HALF, (h + 1) * HALF)
                            out = ST[s % 2][:, cols]
                            pe.matmul(out, KS[0:PAIR_ROWS, i % 2, hd, kt * 128:(kt + 1) * 128],
                                      QS[0:PAIR_ROWS, i % 2, hd, cols], start=True, stop=False)
                            last = pe.matmul(out, KL[0:PAIR_ROWS, i % 2, hd, kt * 128:(kt + 1) * 128],
                                             QS[0:PAIR_ROWS, i % 2, hd, cols], start=False, stop=True)
                        last.then_inc(scores_full, 1)
                    for k in range(4):
                        if k % 2 == 0 and chunks:
                            extra(chunks.pop(0))
                        if s >= 2:
                            pv(s - 2, 2 * k, 2)
                    for name in chunks:
                        extra(name)

                pe.wait_ge(o_norm, b * 2 * HEADS + 2 * HEADS)
                for t in range(CT):
                    for h in range(2):
                        out = bank(("oT", t, h))
                        for q in range(4):
                            last = pe.transpose(out[:, q * 128:(q + 1) * 128], ON[:, 4 * h + q, t * 128:(t + 1) * 128], IDENT)
                        last.then_inc(chunk_full, 1)
                pe.wait_ge(dve_read, dve_at(("oT", CT - 1, 1), b))
                for t in range(CT):
                    for h in range(2):
                        out = bank(("proj", t, h))
                        products(out[:, :], [(WP[:, wp_, k, t * 128:(t + 1) * 128], XHL[:, xp_, k, h * HALF:(h + 1) * HALF])
                                             for k in range(CT) for wp_, xp_ in ((0, 0), (0, 1), (1, 0))]).then_inc(chunk_full, 1)
                norm(1)

                pe.wait_ge(xph_ready, b * 3 + 3)
                pe.wait_ge(xpl_ready, b * 3 + 3)
                for h in range(2):
                    out = bank(("conv", h))
                    terms = [(t, kx * 3 + ky, a) for a in range(2) for t in range(CT) for kx in range(3) for ky in range(3)]
                    half = len(terms) // 2
                    for n in range(half):
                        for c in range(2):
                            t, tap, a = terms[c * half + n]
                            kx, ky = divmod(tap, 3)
                            row = h * (HW // 2) + ky
                            r = c * HEAD_B
                            last = pe.matmul(out[r:r + 2 * OFF_CH, :], WC[:, t * TAPS + tap, :],
                                             XP[:, a, t, row:row + HW // 2, kx:kx + HW],
                                             start=(n == 0), stop=(n == half - 1))
                    last.then_inc(chunk_full, 1)
                for h in range(2):
                    pe.wait_ge(act_read, act_at(("conv", h), b))
                    out = bank(("comb", h))
                    pe.matmul(out[0:ROWS, :], CMB, CV[:, h * HALF:(h + 1) * HALF],
                              start=True, stop=True).then_inc(chunk_full, 1)

                zero = C16[:, SELP + TAPS * 128:SELP + (TAPS + 1) * 128]
                for k in range(6):
                    last = pe.matmul(R6[:, k, :], zero, C16[:, 0:HALF], start=True, stop=False, skip_group_check=True)
                last.then_inc(sampled, 1)

                for kind, sel in (("pos", SELP), ("mask", SELM)):
                    for h in range(2):
                        if kind == "pos":
                            pe.wait_ge(pos_ready, b * 2 + h + 1)
                        out = bank(("pre", kind, h))
                        pe.matmul(out[:, :], C16[:, sel:sel + 128], POSS[:, h * HALF:(h + 1) * HALF],
                                  start=True, stop=True).then_inc(chunk_full, 1)
                hats_b = 2 * (TAPS + 1)
                for h in range(2):
                    pe.wait_ge(hl_ready, b * hats_b + h + 1)
                    out = bank(("pre", "hx", h))
                    pe.matmul(out[:, :], C16[:, SELX:SELX + 128], HL[:, 0, h * HALF:(h + 1) * HALF],
                              start=True, stop=True).then_inc(chunk_full, 1)
                for n, (lo, hi) in enumerate(tap_segments(0, 0)):
                    out = bank(("next", "hy", n))
                    pe.matmul(out[:, 0:hi - lo], C16[:, SELY:SELY + 128], HL[:, 0, lo:hi],
                              start=True, stop=True).then_inc(chunk_full, 1)

                def z_products(out, j, high, low):
                    products(out[:, 0:CH],
                             [(XHL[:, xp_, t, j * 128:(j + 1) * 128], (high, low)[wp_](t))
                              for t in range(CT) for xp_, wp_ in ((0, 0), (0, 1), (1, 0))]).then_inc(chunk_full, 1)

                z_products(bank(("next", "z")), 0, lambda t: WALL[:, WDH + t * CH:WDH + (t + 1) * CH],
                           lambda t: WALL[:, WDL + t * CH:WDL + (t + 1) * CH])

                with pe.Fori(0, KX) as kx:
                    base_a = pe.snap(b * PER_A + kx * LOOP_A + PRE_A)
                    base_d = pe.snap(b * PER_D + kx * LOOP_D + PRE_D)
                    base_seg = pe.snap(b * PER_SEGS + kx * LOOP_SEGS + PRE_SEGS)
                    base_hl = pe.snap(b * hats_b + kx * 6 + 2)

                    def loop_bank(name):
                        g = LINDEX[name]
                        who = (PRE + LOOP)[NPRE + g - 2][2]
                        before = (lambda w: reads(LOOP, g - 1, w) if g >= 1 else -reads(LOOP[-1:], 1, w))
                        if "A" in who:
                            pe.wait_ge(act_read, base_a + before("A"))
                        if "D" in who:
                            pe.wait_ge(dve_read, base_d + before("D"))
                        return G[(NPRE + g) % 2]

                    made = 0
                    for ky in range(3):
                        nky = (ky + 1) % 3
                        wd_at = {}
                        for j in range(QT):
                            last_j = j == QT - 1
                            nj, hky = (0, nky) if last_j else (j + 1, ky)
                            tap = ky + (1 if last_j else 0)
                            segs, now = tap_segments(nj, hky), tap_segments(j, ky)
                            buf = j % 2
                            if last_j:
                                pe.wait_ge(hl_ready, base_hl + (2 * ky + 2))
                            for n, (lo, hi) in enumerate(segs):
                                out = loop_bank(("hy", ky, j, n))
                                pe.matmul(out[:, 0:hi - lo], C16[:, SELY + nj * 128:SELY + (nj + 1) * 128],
                                          HL[:, hky, lo:hi], start=True, stop=True).then_inc(chunk_full, 1)

                            def sample(t):
                                for zp_, mp_ in ((0, 0), (0, 1), (1, 0)):
                                    for lo, hi in now:
                                        o = lo - now[0][0]
                                        bk = 2 * t + lo // HALF
                                        last = pe.matmul(R6[:, bk, lo % HALF:lo % HALF + hi - lo],
                                                         ZHL[:, buf, zp_, t * 128:(t + 1) * 128],
                                                         MHL[:, buf, mp_, o:o + hi - lo],
                                                         start=False, stop=False, skip_group_check=True)
                                return last

                            pe.wait_ge(m_low, base_seg + made)
                            gz = LINDEX[("z",) + ((ky, j - 1) if j else (ky - 1, QT - 1))] if (ky or j) else -1
                            pe.wait_ge(dve_read, base_d + (reads(LOOP, gz + 1, "D")))
                            sample(0)
                            out = loop_bank(("z", ky, j))
                            step = kx * (3 * TAPW) + tap * TAPW
                            z_products(out, nj,
                                       lambda t: WALL[:, bass.ds(step + (WDH + t * CH), CH)],
                                       lambda t: WALL[:, bass.ds(step + (WDL + t * CH), CH)])
                            sample(1)
                            for (kind, h), _ in PREP_AT.get(j, []):
                                cols = slice(h * HALF, (h + 1) * HALF)
                                if kind == "hx":
                                    pe.wait_ge(hl_ready, base_hl + (2 * ky + h + 1))
                                    lhs, rhs = C16[:, SELX:SELX + 128], HL[:, nky, cols]
                                else:
                                    sel = (SELP, SELM)[kind == "mask"]
                                    lhs, rhs = C16[:, bass.ds(kx * 384 + (sel + (ky + 1) * 128), 128)], POSS[:, cols]
                                out = loop_bank(("prep", ky, kind, h))
                                pe.matmul(out[:, :], lhs, rhs, start=True, stop=True).then_inc(chunk_full, 1)
                            sample(2).then_inc(sampled, 1)
                            made += len(segs)


def shape_constants():
    sel = np.zeros((128, 29, 128), np.float16)
    for i in range(TAPS):
        for m in range(128):
            for lo in (0, LO_ROW):
                sel[lo + i + (0 if m < 64 else TAPS), i, m] = 1
                if m >= 64:
                    sel[lo + 2 * TAPS + i, 10 + i, m] = 1
    sel[OFF_CH, 10:20, 0:64] = 1
    for j in range(QT):
        for q in range(128):
            y = TILE_ROWS * j + q // HW
            sel[[y, 32 + y], 20 + j, q] = 1
    for q in range(128):
        sel[[64 + q % HW, 96 + q % HW], 28, q] = 1
    grid = np.zeros((128, HW, HW), np.float16)
    for i in range(TAPS):
        kx, ky = divmod(i, 3)
        grid[i] = (np.arange(HW) - 1 + ky)[:, None]
        grid[TAPS + i] = (np.arange(HW) - 1 + kx)[None, :]
    grid[OFF_CH] = 1
    grid[127] = MAX_UNIT
    c16 = np.concatenate([sel.reshape(128, -1), grid.reshape(128, -1)], 1)
    c32 = np.zeros((128, 128 + 128 + ROWS + 8), np.float32)
    c32[:, 0:128] = np.eye(128)
    per = 128 // GN_GROUPS
    c32[:, 128:256] = np.kron(np.eye(GN_GROUPS), np.full((per, per), 1.0 / per))
    for r in range(OFF_CH):
        c32[[r, OFF_CH + r, HEAD_B + r, HEAD_B + OFF_CH + r], 256 + r] = W_UN
    p = np.arange(128)
    col = 256 + ROWS
    c32[:, col] = p < 2 * TAPS
    c32[:, col + 1] = 2.0 * ((p >= 2 * TAPS) & (p < OFF_CH))
    c32[:, col + 2] = -(p % 32)
    c32[:, col + 3] = -1.0 * (p // 32 % 2)
    c32[:, col + 4] = -0.5
    return c16, c32


def kernel(x, L0_conv_w_qkv, L0_conv_w_proj, L0_conv_b_proj, L1_conv_proj_w, L1_conv_proj_b, L1_conv_off_w,
           L1_conv_off_b, L1_conv_mask_w, L1_conv_mask_b, L1_conv_gamma, L1_conv_beta):
    import concourse.bacc as bacc
    from concourse.bass_utils import run_bass_kernel_spmd

    x = np.asarray(x)
    qkv = np.asarray(L0_conv_w_qkv).reshape(3, PAIRS, 2, HD, PART, CT)
    per_channel = lambda a: np.asarray(a).reshape(PART, CT)
    off = np.asarray(L1_conv_off_w).reshape(3, 3, 2, CH, 3, 3).transpose(2, 1, 0, 3, 4, 5).reshape(2 * TAPS, CH, 3, 3)
    mask = np.asarray(L1_conv_mask_w).reshape(3, 3, CH, 3, 3).transpose(1, 0, 2, 3, 4).reshape(TAPS, CH, 3, 3)
    wc = np.concatenate([off, mask], 0).reshape(OFF_CH, PART, CT, 3, 3).transpose(1, 2, 4, 3, 0)
    off_b = np.asarray(L1_conv_off_b).reshape(3, 3, 2).transpose(2, 1, 0).reshape(-1)
    mask_b = np.asarray(L1_conv_mask_b).reshape(3, 3).T.reshape(-1)
    c16, c32 = shape_constants()
    arrays = {
        "x": x.reshape(BATCH, PART, CT * PIX),
        "wqk": qkv[0:2].transpose(4, 5, 1, 0, 2, 3).reshape(PART, -1),
        "wv": np.asarray(L0_conv_w_qkv).reshape(3, CH, PART, CT)[2].transpose(1, 2, 0).reshape(PART, -1),
        "wp": np.asarray(L0_conv_w_proj).reshape(PART, CT, CT, PART).transpose(3, 2, 1, 0).reshape(PART, -1),
        "wd": np.asarray(L1_conv_proj_w).reshape(PART, CT, PART, CT, 3, 3).transpose(2, 5, 4, 3, 1, 0).reshape(PART, -1),
        "wc": wc.reshape(PART, -1),
        "bias_p": per_channel(L0_conv_b_proj),
        "bias_c": np.concatenate([off_b, mask_b])[:, None],
        "bias_d": per_channel(L1_conv_proj_b),
        "gamma": per_channel(L1_conv_gamma),
        "beta": per_channel(L1_conv_beta),
        "c16": c16,
        "c32": c32,
    }
    arrays = {k: np.ascontiguousarray(v) for k, v in arrays.items()}
    nc = bacc.Bacc("TRN2", target_bir_lowering=False, num_devices=1)
    args = [nc.dram_tensor(k, v.shape, mybir.dt.from_np(v.dtype), kind="ExternalInput").ap() for k, v in arrays.items()]
    shape = [BATCH, PART, CT * PIX]
    out = nc.dram_tensor("out", shape, mybir.dt.float32, kind="ExternalOutput").ap()
    x1_d = nc.dram_tensor("x1_scratch", shape, mybir.dt.float32, kind="Internal").ap()
    y_d = nc.dram_tensor("y_scratch", shape, mybir.dt.float32, kind="Internal").ap()
    build(nc, *args, out, x1_d, y_d)
    r = run_bass_kernel_spmd(nc, [arrays], core_ids=[0])
    return r.results[0]["out"].reshape(BATCH, CH, HW, HW)
```

```python
import concourse.bass as bass
from concourse import mybir
from contextlib import ExitStack
import numpy as np

BATCH, CH, HW, PIX = 8, 384, 32, 1024
PART = 128
CT = CH // PART
HEADS, HD = 8, 48
PAIRS = HEADS // 2
HEAD_B = 64
PAIR_ROWS = HEAD_B + HD
GN_GROUPS = 32
GN_EPS, BN_EPS = 1e-5, 1e-5
TAPS, KX, KY = 9, 3, 3
MAX_OFF = HW // 4
NEAR_OFF = 3
OFF_CH = 3 * TAPS
LO_ROW, GRID_ROW = 32, 64
ONES_ROW = GRID_ROW + 2 * TAPS
HALF = 512
QT = PIX // PART
TILE_ROWS = HW // QT
VCOL = 2 * HD + 1
SCALE = HD ** -0.5
W_SCALE = 256.0
W_UN = 1.0 / W_SCALE
MAX_ROW, MAX_UNIT = HD, 16.0
PAD = HW + 2
MCOLS = (TILE_ROWS + 2 * MAX_OFF) * HW
STEPS = HEADS * QT
TAP_STEPS = TAPS * QT


def tap_segments(j, ky, reach=MAX_OFF):
    if (j, ky) == (0, 0):
        reach = MAX_OFF
    first = max(0, TILE_ROWS * j + 1 - ky - reach)
    last = min(HW - 1, TILE_ROWS * j + TILE_ROWS + reach - ky)
    lo, hi = first * HW, (last + 1) * HW
    segs = []
    if lo < HALF:
        segs.append((lo, min(hi, HALF)))
    if hi > HALF:
        segs.append((max(lo, HALF), hi))
    return segs


def made_segments(j, ky, reach=MAX_OFF):
    segs = tap_segments(j, ky, reach)
    if len(segs) == len(tap_segments(j, ky)):
        return segs
    (lo, hi), = segs
    mid = lo + (hi - lo) // HW // 2 * HW
    return [(lo, mid), (mid, hi)]


def pair_chunks(i):
    return [(("qk", i, w, h), "AD") for w in range(2) for h in range(2)] \
        + [(("max", i, n), "D") for n in range(4 * QT)] + [(("maxT", i), "A")]


def start_chunks():
    return [(("gn", 0), "D")] + [(("v", n), "AD") for n in range(QT)] + pair_chunks(0)


PREP_AT = {0: ("pos", 0), 1: ("pos", 1), 2: ("mask", 0), 3: ("mask", 1), 4: ("hx", 0), 5: ("hx", 1)}
PREP_READER = {"pos": "A", "mask": "D", "hx": "A"}


def start_at(step):
    names = [n for n, _ in start_chunks()]
    if step == 2:
        return names[0:1]
    if 6 <= step < 10:
        return names[1 + 2 * (step - 6):3 + 2 * (step - 6)]
    if 10 <= step < 12:
        return names[9 + 2 * (step - 10):11 + 2 * (step - 10)]
    if step >= 12:
        n = 4 * QT
        return names[13 + n * (step - 12) // 12:13 + n * (step - 11) // 12]
    return []


STATS_AT = {0: (0, 1, 2), 1: (3, 4, 5)}
RSTD_AT, SHIFT_AT = 2, 3
NORM_AT = {3: (0, 1), 4: (2,)}
SPLIT_AT = {4: (0,), 5: (1, 2)}
BIAS_AT = {14: (0,), 16: (1,), 18: (2,)}


def column_chunks(last):
    reader = dict(start_chunks())
    out = []
    for ky in range(KY):
        for j in range(QT):
            end = last and ky == KY - 1
            if not (end and j == QT - 1):
                nj, nky = (j + 1, ky) if j < QT - 1 else (0, (ky + 1) % KY)
                out += [(("hy", ky, j, n), "D") for n in range(len(tap_segments(nj, nky)))]
            if j in PREP_AT and not end:
                out.append((("prep", ky) + PREP_AT[j], PREP_READER[PREP_AT[j][0]]))
            if not (end and j == QT - 1):
                out.append((("z", ky, j), "AD"))
            if last:
                out += [(n, reader[n]) for n in start_at(ky * QT + j)]
    if last:
        out.append((("maxT", 0), "A"))
    return out


START = start_chunks()
BEFORE_TAPS = sum((pair_chunks(i) for i in range(1, PAIRS)), []) \
    + [(("oT", t, h), "AD") for t in range(CT) for h in range(2)] \
    + [(("proj", t, h), "D") for t in range(CT) for h in range(2)] \
    + [(("gn", 1), "D")] + [(("conv", h), "A") for h in range(2)] + [(("comb",), "AD")] \
    + [(("first",) + PREP_AT[j], PREP_READER[PREP_AT[j][0]]) for j in range(4)] + [(("reach",), "D")] \
    + [(("first",) + PREP_AT[j], PREP_READER[PREP_AT[j][0]]) for j in range(4, 6)] \
    + [(("first", "hy"), "D"), (("first", "z"), "AD")]
COLUMN, LAST_COLUMN = column_chunks(False), column_chunks(True)
PER_BATCH = BEFORE_TAPS + (KX - 1) * COLUMN + LAST_COLUMN
if len(PER_BATCH) % 2:
    BEFORE_TAPS = [("pass", "")] + BEFORE_TAPS
    PER_BATCH = [("pass", "")] + PER_BATCH
if len(COLUMN) % 2 or len(tap_segments(0, 0)) != 1:
    raise ValueError("a column's chunks must pair up")


def reads(chunks, who):
    return sum(r != "" if who == "F" else who in r for _, r in chunks)


class Section:

    def __init__(self, chunks, ahead, before, batch=0, column=0):
        self.chunks, self.before, self.start = chunks, before, len(ahead)
        self.index = {n: g for g, (n, _) in enumerate(chunks)}
        self.base = {w: batch * reads(PER_BATCH, w) + column * reads(COLUMN, w) + reads(ahead, w) for w in "FAD"}

    def at(self, name, who):
        return self.base[who] + reads(self.chunks[:self.index[name] + 1], who)

    def bank(self, name):
        return (self.start + self.index[name]) % 2

    def replaced(self, name):
        g = self.index[name] - 2
        if g >= 0:
            return [(w, self.base[w] + reads(self.chunks[:g + 1], w)) for w in self.chunks[g][1]]
        if not self.before:
            return []
        after = self.before[len(self.before) + g + 1:]
        return [(w, self.base[w] - reads(after, w)) for w in self.before[g][1]]


def start_section():
    return Section(START, [], [])


def before_taps(b):
    return Section(BEFORE_TAPS, START, START[-2:], b)


def column_section(b, kx):
    return Section(COLUMN, START + BEFORE_TAPS, BEFORE_TAPS[-2:], b, kx)


def last_column(b):
    return Section(LAST_COLUMN, START + BEFORE_TAPS + (KX - 1) * COLUMN, COLUMN[-2:], b)


for _tail, _other in ((START, LAST_COLUMN), (BEFORE_TAPS, COLUMN)):
    if [r for _, r in _tail[-2:]] != [r for _, r in _other[-2:]]:
        raise ValueError("a section's predecessors must be read alike")

POOL_STEPS = [s for s in range(STEPS) if s % 3 != 0]
DVE_STEPS = [s for s in range(STEPS) if s % 3 == 0]
NEXT_AT = [[] for _ in range(2 * QT)]
for _n in range(4):
    NEXT_AT[_n].append(("qk", _n // 2, _n % 2))
for _n in range(4 * QT):
    NEXT_AT[4 + _n * 9 // (4 * QT)].append(("max", _n))
NEXT_AT[13].append(("maxT",))


TRANSPOSE_AT = {4: [("oT", 0, 0)], 5: [("oT", 0, 1)], 6: [("oT", 1, 0)], 7: [("oT", 1, 1)]}


def next_chunks(i, s16):
    if i + 1 == PAIRS:
        return TRANSPOSE_AT.get(s16, [])
    return [(n[0], i + 1) + n[1:] for n in NEXT_AT[s16]]


START_LINKS, BATCH_LINKS = 6, 20
PER_LINKS = START_LINKS + BATCH_LINKS
FIRST_SEGS = 1
COLUMN_SEGS = sum(n[0] == "hy" for n, _ in COLUMN)
PER_SEGS = FIRST_SEGS + (KX - 1) * COLUMN_SEGS + sum(n[0] == "hy" for n, _ in LAST_COLUMN)
PER_SAMPLED = TAP_STEPS + 1
PER_HATS, PER_SPLIT_HATS = 2 * TAPS, 2 * (TAPS - 1)
BOTH = HEAD_B + OFF_CH


def build(nc, x, wqk, wv, wp, wd, wc, bias_p, bias_c, bias_d, gamma, beta, c16, grid, c32, out, x1_d, y_d):
    fp32, fp16, bf16 = mybir.dt.float32, mybir.dt.float16, mybir.dt.bfloat16
    ALU, ACT, AX = mybir.AluOpType, mybir.ActivationFunctionType, mybir.AxisListType
    ctx = ExitStack()
    with ctx:
        def sb(name, shape, dt):
            return ctx.enter_context(nc.sbuf_tensor(name, shape, dt))

        def sem(name):
            return ctx.enter_context(nc.semaphore(name))

        X1 = sb("X1", [128, CT, PIX], fp32)
        XN = sb("XN", [128, CT, PIX], fp32)
        XA = sb("XA", [128, 2, CT, PIX], fp16)
        XB = sb("XB", [128, 2, CT, PIX], fp16)
        XP = sb("XP", [128, 2, CT, PAD, PAD], fp16)
        QS = sb("QS", [128, 2, 2, PIX], fp16)
        KS = sb("KS", [128, 2, 2, PIX], fp16)
        KL = sb("KL", [128, 2, 2, PIX], fp16)
        VS = sb("VS", [128, QT, HEADS, VCOL + 1], fp16)
        P32 = sb("P32", [128, 3, PIX], fp32)
        PL = sb("PL", [128, 3, PIX], fp16)
        TAPW = CT * CH
        WALL = sb("WALL", [128, (2 * TAPS + 2) * TAPW], fp16)
        WQK = sb("WQK", [128, 2, CT, 2 * PAIRS, PAIR_ROWS], fp16)
        WP = sb("WP", [128, 2, CT, CH], fp16)
        WC = sb("WC", [128, CT * TAPS, 2 * OFF_CH], fp16)
        SEL = sb("SEL", [128, 2 * TAPS + QT + 2, 128], fp16)
        C32 = sb("C32", [128, 128 + 128 + HEAD_B + 5], fp32)
        BIAS = sb("BIAS", [128, 4, CT], fp32)
        CBIAS = sb("CBIAS", [128, 2], fp32)
        MXP = sb("MXP", [128, 2 * QT, 2], fp32)
        MX = sb("MX", [128, 2 * QT], fp32)
        MR = sb("MR", [2 * QT, 128], fp16)
        ORS = sb("ORS", [128, QT], fp32)
        ST6 = sb("ST6", [128, 6, 6], fp32)
        MV = sb("MV", [128, 2], fp32)
        GM = sb("GM", [128, 8], fp32)
        BST = sb("BST", [128, CT, 2 * BATCH, 6], fp32)
        BMV = sb("BMV", [128, CT, 2], fp32)
        BSC = sb("BSC", [128, 4, CT], fp32)
        CV = P32[:, 0, :]
        POSS = sb("POSS", [128, PIX], fp16)
        RMX = sb("RMX", [128, 1], fp32)
        FAR = sb("FAR", [1, 2], mybir.dt.int32)
        FMX = sb("FMX", [1, 2], fp32)
        TV = P32
        H16 = PL[:, 0, :]
        HL = sb("HL", [128, 3, PIX], fp16)
        XPF = XP[:, :, :, :, :].rearrange("p a t h w -> p (a t h w)")[:, 0:2 * CT * PIX].bitcast(fp32)
        HX = XPF.rearrange("p (k n) -> p k n", k=3)
        YS = XPF.rearrange("p (t n) -> p t n", t=CT)
        M32 = sb("M32", [128, 2, MCOLS], fp32)
        CLIP, MSK = M32[0:BOTH, 0, 0:HALF], M32[0:BOTH, 1, 0:HALF]
        MHL = sb("MHL", [128, 2, 2, MCOLS], fp16)
        ZHL = PL[:, 1:3, :].rearrange("p a n -> p (a n)")[:, 0:4 * CH].rearrange("p (a b n) -> p a b n", a=2, b=2)

        WDH, WDL, WVO = 0, TAPS * TAPW, 2 * TAPS * TAPW
        SELP, SELM, SELY, SELX, ZERO = 0, TAPS, 2 * TAPS, 2 * TAPS + QT, 2 * TAPS + QT + 1
        IDENT, GMAT, CMB, COL = C32[:, 0:128], C32[:, 128:256], C32[:, 256:256 + HEAD_B], 256 + HEAD_B
        IS_POS, IS_MASK, NEG_POS, IS_LO, MHALF = [C32[:, COL + n:COL + n + 1] for n in range(5)]

        G = [ctx.enter_context(nc.psum_tensor(f"G{n}", [128, HALF], fp32)) for n in range(2)]
        R6 = ctx.enter_context(nc.psum_tensor("R6", [128, 6, HALF], fp32))
        ST = [R6[:, 2 * n:2 * n + 2, :].rearrange("p a n -> p (a n)") for n in range(2)]
        O = [R6[:, 4 + n, 0:QT * (HD + 1)].rearrange("p (q d) -> p q d", q=QT) for n in range(2)]

        consts_in = sem("consts_in")
        maxunit_in = sem("maxunit_in")
        stage_in = [sem(f"stage_in{n}") for n in range(3)]
        cleared = sem("cleared")
        half_bias = sem("half_bias")
        border_zero = sem("border_zero")
        w_high = sem("w_high")
        w_low = sem("w_low")
        x_in = sem("x_in")
        chunk_full = sem("chunk_full")
        act_read = sem("act_read")
        dve_read = sem("dve_read")
        gn_stats = sem("gn_stats")
        gn_var = sem("gn_var")
        gn_rstd = sem("gn_rstd")
        gn_shift = sem("gn_shift")
        xn_ready = sem("xn_ready")
        x_split = sem("x_split")
        x_biased = sem("x_biased")
        xph_ready = sem("xph_ready")
        xpl_ready = sem("xpl_ready")
        max_ready = sem("max_ready")
        maxrow_in = sem("maxrow_in")
        scores_full = sem("scores_full")
        p_exp = sem("p_exp")
        p_low_dve = sem("p_low_dve")
        p_low_pool = sem("p_low_pool")
        pv_done = sem("pv_done")
        o_norm = sem("o_norm")
        x1_out = sem("x1_out")
        mask_ready = sem("mask_ready")
        pos_ready = sem("pos_ready")
        rows_max = sem("rows_max")
        reach_known = sem("reach_known")
        hat_ready = sem("hat_ready")
        hl_ready = sem("hl_ready")
        m_high = sem("m_high")
        m_low = sem("m_low")
        sampled = sem("sampled")
        y_act = sem("y_act")
        y_dve = sem("y_dve")
        y_stats = sem("y_stats")
        y_out = sem("y_out")
        dve_chain = sem("dve_chain")
        hats_scaled = sem("hats_scaled")
        first_hats = sem("first_hats")
        bn_var = sem("bn_var")
        bn_rstd = sem("bn_rstd")
        bn_ready = sem("bn_ready")
        yf_in = [sem(f"yf_in{n}") for n in range(3)]
        xf_in = [sem(f"xf_in{n}") for n in range(3)]
        gelu_done = sem("gelu_done")
        added = sem("added")
        out_done = [sem(f"out_done{n}") for n in range(3)]
        count_of = {"F": chunk_full, "A": act_read, "D": dve_read}

        stage = [P32[:, :, :].rearrange("p a n -> p (a n)")[:, n * TAPW:(n + 1) * TAPW] for n in range(2)]
        stage.append(M32[:, :, :].rearrange("p a n -> p (a n)")[:, 0:TAPW])
        pieces = []
        for t in range(CT):
            n = 2 * PAIRS * 2 * HD
            dst = [[WQK[:, hl, t, :, half * HEAD_B:half * HEAD_B + HD] for hl in range(2)] for half in range(2)]
            pieces.append((wqk[:, t * n:(t + 1) * n], n, dst))
        pieces.append((wv, TAPW, [[WALL[:, WVO + hl * TAPW:WVO + (hl + 1) * TAPW] for hl in range(2)]]))
        pieces.append((wp, TAPW, [[WP[:, hl, :, :].rearrange("p t n -> p (t n)") for hl in range(2)]]))
        pieces.append((wc, CT * TAPS * OFF_CH, [[WC[:, :, hl * OFF_CH:(hl + 1) * OFF_CH] for hl in range(2)]]))
        START_PIECES = CT + 1
        for n in range(TAPS):
            pieces.append((wd[:, n * TAPW:(n + 1) * TAPW], TAPW,
                           [[WALL[:, o + n * TAPW:o + (n + 1) * TAPW] for o in (WDH, WDL)]]))

        def staged(n, k):
            src, cols, dst = pieces[n]
            s = stage[n % 3][:, 0:cols]
            if len(dst) == 2:
                return s.rearrange("p (m a d) -> p m a d", a=2, d=HD)[:, :, k, :]
            if dst[0][0].shape[1:] != s.shape[1:]:
                return s.rearrange("p (m d) -> p m d", d=OFF_CH)
            return s

        NP = len(pieces)
        ring = [X1[:, :, :].rearrange("p t n -> p (t n)"), XN[:, :, :].rearrange("p t n -> p (t n)"),
                XA[:, :, :, :].rearrange("p a t n -> p (a t n)").bitcast(fp32)]

        def YF(n):
            return WALL[:, (n % 3) * 2 * CT * PIX:(n % 3 + 1) * 2 * CT * PIX].bitcast(fp32)

        def XF(n):
            return ring[n % 3]

        ON = XN[:, :, :].rearrange("p t n -> p (t n)").rearrange("p (q c) -> p q c", q=QT)
        X1F, YSF = ring[0], YS[:, :, :].rearrange("p t n -> p (t n)")
        SELF = SEL[:, :, :].rearrange("p a n -> p (a n)")
        START_NAMES = [n for n, _ in START]

        def cols_of(h):
            return slice(h * HALF, (h + 1) * HALF)

        def high_view(s):
            return P32[:, s % 3, :].bitcast(bf16).rearrange("p (n two) -> p n two", two=2)[:, :, 1]

        def columns(n, first):
            return bass.ds(n + first, 128)

        def snapped(eng, sec):
            sec.base = {w: eng.snap(v) for w, v in sec.base.items()}
            return sec

        def next_step(ky, j):
            return (j + 1, ky) if j < QT - 1 else (0, (ky + 1) % KY)

        def by_reach(eng, far, taps):
            with eng.If(far < 1):
                taps(NEAR_OFF)
            with eng.Else():
                taps(MAX_OFF)

        block = ctx.enter_context(nc.Block())

        @block.sync
        def _(sp):
            def load_x(b):
                sp.dma_start(X1F, x[bass.ds(b, 1), :, :].rearrange("a p n -> (a p) n")).then_inc(x_in, 16)

            def maxima_row(i):
                for hd in range(2):
                    sp.dma_start(QS[MAX_ROW:MAX_ROW + 1, i % 2, hd, :],
                                 MR[hd * QT:(hd + 1) * QT, :]).then_inc(maxrow_in, 16)

            def load_piece(n):
                if n >= 3:
                    sp.wait_ge(w_low, n - 2)
                sp.dma_start(stage[n % 3][:, 0:pieces[n][1]], pieces[n][0]).then_inc(stage_in[n % 3], 16)

            for n in range(3):
                load_piece(n)
            load_x(0)
            sp.dma_start(C32[:, :], c32).then_inc(consts_in, 16)
            load_piece(3)
            sp.dma_start(SELF, c16).then_inc(consts_in, 16)
            for n, a in enumerate((bias_p, bias_d, gamma, beta)):
                sp.dma_start(BIAS[:, n, :], a).then_inc(consts_in, 16)
            sp.wait_ge(cleared, 1)
            for r in (0, HEAD_B):
                sp.dma_start(CBIAS[r:r + OFF_CH, 0:1], bias_c).then_inc(consts_in, 16)
            sp.dma_start(POSS[GRID_ROW:ONES_ROW + 1, :], grid[0:2 * TAPS + 1, :]).then_inc(consts_in, 16)
            for pp in range(2):
                for hd in range(2):
                    sp.dma_start(KL[MAX_ROW:MAX_ROW + 1, pp, hd, :],
                                 grid[2 * TAPS + 1:2 * TAPS + 2, :]).then_inc(maxunit_in, 16)
            for n in range(START_PIECES, NP):
                load_piece(n)

            def batch(b, next_x):
                sec = before_taps(b)
                for i in range(1, PAIRS):
                    sp.wait_ge(act_read, sec.at(("maxT", i), "A"))
                    maxima_row(i)
                sp.wait_ge(dve_read, sec.at(("proj", CT - 1, 1), "D"))
                sp.dma_start(x1_d[bass.ds(b, 1), :, :].rearrange("a p n -> (a p) n"), X1F).then_inc(x1_out, 16)
                sp.wait_ge(xn_ready, b * 6 + 6)
                sp.wait_ge(x1_out, b * 16 + 16)
                load_x(next_x)
                sp.wait_ge(act_read, last_column(b).at(("maxT", 0), "A"))
                maxima_row(0)

            sp.wait_ge(act_read, start_section().at(("maxT", 0), "A"))
            maxima_row(0)
            if BATCH > 1:
                with sp.Fori(0, BATCH - 1) as b:
                    batch(b, b + 1)
            batch(BATCH - 1, 0)
            sp.wait_ge(maxrow_in, 32 * (BATCH * PAIRS + 1))
            sp.wait_ge(x_biased, 3 * (BATCH + 1))
            sp.wait_ge(y_out, BATCH * 16)
            sp.wait_ge(y_stats, BATCH)
            for n in range(BATCH):
                if n >= 3:
                    sp.wait_ge(out_done[n % 3], 16 * (n // 3))
                sp.dma_start(YF(n), y_d[n, :, :]).then_inc(yf_in[n % 3], 16)
                sp.dma_start(XF(n), x1_d[n, :, :]).then_inc(xf_in[n % 3], 16)

        @block.gpsimd
        def _(pool):
            XPV = XP[:, :, :, :, :].rearrange("p a t h w -> p (a t) h w")

            def group_rstd(count):
                pool.wait_ge(gn_var, count)
                pool.tensor_tensor(GM[:, 4:5], GM[:, 3:4], MHALF, ALU.pow).then_inc(gn_rstd, 1)

            pool.memset(WQK[:, :, :, :, :].rearrange("p a t m n -> p (a t m) n")[:, :, HD:HEAD_B], 0.0)
            for t in (QS, KS, KL):
                pool.memset(t[:, :, :, :].rearrange("p a b n -> p (a b n)"), 0.0)
            pool.memset(POSS[:, :], 0.0)
            pool.memset(CBIAS[:, :], 0.0)
            pool.memset(RMX[:, :], 0.0)
            pool.memset(VS[:, :, :, 2 * HD:2 * HD + 1], 1.0).then_inc(cleared, 1)
            for a in range(2 * CT):
                last = pool.memset(XPV[:, a, :, :], 0.0)
            last.then_inc(border_zero, 1)
            pool.memset(FAR[:, 1:2], 0).then_inc(hl_ready, 2)
            pool.wait_ge(consts_in, 16 * 9)
            group_rstd(1)
            with pool.Fori(0, BATCH) as b:
                for s in POOL_STEPS:
                    pool.wait_ge(p_exp, b * STEPS + s + 1)
                    pool.tensor_tensor(PL[:, s % 3, :], P32[:, s % 3, :], high_view(s),
                                       ALU.subtract).then_inc(p_low_pool, 1)
                group_rstd(b * 2 + 2)
                def hat_halves(h, buf, count, read_count):
                    v, low = TV[:, 1, cols_of(h)], H16[:, cols_of(h)]
                    pool.wait_ge(dve_read, read_count)
                    pool.tensor_tensor(low, v, IS_LO.to_broadcast([128, HALF]), ALU.mult).then_inc(hats_scaled, 1)
                    pool.wait_ge(hats_scaled, count)
                    pool.tensor_tensor(HL[:, buf, cols_of(h)], v, low, ALU.subtract).then_inc(hl_ready, 1)

                def split_m(buf, segs, count):
                    for n, (lo, hi) in enumerate(segs):
                        o = lo - segs[0][0]
                        pool.wait_ge(m_high, count + n)
                        pool.tensor_tensor(MHL[:, buf, 1, o:o + hi - lo], M32[:, buf, o:o + hi - lo],
                                           MHL[:, buf, 0, o:o + hi - lo], ALU.subtract).then_inc(m_low, 1)

                pool.wait_ge(reach_known, b + 1)
                split_m(0, made_segments(0, 0), b * PER_SEGS + 1)
                far = pool.value_load(FAR[0:1, 0:1])

                def taps(sec, end, seg, hats_0, reach):
                    made = 0
                    for ky in range(KY):
                        for j in range(QT):
                            nj, nky = next_step(ky, j)
                            last_tap = end and ky == KY - 1
                            if not (last_tap and j == QT - 1):
                                segs = made_segments(nj, nky, reach)
                                split_m(nj % 2, segs, seg + (made + 1))
                                made += len(segs)
                            kind, h = PREP_AT.get(j, ("", 0))
                            if kind == "mask" and not last_tap:
                                hat_halves(h, (ky + 1) % KY, hats_0 + (2 * ky + h + 1),
                                           sec.at(("prep", ky, kind, h), "D"))
                            if end and ky * QT + j == RSTD_AT:
                                group_rstd(b * 2 + 3)

                def column(sec, kx, end):
                    sec = snapped(pool, sec)
                    seg = pool.snap(b * PER_SEGS + kx * COLUMN_SEGS + FIRST_SEGS)
                    hats_0 = pool.snap(b * PER_SPLIT_HATS + kx * (2 * KY))
                    by_reach(pool, far, lambda reach: taps(sec, end, seg, hats_0, reach))

                with pool.Fori(0, KX - 1) as kx:
                    column(column_section(b, kx), kx, False)
                column(last_column(b), KX - 1, True)
                pool.wait_ge(y_stats, b + 1)
                pool.wait_ge(y_out, b * 16 + 16)
                zeros = SEL[:, ZERO, 0:PAD].unsqueeze(1).to_broadcast([128, 2 * CT, PAD])
                pool.tensor_tensor(XPV[:, :, 0, :], zeros, zeros, ALU.add)
                pool.memset(XPV[:, :, PAD - 1, :], 0.0)
                for e in (0, PAD - 1):
                    last = pool.memset(XPV[:, :, 1:HW + 1, e], 0.0)
                last.then_inc(border_zero, 1)
            pool.wait_ge(bn_var, 1)
            for t in range(CT):
                last = pool.tensor_tensor(BSC[:, 1, t:t + 1], BSC[:, 0, t:t + 1], MHALF, ALU.pow)
            last.then_inc(bn_rstd, 1)
            for n in range(BATCH):
                pool.wait_ge(added, n + 1)
                pool.dma_start(out[n, :, :], YF(n)).then_inc(out_done[n % 3], 16)
            for n in range(3):
                pool.wait_ge(out_done[n], 16 * len(range(n, BATCH, 3)))

        @block.scalar
        def _(act):
            def chunk(sec, name):
                act.wait_ge(chunk_full, sec.at(name, "F"))
                return G[sec.bank(name)]

            def split_piece(n):
                act.wait_ge(stage_in[n % 3], 16 * (n // 3 + 1))
                for k, (hi, lo) in enumerate(pieces[n][2]):
                    last = act.activation(hi, staged(n, k), ACT.Copy, scale=W_SCALE)
                last.then_inc(w_high, 1)

            def normalise(t):
                act.activation(XN[:, t, :], X1[:, t, :], ACT.Identity, bias=GM[:, 5:6],
                               scale=GM[:, 4:5]).then_inc(xn_ready, 1)

            def bias_residual(t, b):
                act.wait_ge(xn_ready, b * 6 + t + 1)
                act.activation(X1[:, t, :], X1[:, t, :], ACT.Identity, bias=BIAS[:, 0, t:t + 1]).then_inc(x_biased, 1)

            def read_chunk(name, sec, b):
                if name[0] == "v":
                    act.activation(VS[:, name[1], :, HD:2 * HD],
                                   chunk(sec, name)[:, 0:CH].rearrange("p (h d) -> p h d", d=HD),
                                   ACT.Copy, scale=W_UN).then_inc(act_read, 1)
                if name[0] == "qk":
                    _, i, w, h = name
                    ps = chunk(sec, name)
                    for hd in range(2):
                        r = hd * HEAD_B
                        last = act.activation((QS, KS)[w][r:r + HD, i % 2, hd, cols_of(h)], ps[r:r + HD, :],
                                              ACT.Copy, scale=W_UN)
                    last.then_inc(act_read, 1)
                if name[0] == "oT":
                    act.activation(XB[:, 0, name[1], cols_of(name[2])], chunk(sec, name)[:, :],
                                   ACT.Copy).then_inc(act_read, 1)
                if name[0] == "maxT":
                    ps = chunk(sec, name)
                    if not (isinstance(b, int) and b == 0 and name[1] == 0):
                        act.wait_ge(maxrow_in, b * 32 * PAIRS + 32 * name[1])
                    act.activation(MR[:, :], ps[0:2 * QT, 0:128], ACT.Copy,
                                   scale=-1.0 / MAX_UNIT).then_inc(act_read, 1)

            act.wait_ge(cleared, 1)
            for n in range(START_PIECES):
                split_piece(n)
            act.wait_ge(consts_in, 16 * 9)
            act.wait_ge(half_bias, 1)
            act.wait_ge(gn_shift, 1)
            for t in range(CT):
                normalise(t)
            for t in range(CT):
                bias_residual(t, 0)
            sec, n = start_section(), START_PIECES
            for name in START_NAMES:
                read_chunk(name, sec, 0)
                if name[0] in ("v", "qk") and n < NP:
                    split_piece(n)
                    n += 1

            with act.Fori(0, BATCH) as b:
                sec = before_taps(b)
                for s in range(STEPS):
                    act.wait_ge(scores_full, b * STEPS + s + 1)
                    if s >= 3:
                        act.wait_ge(pv_done, b * STEPS + s - 2)
                    act.activation(P32[:, s % 3, :], ST[s % 2], ACT.Exp, scale=SCALE).then_inc(p_exp, 1)
                    i, s16 = divmod(s, 2 * QT)
                    for name in next_chunks(i, s16):
                        read_chunk(name, sec, b)
                for h in range(2):
                    read_chunk(("oT", CT - 1, h), sec, b)
                act.wait_ge(gn_shift, b * 2 + 2)
                act.wait_ge(border_zero, b + 1)
                for t in range(CT):
                    normalise(t)
                    act.wait_ge(xn_ready, b * 6 + 3 + t + 1)
                    act.activation(XP[:, 0, t, 1:HW + 1, 1:HW + 1],
                                   XN[:, t, :].rearrange("p (h w) -> p h w", w=HW),
                                   ACT.Copy).then_inc(xph_ready, 1)
                for h in range(2):
                    ps = chunk(sec, ("conv", h))
                    for r in (0, HEAD_B):
                        last = act.activation(CV[r:r + 2 * OFF_CH, cols_of(h)], ps[r:r + 2 * OFF_CH, :], ACT.Copy)
                    last.then_inc(act_read, 1)
                act.wait_ge(dve_read, sec.at(("comb",), "D"))
                act.activation(MSK, chunk(sec, ("comb",))[0:BOTH, :], ACT.Tanh, bias=CBIAS[0:BOTH, 1:2],
                               scale=0.5).then_inc(act_read, 1)

                def hats(ps, h, read_count):
                    d, v = TV[:, 0, cols_of(h)], TV[:, 1, cols_of(h)]
                    act.activation(d, ps[:, :], ACT.Abs, bias=NEG_POS).then_inc(act_read, 1)
                    act.wait_ge(act_read, read_count)
                    act.activation(v, d, ACT.Relu, bias=1.0, scale=-1.0).then_inc(hat_ready, 1)

                for h in range(2):
                    name = ("first", "pos", h)
                    hats(chunk(sec, name), h, sec.at(name, "A"))
                act.wait_ge(reach_known, b + 1)
                for h in range(2):
                    act.activation(HX[:, 0, cols_of(h)], chunk(sec, ("first", "hx", h))[:, :],
                                   ACT.Copy).then_inc(act_read, 1)
                lo, hi = tap_segments(0, 0)[0]
                act.wait_ge(dve_read, sec.at(("first", "hy"), "D"))
                act.activation(MHL[:, 0, 0, 0:hi - lo], M32[:, 0, 0:hi - lo], ACT.Copy).then_inc(m_high, 1)
                act.activation(ZHL[:, 0, 0, :], chunk(sec, ("first", "z"))[:, 0:CH], ACT.Copy,
                               scale=W_UN).then_inc(act_read, 1)

                far = act.value_load(FAR[0:1, 0:1])

                def taps(sec, end, sampled_0, hats_0, reach):
                    for ky in range(KY):
                        for j in range(QT):
                            step = ky * QT + j
                            nj, nky = next_step(ky, j)
                            buf = nj % 2
                            last_tap = end and ky == KY - 1
                            if not (last_tap and j == QT - 1):
                                segs = made_segments(nj, nky, reach)
                                act.wait_ge(sampled, sampled_0 + step)
                                for n, (lo, hi) in enumerate(segs):
                                    o = lo - segs[0][0]
                                    act.wait_ge(dve_read, sec.at(("hy", ky, j, n), "D"))
                                    act.activation(MHL[:, buf, 0, o:o + hi - lo], M32[:, buf, o:o + hi - lo],
                                                   ACT.Copy).then_inc(m_high, 1)
                            kind, h = PREP_AT.get(j, ("", 0))
                            if PREP_READER.get(kind) == "A" and not last_tap:
                                name = ("prep", ky, kind, h)
                                ps = chunk(sec, name)
                                if kind == "pos":
                                    if h == 0:
                                        act.wait_ge(hl_ready, hats_0 + (2 * ky + 2))
                                    hats(ps, h, sec.at(name, "A"))
                                else:
                                    act.activation(HX[:, (ky + 1) % KY, cols_of(h)], ps[:, :],
                                                   ACT.Copy).then_inc(act_read, 1)
                            if not (last_tap and j == QT - 1):
                                act.activation(ZHL[:, buf, 0, :], chunk(sec, ("z", ky, j))[:, 0:CH], ACT.Copy,
                                               scale=W_UN).then_inc(act_read, 1)
                            if end:
                                if step in NORM_AT and NORM_AT[step][0] == 0:
                                    act.wait_ge(gn_shift, b * 2 + 3)
                                for t in NORM_AT.get(step, ()):
                                    normalise(t)
                                for name in start_at(step):
                                    read_chunk(name, sec, b + 1)
                                for t in BIAS_AT.get(step, ()):
                                    bias_residual(t, b + 1)

                def column(sec, kx, end):
                    sec = snapped(act, sec)
                    sampled_0 = act.snap(b * PER_SAMPLED + kx * (KY * QT) + 1)
                    hats_0 = act.snap(b * PER_SPLIT_HATS + kx * (2 * KY))
                    by_reach(act, far, lambda reach: taps(sec, end, sampled_0, hats_0, reach))
                    return sec

                with act.Fori(0, KX - 1) as kx:
                    column(column_section(b, kx), kx, False)
                sec = column(last_column(b), KX - 1, True)
                act.wait_ge(sampled, b * PER_SAMPLED + PER_SAMPLED)
                for t in range(CT):
                    act.activation(YS[:, t, HALF:PIX], R6[:, 2 * t + 1, :], ACT.Identity,
                                   bias=BIAS[:, 1, t:t + 1]).then_inc(y_act, 1)
                read_chunk(("maxT", 0), sec, b + 1)
                act.wait_ge(y_act, b * CT + CT)
                act.wait_ge(y_dve, b * CT + CT)
                act.dma_start(y_d[bass.ds(b, 1), :, :].rearrange("a p n -> (a p) n"), YSF).then_inc(y_out, 16)
            act.wait_ge(bn_ready, 1)
            for n in range(BATCH):
                act.wait_ge(yf_in[n % 3], 16 * (n // 3 + 1))
                for t in range(CT):
                    y = YF(n)[:, t * PIX:(t + 1) * PIX]
                    act.activation(y, y, ACT.Gelu, bias=BSC[:, 3, t:t + 1], scale=BSC[:, 2, t:t + 1]).then_inc(gelu_done, 1)

        @block.vector
        def _(dve):
            chained = [0, 0]

            def chain_from(base):
                chained[:] = [base, 0]

            def link(ins):
                chained[1] += 1
                ins.then_inc(dve_chain, 1)
                dve.wait_ge(dve_chain, chained[0] + chained[1])

            def expect(name, count):
                if chained[1] != count:
                    raise ValueError(f"{name} is {chained[1]}")

            def chunk(sec, name):
                dve.wait_ge(chunk_full, sec.at(name, "F"))
                return G[sec.bank(name)]

            def split_piece(n):
                dve.wait_ge(w_high, n + 1)
                for k, (hi, lo) in enumerate(pieces[n][2]):
                    last = dve.scalar_tensor_tensor(lo, staged(n, k), W_SCALE, hi, ALU.mult, ALU.subtract)
                last.then_inc(w_low, 1)

            def half_stats(n):
                t, h = divmod(n, 2)
                return dve.bn_stats(ST6[:, n, :], X1[:, t, cols_of(h)])

            def partition_stats(last):
                link(last)
                dve.memset(GM[:, 6:7], 0.0)
                link(dve.bn_aggr(MV[:, :], ST6[:, :, :].rearrange("p a s -> p (a s)")))
                dve.scalar_tensor_tensor(MV[:, 1:2], MV[:, 0:1], MV[:, 0:1], MV[:, 1:2],
                                         ALU.mult, ALU.add).then_inc(gn_stats, 1)

            def group_var(name, sec):
                dve.tensor_copy(GM[:, 0:2], chunk(sec, name)[:, 0:2]).then_inc(dve_read, 1)
                dve.wait_ge(dve_read, sec.at(name, "D"))
                link(dve.scalar_tensor_tensor(GM[:, 2:3], GM[:, 0:1], GM[:, 0:1], GM[:, 1:2],
                                              ALU.mult, ALU.subtract))
                dve.tensor_scalar(GM[:, 3:4], GM[:, 2:3], -1.0, GN_EPS, ALU.mult, ALU.add).then_inc(gn_var, 1)

            def group_shift(count):
                dve.wait_ge(gn_rstd, count)
                dve.scalar_tensor_tensor(GM[:, 5:6], GM[:, 0:1], -1.0, GM[:, 4:5],
                                         ALU.mult, ALU.mult).then_inc(gn_shift, 1)

            def split_x(tile, t, count):
                dve.wait_ge(xn_ready, count)
                link(dve.tensor_copy(tile[:, 0, t, :], XN[:, t, :]))
                dve.tensor_tensor(tile[:, 1, t, :], XN[:, t, :], tile[:, 0, t, :], ALU.subtract).then_inc(x_split, 1)

            def read_chunk(name, sec, b):
                if name[0] == "gn":
                    group_var(name, sec)
                if name[0] == "v":
                    ps = chunk(sec, name)
                    dve.wait_ge(act_read, sec.at(name, "A"))
                    dve.scalar_tensor_tensor(VS[:, name[1], :, 0:HD], ps[:, 0:CH].rearrange("p (h d) -> p h d", d=HD),
                                             W_UN, VS[:, name[1], :, HD:2 * HD],
                                             ALU.mult, ALU.subtract).then_inc(dve_read, 1)
                if name[0] == "qk":
                    _, i, w, h = name
                    ps = chunk(sec, name)
                    dve.wait_ge(act_read, sec.at(name, "A"))

                    def repeat_k():
                        for hd in range(2):
                            r = hd * HEAD_B
                            dve.tensor_copy(KS[HEAD_B - r:HEAD_B - r + HD, i % 2, hd, cols_of(h)],
                                            KS[r:r + HD, i % 2, hd, cols_of(h)])

                    if w == 1 and h == 1:
                        repeat_k()
                    for hd in range(2):
                        r = hd * HEAD_B
                        o = (HEAD_B - r, r)[w]
                        high, low = (QS, KS)[w], (QS, KL)[w]
                        last = dve.scalar_tensor_tensor(low[o:o + HD, i % 2, hd, cols_of(h)], ps[r:r + HD, :], W_UN,
                                                        high[r:r + HD, i % 2, hd, cols_of(h)], ALU.mult, ALU.subtract)
                    last.then_inc(dve_read, 1)
                    if w == 1 and h == 0:
                        repeat_k()
                if name[0] == "oT":
                    _, t, h = name
                    ps = chunk(sec, name)
                    dve.wait_ge(act_read, sec.at(name, "A"))
                    dve.tensor_tensor(XB[:, 1, t, cols_of(h)], ps[:, :], XB[:, 0, t, cols_of(h)],
                                      ALU.subtract).then_inc(dve_read, 1)
                if name[0] == "max":
                    n = name[2]
                    dve.reduce_max(MXP[:, n // 2, n % 2:n % 2 + 1], chunk(sec, name)[:, :], AX.X).then_inc(dve_read, 1)
                    if n == 4 * QT - 1:
                        dve.wait_ge(dve_read, sec.at(name, "D"))
                        dve.reduce_max(MX[:, :], MXP[:, :, :], AX.X).then_inc(max_ready, 1)

            dve.wait_ge(cleared, 1)
            for n in range(START_PIECES):
                split_piece(n)
            dve.wait_ge(consts_in, 16 * 9)
            dve.tensor_scalar_mul(CBIAS[:, 1:2], CBIAS[:, 0:1], 0.5).then_inc(half_bias, 1)
            chain_from(0)
            dve.wait_ge(x_in, 16)
            for n in range(6):
                last = half_stats(n)
            partition_stats(last)
            sec, n = start_section(), START_PIECES
            read_chunk(("gn", 0), sec, 0)
            group_shift(1)
            for t in range(CT):
                split_x(XA, t, t + 1)
            for name in START_NAMES[1:]:
                read_chunk(name, sec, 0)
                if name[0] in ("v", "qk") and n < NP:
                    split_piece(n)
                    n += 1
            expect("START_LINKS", START_LINKS)

            with dve.Fori(0, BATCH) as b:
                chain_from(b * PER_LINKS + START_LINKS)
                sec = before_taps(b)
                for s in range(STEPS + 2):
                    i, s16 = divmod(s, 2 * QT)
                    if s < STEPS:
                        for name in next_chunks(i, s16):
                            read_chunk(name, sec, b)
                    if s in DVE_STEPS:
                        dve.wait_ge(p_exp, b * STEPS + s + 1)
                        dve.tensor_tensor(PL[:, s % 3, :], P32[:, s % 3, :], high_view(s),
                                          ALU.subtract).then_inc(p_low_dve, 1)
                    if s >= 2 and (s - 2) % QT == QT - 1:
                        head = (s - 2) // QT
                        dve.wait_ge(pv_done, b * STEPS + s - 1)
                        link(dve.reciprocal(ORS[:, :], O[head % 2][:, :, HD]))
                        dve.tensor_tensor(ON[:, :, head * HD:(head + 1) * HD], O[head % 2][:, :, 0:HD],
                                          ORS[:, :].unsqueeze(2).to_broadcast([128, QT, HD]),
                                          ALU.mult).then_inc(o_norm, 1)
                for h in range(2):
                    read_chunk(("oT", CT - 1, h), sec, b)
                dve.wait_ge(x_biased, b * 3 + 3)
                for n in range(7):
                    if n < 6:
                        t, h = divmod(n, 2)
                        dve.scalar_tensor_tensor(X1[:, t, cols_of(h)], chunk(sec, ("proj", t, h))[:, :], W_UN,
                                                 X1[:, t, cols_of(h)], ALU.mult, ALU.add).then_inc(dve_read, 1)
                    if n >= 1:
                        dve.wait_ge(dve_read, sec.at(("proj",) + divmod(n - 1, 2), "D"))
                        last = half_stats(n - 1)
                partition_stats(last)
                group_var(("gn", 1), sec)
                group_shift(b * 2 + 2)
                dve.wait_ge(border_zero, b + 1)
                for t in range(CT):
                    split_x(XB, t, b * 6 + 3 + t + 1)
                    dve.wait_ge(x_split, b * 6 + 3 + t + 1)
                    dve.tensor_copy(XP[:, 1, t, 1:HW + 1, 1:HW + 1],
                                    XB[:, 1, t, :].rearrange("p (h w) -> p h w", w=HW)).then_inc(xpl_ready, 1)

                dve.tensor_scalar(CLIP, chunk(sec, ("comb",))[0:BOTH, :], CBIAS[0:BOTH, 0:1], -float(MAX_OFF),
                                  ALU.add, ALU.max).then_inc(dve_read, 1)
                dve.wait_ge(dve_read, sec.at(("comb",), "D"))
                link(dve.tensor_scalar(CLIP, CLIP, float(MAX_OFF), IS_POS[0:BOTH, :], ALU.min, ALU.mult))
                dve.wait_ge(act_read, sec.at(("comb",), "A"))
                link(dve.scalar_tensor_tensor(CLIP, MSK, IS_MASK[0:BOTH, :], CLIP, ALU.mult, ALU.add))
                for h in range(2):
                    half, cols = CLIP[h * HEAD_B:h * HEAD_B + OFF_CH, :], cols_of(h)
                    link(dve.tensor_copy(POSS[0:OFF_CH, cols], half))
                    dve.tensor_tensor(POSS[LO_ROW:LO_ROW + OFF_CH, cols], half, POSS[0:OFF_CH, cols],
                                      ALU.subtract).then_inc(pos_ready, 1)
                dve.tensor_reduce(RMX[0:BOTH, :], CLIP, AX.X, ALU.max,
                                  apply_absolute_value=True).then_inc(rows_max, 1)

                def mask_hats(ps, h, hat_count):
                    v = TV[:, 1, cols_of(h)]
                    dve.wait_ge(hat_ready, hat_count)
                    dve.tensor_tensor(v, ps[:, :], v, ALU.mult).then_inc(dve_read, 1)

                def split_z(buf, name, sec):
                    dve.wait_ge(act_read, sec.at(name, "A"))
                    dve.scalar_tensor_tensor(ZHL[:, buf, 1, :], G[sec.bank(name)][:, 0:CH], W_UN, ZHL[:, buf, 0, :],
                                             ALU.mult, ALU.subtract).then_inc(dve_read, 1)

                for h in range(2):
                    name = ("first", "mask", h)
                    mask_hats(chunk(sec, name), h, b * PER_HATS + h + 1)
                    dve.wait_ge(dve_read, sec.at(name, "D"))
                    link(dve.tensor_tensor(H16[:, cols_of(h)], TV[:, 1, cols_of(h)],
                                           IS_LO.to_broadcast([128, HALF]), ALU.mult))
                    dve.tensor_tensor(HL[:, 0, cols_of(h)], TV[:, 1, cols_of(h)], H16[:, cols_of(h)],
                                      ALU.subtract).then_inc(first_hats, 1)
                dve.reduce_max(FMX[:, 0:1], chunk(sec, ("reach",))[0:1, 0:128], AX.X).then_inc(dve_read, 1)
                dve.wait_ge(dve_read, sec.at(("reach",), "D"))
                dve.tensor_scalar(FAR[:, 0:1], FMX[:, 0:1], NEAR_OFF - 2.0 ** -6, 0.0,
                                  ALU.is_gt, ALU.add).then_inc(reach_known, 1)
                dve.wait_ge(reach_known, b + 1)
                dve.wait_ge(act_read, sec.at(("first", "hx", 1), "A"))
                lo, hi = tap_segments(0, 0)[0]
                dve.tensor_tensor(M32[:, 0, 0:hi - lo], chunk(sec, ("first", "hy"))[:, 0:hi - lo], HX[:, 0, lo:hi],
                                  ALU.mult).then_inc(dve_read, 1)
                split_z(0, ("first", "z"), sec)
                expect("BATCH_LINKS", BATCH_LINKS)
                far = dve.value_load(FAR[0:1, 0:1])

                def taps(sec, end, seg, hats_0, links_0, reach):
                    chain_from(links_0)
                    before, made = 0, 0
                    for ky in range(KY):
                        for j in range(QT):
                            step = ky * QT + j
                            nj, nky = next_step(ky, j)
                            buf = nj % 2
                            last_tap = end and ky == KY - 1
                            if not (last_tap and j == QT - 1):
                                if j == QT - 1:
                                    dve.wait_ge(act_read, sec.at(("prep", ky, "hx", 1), "A"))
                                segs = made_segments(nj, nky, reach)
                                if (ky, j) != (0, 0):
                                    dve.wait_ge(m_low, seg + before)
                                before, made = made, made + len(segs)
                                for n, (lo, hi) in enumerate(segs):
                                    o = lo - segs[0][0]
                                    dve.tensor_tensor(M32[:, buf, o:o + hi - lo],
                                                      chunk(sec, ("hy", ky, j, n))[:, 0:hi - lo],
                                                      HX[:, nky, lo:hi], ALU.mult).then_inc(dve_read, 1)
                            kind, h = PREP_AT.get(j, ("", 0))
                            if PREP_READER.get(kind) == "D" and not last_tap:
                                name = ("prep", ky, kind, h)
                                mask_hats(chunk(sec, name), h, hats_0 + (2 * ky + h + 1))
                            if not (last_tap and j == QT - 1):
                                split_z(buf, ("z", ky, j), sec)
                            if end:
                                if step == 0:
                                    dve.wait_ge(x_in, b * 16 + 32)
                                for n in STATS_AT.get(step, ()):
                                    last = half_stats(n)
                                    if n == 5:
                                        partition_stats(last)
                                if step == SHIFT_AT:
                                    group_shift(b * 2 + 3)
                                for t in SPLIT_AT.get(step, ()):
                                    split_x(XA, t, b * 6 + 6 + t + 1)
                                for name in start_at(step):
                                    read_chunk(name, sec, b + 1)

                def column(sec, kx, end):
                    sec = snapped(dve, sec)
                    seg = dve.snap(b * PER_SEGS + kx * COLUMN_SEGS + FIRST_SEGS)
                    hats_0 = dve.snap(b * PER_HATS + kx * (2 * KY) + 2)
                    links_0 = dve.snap(b * PER_LINKS + (START_LINKS + BATCH_LINKS))
                    by_reach(dve, far, lambda reach: taps(sec, end, seg, hats_0, links_0, reach))

                with dve.Fori(0, KX - 1) as kx:
                    column(column_section(b, kx), kx, False)
                column(last_column(b), KX - 1, True)
                expect("START_LINKS", START_LINKS)

                dve.wait_ge(sampled, b * PER_SAMPLED + PER_SAMPLED)
                for t in range(CT):
                    dve.tensor_scalar_add(YS[:, t, 0:HALF], R6[:, 2 * t, :], BIAS[:, 1, t:t + 1]).then_inc(y_dve, 1)
                for h in range(2):
                    for t in range(CT):
                        dve.wait_ge((y_dve, y_act)[h], b * CT + (t + 1))
                        last = dve.bn_stats(BST[:, t, bass.ds(b * 2 + h, 1), :].rearrange("p a s -> p (a s)"),
                                            YS[:, t, cols_of(h)])
                last.then_inc(y_stats, 1)

            dve.wait_ge(y_stats, BATCH)
            chain_from(BATCH * PER_LINKS + START_LINKS)
            for t in range(CT):
                last = dve.bn_aggr(BMV[:, t, :], BST[:, t, :, :].rearrange("p a s -> p (a s)"))
            link(last)
            dve.tensor_scalar_add(BSC[:, 0, :], BMV[:, :, 1], BN_EPS).then_inc(bn_var, 1)
            dve.wait_ge(bn_rstd, 1)
            link(dve.tensor_tensor(BSC[:, 2, :], BSC[:, 1, :], BIAS[:, 2, :], ALU.mult))
            link(dve.tensor_tensor(BSC[:, 0, :], BMV[:, :, 0], BSC[:, 2, :], ALU.mult))
            dve.tensor_tensor(BSC[:, 3, :], BIAS[:, 3, :], BSC[:, 0, :], ALU.subtract).then_inc(bn_ready, 1)
            for n in range(BATCH):
                dve.wait_ge(xf_in[n % 3], 16 * (n // 3 + 1))
                for t in range(CT):
                    y = YF(n)[:, t * PIX:(t + 1) * PIX]
                    dve.wait_ge(gelu_done, n * CT + t + 1)
                    last = dve.tensor_tensor(y, y, XF(n)[:, t * PIX:(t + 1) * PIX], ALU.add)
                last.then_inc(added, 1)

        @block.tensor
        def _(pe):
            def bank(sec, name):
                for w, count in sec.replaced(name):
                    pe.wait_ge(count_of[w], count)
                return G[sec.bank(name)]

            def products(out, operands):
                for n, (l, r) in enumerate(operands):
                    last = pe.matmul(out, l, r, start=(n == 0), stop=(n == len(operands) - 1))
                return last

            def group_mean(name, sec, count):
                pe.wait_ge(gn_stats, count)
                pe.matmul(bank(sec, name)[:, 0:2], GMAT, MV[:, :], start=True, stop=True).then_inc(chunk_full, 1)

            def z_products(out, j, high, low):
                products(out[:, 0:CH],
                         [(XB[:, xp_, t, j * 128:(j + 1) * 128], (high, low)[wp_](t))
                          for t in range(CT) for xp_, wp_ in ((0, 0), (0, 1), (1, 0))]).then_inc(chunk_full, 1)

            def fill_chunk(name, sec, b):
                if name[0] == "gn":
                    group_mean(name, sec, b * 2 + 1)
                if name[0] == "v":
                    n = name[1]
                    if n == 0:
                        pe.wait_ge(x_split, b * 6 + 3)
                    v_w = [WALL[:, WVO + a * TAPW:WVO + (a + 1) * TAPW].rearrange("p (t c) -> p t c", t=CT)
                           for a in range(2)]
                    products(bank(sec, name)[:, 0:CH],
                             [(XA[:, xp_, t, n * 128:(n + 1) * 128], v_w[wp_][:, t, :])
                              for t in range(CT) for xp_, wp_ in ((0, 0), (0, 1), (1, 0))]).then_inc(chunk_full, 1)
                if name[0] == "qk":
                    _, i, w, h = name
                    products(bank(sec, name)[0:PAIR_ROWS, :],
                             [(WQK[:, wp_, t, 2 * i + w, :], XA[:, xp_, t, cols_of(h)])
                              for t in range(CT) for wp_, xp_ in ((0, 0), (0, 1), (1, 0))]).then_inc(chunk_full, 1)
                if name[0] == "max":
                    _, i, n = name
                    hd, q, h = n // (2 * QT), n // 2 % QT, n % 2
                    if n == 0:
                        pe.wait_ge(dve_read, sec.at(("qk", i, 1, 1), "D"))
                    pe.matmul(bank(sec, name)[:, :], QS[0:PAIR_ROWS, i % 2, hd, q * 128:(q + 1) * 128],
                              KS[0:PAIR_ROWS, i % 2, hd, cols_of(h)], start=True, stop=True).then_inc(chunk_full, 1)
                if name[0] == "oT":
                    _, t, h = name
                    if h == 0:
                        pe.wait_ge(o_norm, b * HEADS + ((t + 1) * 128 + HD - 1) // HD)
                    out = bank(sec, name)
                    for q in range(4):
                        last = pe.transpose(out[:, q * 128:(q + 1) * 128], ON[:, 4 * h + q, t * 128:(t + 1) * 128],
                                            IDENT)
                    last.then_inc(chunk_full, 1)
                if name[0] == "maxT":
                    pe.wait_ge(max_ready, b * PAIRS + name[1] + 1)
                    pe.transpose(bank(sec, name)[0:2 * QT, 0:128], MX[:, :], IDENT).then_inc(chunk_full, 1)

            pe.wait_ge(cleared, 1)
            pe.wait_ge(w_low, START_PIECES)
            pe.wait_ge(consts_in, 16 * 9)
            pe.wait_ge(maxunit_in, 16 * 4)
            sec = start_section()
            for name in START_NAMES:
                fill_chunk(name, sec, 0)
            pe.wait_ge(w_low, NP)

            with pe.Fori(0, BATCH) as b:
                sec = before_taps(b)

                def pv(s, first, count):
                    head, kt = divmod(s, QT)
                    if first == 0:
                        if s in POOL_STEPS:
                            pe.wait_ge(p_low_pool, b * len(POOL_STEPS) + POOL_STEPS.index(s) + 1)
                        else:
                            pe.wait_ge(p_low_dve, b * len(DVE_STEPS) + DVE_STEPS.index(s) + 1)
                        if kt == 0 and head > 1:
                            pe.wait_ge(o_norm, b * HEADS + head - 1)
                    for q in range(first, first + count):
                        out, pixels = O[head % 2][:, q, :], slice(q * 128, (q + 1) * 128)
                        pe.matmul(out, high_view(s)[:, pixels], VS[:, kt, head, HD:VCOL],
                                  start=(kt == 0 and q == 0), stop=False, skip_group_check=True)
                        pe.matmul(out[:, 0:HD], high_view(s)[:, pixels], VS[:, kt, head, 0:HD],
                                  start=False, stop=False, skip_group_check=True)
                        last = pe.matmul(out, PL[:, s % 3, pixels], VS[:, kt, head, HD:VCOL],
                                         start=False, stop=(kt == QT - 1), skip_group_check=True)
                    if first + count == QT:
                        last.then_inc(pv_done, 1)

                for s in range(STEPS + 2):
                    i, s16 = divmod(s, 2 * QT)
                    chunks = []
                    if s < STEPS:
                        hd, kt = divmod(s16, QT)
                        chunks = next_chunks(i, s16)
                        if s16 == 0:
                            pe.wait_ge(maxrow_in, b * 32 * PAIRS + 32 * (i + 1))
                        if s >= 2:
                            pe.wait_ge(p_exp, b * STEPS + s - 1)
                        for h in range(2):
                            if h == 1 and chunks and chunks[0][0] == "max":
                                fill_chunk(chunks.pop(0), sec, b)
                            out = ST[s % 2][:, cols_of(h)]
                            pe.matmul(out, KS[0:PAIR_ROWS, i % 2, hd, kt * 128:(kt + 1) * 128],
                                      QS[0:PAIR_ROWS, i % 2, hd, cols_of(h)], start=True, stop=False)
                            last = pe.matmul(out, KL[0:PAIR_ROWS, i % 2, hd, kt * 128:(kt + 1) * 128],
                                             QS[0:PAIR_ROWS, i % 2, hd, cols_of(h)], start=False, stop=True)
                        last.then_inc(scores_full, 1)
                    for k in range(4):
                        if k % 2 == 0 and chunks:
                            fill_chunk(chunks.pop(0), sec, b)
                        if s >= 2:
                            pv(s - 2, 2 * k, 2)
                    for name in chunks:
                        fill_chunk(name, sec, b)

                for h in range(2):
                    fill_chunk(("oT", CT - 1, h), sec, b)
                pe.wait_ge(dve_read, sec.at(("oT", CT - 1, 1), "D"))
                for t in range(CT):
                    for h in range(2):
                        products(bank(sec, ("proj", t, h))[:, :],
                                 [(WP[:, wp_, k, t * 128:(t + 1) * 128], XB[:, xp_, k, cols_of(h)])
                                  for k in range(CT) for wp_, xp_ in ((0, 0), (0, 1), (1, 0))]).then_inc(chunk_full, 1)
                group_mean(("gn", 1), sec, b * 2 + 2)

                outs = [bank(sec, ("conv", h)) for h in range(2)]
                for a, ready in ((0, xph_ready), (1, xpl_ready)):
                    for h in range(2):
                        for n, (t, kx, ky) in enumerate([(t, kx, ky) for t in range(CT) for kx in range(KX)
                                                         for ky in range(KY)]):
                            if h == 0 and n % TAPS == 0:
                                pe.wait_ge(ready, b * 3 + t + 1)
                            m = a * CT * TAPS + n
                            row, r = h * (HW // 2) + ky, m % 2 * HEAD_B
                            last = pe.matmul(outs[h][r:r + 2 * OFF_CH, :], WC[:, t * TAPS + kx * KY + ky, :],
                                             XP[:, a, t, row:row + HW // 2, kx:kx + HW],
                                             start=(m < 2), stop=(m >= 2 * CT * TAPS - 2))
                        if a == 1:
                            last.then_inc(chunk_full, 1)
                out = bank(sec, ("comb",))
                for h, (lo, hi) in enumerate(((0, HEAD_B), (HEAD_B, BOTH))):
                    pe.wait_ge(act_read, sec.at(("conv", h), "A"))
                    last = pe.matmul(out[lo:hi, :], CMB[:, 0:hi - lo], CV[:, cols_of(h)], start=True, stop=True)
                last.then_inc(chunk_full, 1)

                for k in range(6):
                    last = pe.matmul(R6[:, k, :], SEL[:, ZERO, :], SELF[:, 0:HALF], start=True, stop=False,
                                     skip_group_check=True)
                last.then_inc(sampled, 1)

                for kind, sel in (("pos", SELP), ("mask", SELM)):
                    for h in range(2):
                        if kind == "pos":
                            pe.wait_ge(pos_ready, b * 2 + h + 1)
                        pe.matmul(bank(sec, ("first", kind, h))[:, :], SEL[:, sel, :], POSS[:, cols_of(h)],
                                  start=True, stop=True).then_inc(chunk_full, 1)
                pe.wait_ge(rows_max, b + 1)
                pe.transpose(bank(sec, ("reach",))[0:1, 0:128], RMX[:, :], IDENT).then_inc(chunk_full, 1)
                for h in range(2):
                    pe.wait_ge(first_hats, b * 2 + h + 1)
                    pe.matmul(bank(sec, ("first", "hx", h))[:, :], SEL[:, SELX, :], HL[:, 0, cols_of(h)],
                              start=True, stop=True).then_inc(chunk_full, 1)
                lo, hi = tap_segments(0, 0)[0]
                pe.wait_ge(reach_known, b + 1)
                pe.matmul(bank(sec, ("first", "hy"))[:, 0:hi - lo], SEL[:, SELY, :], HL[:, 0, lo:hi],
                          start=True, stop=True).then_inc(chunk_full, 1)
                z_products(bank(sec, ("first", "z")), 0, lambda t: WALL[:, WDH + t * CH:WDH + (t + 1) * CH],
                           lambda t: WALL[:, WDL + t * CH:WDL + (t + 1) * CH])

                far = pe.value_load(FAR[0:1, 0:1])

                def taps(sec, kx, end, seg, hats_0, reach):
                    made = 0
                    z_high, z_low = sec.base["A"], sec.base["D"]
                    for ky in range(KY):
                        for j in range(QT):
                            step = ky * QT + j
                            nj, nky = next_step(ky, j)
                            buf = j % 2
                            last_tap = end and ky == KY - 1
                            has_next = not (last_tap and j == QT - 1)
                            now = tap_segments(j, ky, reach)
                            segs = made_segments(nj, nky, reach) if has_next else []

                            def y_hats(n):
                                lo, hi = segs[n]
                                pe.matmul(bank(sec, ("hy", ky, j, n))[:, 0:hi - lo], SEL[:, SELY + nj, :],
                                          HL[:, nky, lo:hi], start=True, stop=True).then_inc(chunk_full, 1)

                            def sample(z_part, m_part, tiles=range(CT)):
                                for t in tiles:
                                    for lo, hi in now:
                                        o = lo - now[0][0]
                                        bk = 2 * t + lo // HALF
                                        last = pe.matmul(R6[:, bk, lo % HALF:lo % HALF + hi - lo],
                                                         ZHL[:, buf, z_part, t * 128:(t + 1) * 128],
                                                         MHL[:, buf, m_part, o:o + hi - lo],
                                                         start=False, stop=False, skip_group_check=True)
                                return last

                            if j == QT - 1 and has_next:
                                pe.wait_ge(hl_ready, hats_0 + (2 * ky + 2))
                            if segs:
                                y_hats(0)
                            pe.wait_ge(m_high, seg + made)
                            pe.wait_ge(act_read, z_high)
                            sample(0, 0)
                            if len(segs) == 2:
                                y_hats(1)
                            early = range(0)
                            if j in PREP_AT and not last_tap:
                                if len(segs) == 2:
                                    pe.wait_ge(m_low, seg + made)
                                    early = range(CT - 1)
                                    sample(0, 1, early)
                                kind, h = PREP_AT[j]
                                if kind == "hx":
                                    pe.wait_ge(hl_ready, hats_0 + (2 * ky + h + 1))
                                    lhs, rhs = SEL[:, SELX, :], HL[:, (ky + 1) % KY, cols_of(h)]
                                else:
                                    sel = (SELP if kind == "pos" else SELM) + ky + 1
                                    lhs, rhs = SELF[:, bass.ds(kx * (KY * 128) + sel * 128, 128)], POSS[:, cols_of(h)]
                                pe.matmul(bank(sec, ("prep", ky, kind, h))[:, :], lhs, rhs,
                                          start=True, stop=True).then_inc(chunk_full, 1)
                            z_before = z_low
                            if has_next:
                                name = ("z", ky, j)
                                tap = kx * (KY * TAPW) + (ky + (j == QT - 1)) * TAPW
                                z_products(bank(sec, name), nj,
                                           lambda t: WALL[:, bass.ds(tap + (WDH + t * CH), CH)],
                                           lambda t: WALL[:, bass.ds(tap + (WDL + t * CH), CH)])
                                z_high, z_low = sec.at(name, "A"), sec.at(name, "D")
                            if not early:
                                pe.wait_ge(m_low, seg + made)
                            sample(0, 1, range(len(early), CT))
                            pe.wait_ge(dve_read, z_before)
                            start = start_at(step) if end else []
                            for t in range(CT):
                                last = sample(1, 0, [t])
                                if t < CT - 1 and t < len(start):
                                    fill_chunk(start[t], sec, b + 1)
                            for name in start[CT - 1:]:
                                fill_chunk(name, sec, b + 1)
                            last.then_inc(sampled, 1)
                            made += len(segs)

                def column(sec, kx, end):
                    sec = snapped(pe, sec)
                    seg = pe.snap(b * PER_SEGS + kx * COLUMN_SEGS + FIRST_SEGS)
                    hats_0 = pe.snap(b * PER_SPLIT_HATS + kx * (2 * KY) + 2)
                    by_reach(pe, far, lambda reach: taps(sec, kx, end, seg, hats_0, reach))
                    return sec

                with pe.Fori(0, KX - 1) as kx:
                    column(column_section(b, kx), kx, False)
                sec = column(last_column(b), KX - 1, True)
                fill_chunk(("maxT", 0), sec, b + 1)
                pe.wait_ge(y_act, b * CT + CT)
                pe.wait_ge(y_dve, b * CT + CT)


def shape_constants():
    m = np.arange(128)
    sel = np.zeros((128, 2 * TAPS + QT + 2, 128), np.float16)
    for i in range(TAPS):
        for r in (0, LO_ROW, GRID_ROW):
            sel[r + i, i, 0:64] = 1
            sel[r + TAPS + i, i, 64:128] = 1
            if r < GRID_ROW:
                sel[r + 2 * TAPS + i, TAPS + i, 64:128] = 1
        sel[ONES_ROW, TAPS + i, :] = 1
    for j in range(QT):
        y = TILE_ROWS * j + m // HW
        sel[y, 2 * TAPS + j, m] = 1
        sel[32 + y, 2 * TAPS + j, m] = 1
    for r in (64, 96):
        sel[r + m % HW, 2 * TAPS + QT, m] = 1
    grid = np.zeros((2 * TAPS + 2, HW, HW), np.float16)
    for i in range(TAPS):
        kx, ky = divmod(i, KY)
        grid[i] = (np.arange(HW) - 1 + ky)[:, None]
        grid[TAPS + i] = (np.arange(HW) - 1 + kx)[None, :]
    grid[2 * TAPS] = 1
    grid[2 * TAPS + 1] = MAX_UNIT
    c32 = np.zeros((128, 128 + 128 + HEAD_B + 5), np.float32)
    c32[:, 0:128] = np.eye(128)
    per = 128 // GN_GROUPS
    c32[:, 128:256] = np.kron(np.eye(GN_GROUPS), np.full((per, per), 1.0 / per))
    for r in range(OFF_CH):
        c32[[r, OFF_CH + r, HEAD_B + r, HEAD_B + OFF_CH + r], 256 + r] = W_UN
    col = 256 + HEAD_B
    c32[:, col] = m % HEAD_B < 2 * TAPS
    c32[:, col + 1] = (m % HEAD_B >= 2 * TAPS) & (m % HEAD_B < OFF_CH)
    c32[:, col + 2] = -(m % 32)
    c32[:, col + 3] = m // 32 % 2
    c32[:, col + 4] = -0.5
    return sel.reshape(128, -1), grid.reshape(2 * TAPS + 2, -1), c32


def kernel(x, L0_conv_w_qkv, L0_conv_w_proj, L0_conv_b_proj, L1_conv_proj_w, L1_conv_proj_b, L1_conv_off_w,
           L1_conv_off_b, L1_conv_mask_w, L1_conv_mask_b, L1_conv_gamma, L1_conv_beta):
    import concourse.bacc as bacc
    from concourse.bass_utils import run_bass_kernel_spmd

    x = np.asarray(x)
    qkv = np.asarray(L0_conv_w_qkv).reshape(3, PAIRS, 2, HD, PART, CT)
    per_channel = lambda a: np.asarray(a).reshape(PART, CT)
    off = np.asarray(L1_conv_off_w).reshape(3, 3, 2, CH, 3, 3).transpose(2, 1, 0, 3, 4, 5).reshape(2 * TAPS, CH, 3, 3)
    mask = np.asarray(L1_conv_mask_w).reshape(3, 3, CH, 3, 3).transpose(1, 0, 2, 3, 4).reshape(TAPS, CH, 3, 3)
    wc = np.concatenate([off, mask], 0).reshape(OFF_CH, PART, CT, 3, 3).transpose(1, 2, 4, 3, 0)
    off_b = np.asarray(L1_conv_off_b).reshape(3, 3, 2).transpose(2, 1, 0).reshape(-1)
    mask_b = np.asarray(L1_conv_mask_b).reshape(3, 3).T.reshape(-1)
    c16, grid, c32 = shape_constants()
    arrays = {
        "x": x.reshape(BATCH, PART, CT * PIX),
        "wqk": qkv[0:2].transpose(4, 5, 1, 0, 2, 3).reshape(PART, -1),
        "wv": np.asarray(L0_conv_w_qkv).reshape(3, CH, PART, CT)[2].transpose(1, 2, 0).reshape(PART, -1),
        "wp": np.asarray(L0_conv_w_proj).reshape(PART, CT, CT, PART).transpose(3, 2, 1, 0).reshape(PART, -1),
        "wd": np.asarray(L1_conv_proj_w).reshape(PART, CT, PART, CT, 3, 3).transpose(2, 5, 4, 3, 1, 0).reshape(PART, -1),
        "wc": wc.reshape(PART, -1),
        "bias_p": per_channel(L0_conv_b_proj),
        "bias_c": np.concatenate([off_b, mask_b])[:, None],
        "bias_d": per_channel(L1_conv_proj_b),
        "gamma": per_channel(L1_conv_gamma),
        "beta": per_channel(L1_conv_beta),
        "c16": c16,
        "grid": grid,
        "c32": c32,
    }
    arrays = {k: np.ascontiguousarray(v) for k, v in arrays.items()}
    nc = bacc.Bacc("TRN2", target_bir_lowering=False, num_devices=1)
    args = [nc.dram_tensor(k, v.shape, mybir.dt.from_np(v.dtype), kind="ExternalInput").ap() for k, v in arrays.items()]
    shape = [BATCH, PART, CT * PIX]
    out = nc.dram_tensor("out", shape, mybir.dt.float32, kind="ExternalOutput").ap()
    x1_d = nc.dram_tensor("x1_scratch", shape, mybir.dt.float32, kind="Internal").ap()
    y_d = nc.dram_tensor("y_scratch", shape, mybir.dt.float32, kind="Internal").ap()
    build(nc, *args, out, x1_d, y_d)
    r = run_bass_kernel_spmd(nc, [arrays], core_ids=[0])
    return r.results[0]["out"].reshape(BATCH, CH, HW, HW)
```

```python
import concourse.bass as bass
from concourse import mybir
from contextlib import ExitStack
import numpy as np

BATCH, CH, HW, PIX = 8, 384, 32, 1024
PART = 128
CT = CH // PART
HEADS, HD = 8, 48
PAIRS = HEADS // 2
HEAD_B = 64
PAIR_ROWS = HEAD_B + HD
GN_GROUPS = 32
GN_EPS, BN_EPS = 1e-5, 1e-5
TAPS, KX, KY = 9, 3, 3
MAX_OFF = HW // 4
NEAR_OFF = 3
OFF_CH = 3 * TAPS
LO_ROW, GRID_ROW = 32, 64
ONES_ROW = GRID_ROW + 2 * TAPS
CONV_TILES = PART // LO_ROW
HALF = 512
QT = PIX // PART
TILE_ROWS = HW // QT
VCOL = 2 * HD + 1
SCALE = HD ** -0.5
W_SCALE = 256.0
W_UN = 1.0 / W_SCALE
MAX_ROW, MAX_UNIT = HD, 16.0
PAD = HW + 2
MCOLS = (TILE_ROWS + 2 * MAX_OFF) * HW
STEPS = HEADS * QT
TAP_STEPS = TAPS * QT


def tap_segments(j, ky, reach=MAX_OFF):
    if (j, ky) == (0, 0):
        reach = MAX_OFF
    first = max(0, TILE_ROWS * j + 1 - ky - reach)
    last = min(HW - 1, TILE_ROWS * j + TILE_ROWS + reach - ky)
    lo, hi = first * HW, (last + 1) * HW
    segs = []
    if lo < HALF:
        segs.append((lo, min(hi, HALF)))
    if hi > HALF:
        segs.append((max(lo, HALF), hi))
    return segs


def made_segments(j, ky, reach=MAX_OFF):
    segs = tap_segments(j, ky, reach)
    if len(segs) == len(tap_segments(j, ky)):
        return segs
    (lo, hi), = segs
    mid = lo + (hi - lo) // HW // 2 * HW
    return [(lo, mid), (mid, hi)]


STATS_AT = {0: (0, 1, 2), 1: (3, 4, 5)}
GROUPS_AT, SHIFT_AT = 2, 3
NORM_AT = {3: (0, 1), 4: (2,)}
SPLIT_AT = {4: (0,), 5: (1, 2)}
BIAS_AT = {14: (0,), 16: (1,), 18: (2,)}
V_AT, QK_AT, MAX_AT = 6, 12, 14

def pair_chunks(i):
    return [(("qk", i, w, h), "AD") for w in range(2) for h in range(2)] \
        + [(("max", i, n), "D") for n in range(4 * QT)] + [(("maxT", i), "A")]


def start_at(step):
    pair, per_step = pair_chunks(0), 4 // (MAX_AT - QK_AT)
    qk, maxima = pair[:4], pair[4:-1]
    if step == GROUPS_AT:
        return [(("gn", 0), "D")]
    if step >= MAX_AT:
        n, steps = step - MAX_AT, KY * QT - MAX_AT
        return maxima[4 * QT * n // steps:4 * QT * (n + 1) // steps]
    v = [(("v", step - V_AT), "AD")] if 0 <= step - V_AT < QT else []
    return (qk[per_step * (step - QK_AT):per_step * (step - QK_AT + 1)] if step >= QK_AT else []) + v


def start_chunks():
    return sum((start_at(step) for step in range(KY * QT)), []) + pair_chunks(0)[-1:]


PREP_AT = {0: ("pos", 0), 1: ("pos", 1), 2: ("mask", 0), 3: ("mask", 1), 4: ("hx", 0), 5: ("hx", 1)}
PREP_READER = {"pos": "A", "mask": "D", "hx": "A"}


def column_chunks(last, start):
    out = []
    for ky in range(KY):
        for j in range(QT):
            end = last and ky == KY - 1
            if not (end and j == QT - 1):
                nj, nky = (j + 1, ky) if j < QT - 1 else (0, (ky + 1) % KY)
                out += [(("hy", ky, j, n), "D") for n in range(len(tap_segments(nj, nky)))]
            if j in PREP_AT and not end:
                out.append((("prep", ky) + PREP_AT[j], PREP_READER[PREP_AT[j][0]]))
            if not (end and j == QT - 1):
                out.append((("z", ky, j), "AD"))
            if start:
                out += start_at(ky * QT + j)
    if start:
        out.append((("maxT", 0), "A"))
    return out


START = start_chunks()
BEFORE_TAPS = sum((pair_chunks(i) for i in range(1, PAIRS)), []) \
    + [(("oT", t, h), "AD") for t in range(CT) for h in range(2)] \
    + [(("proj", t, h), "D") for t in range(CT) for h in range(2)] \
    + [(("gn", 1), "D")] + [(("conv", h), "A") for h in range(2)] + [(("first", "z"), "AD")] + [(("comb",), "AD")] \
    + [(("first",) + PREP_AT[j], PREP_READER[PREP_AT[j][0]]) for j in range(4)] + [(("reach",), "D")] \
    + [(("first",) + PREP_AT[j], PREP_READER[PREP_AT[j][0]]) for j in range(4, 6)] \
    + [(("first", "hy"), "D")]
COLUMN, LAST_COLUMN, FINAL_COLUMN = [column_chunks(*a) for a in ((False, False), (True, True), (True, False))]
PER_BATCH = BEFORE_TAPS + (KX - 1) * COLUMN + LAST_COLUMN
if len(PER_BATCH) % 2:
    BEFORE_TAPS = [("pass", "")] + BEFORE_TAPS
    PER_BATCH = [("pass", "")] + PER_BATCH
if len(COLUMN) % 2 or len(tap_segments(0, 0)) != 1:
    raise ValueError("a column's chunks must pair up")


def reads(chunks, who):
    return sum(r != "" if who == "F" else who in r for _, r in chunks)


class Section:

    def __init__(self, chunks, ahead, batch=0, column=0):
        self.chunks, self.follows, self.start = chunks, bool(ahead), len(ahead)
        self.index = {n: g for g, (n, _) in enumerate(chunks)}
        self.base = {w: batch * reads(PER_BATCH, w) + column * reads(COLUMN, w) + reads(ahead, w) for w in "FAD"}

    def at(self, name, who):
        return self.base[who] + reads(self.chunks[:self.index[name] + 1], who)

    def bank(self, name):
        return (self.start + self.index[name]) % 2

    def replaced(self, name):
        g = self.index[name] - 2
        if g >= 0:
            return [(w, self.base[w] + reads(self.chunks[:g + 1], w)) for w in self.chunks[g][1]]
        return [(w, self.base[w]) for w in "AD"] if self.follows else []


def start_section():
    return Section(START, [])


def before_taps(b):
    return Section(BEFORE_TAPS, START, b)


def column_section(b, kx):
    return Section(COLUMN, START + BEFORE_TAPS, b, kx)


def last_column(b, final=False):
    return Section(FINAL_COLUMN if final else LAST_COLUMN, START + BEFORE_TAPS + (KX - 1) * COLUMN, b)


POOL_STEPS = [s for s in range(STEPS) if s % 3 != 0]
DVE_STEPS = [s for s in range(STEPS) if s % 3 == 0]
NEXT_AT = [[] for _ in range(2 * QT)]
for _n in range(4):
    NEXT_AT[_n].append(("qk", _n // 2, _n % 2))
for _n in range(4 * QT):
    NEXT_AT[4 + _n * 9 // (4 * QT)].append(("max", _n))
NEXT_AT[13].append(("maxT",))


TRANSPOSE_AT = {4: [("oT", 0, 0)], 5: [("oT", 0, 1)], 6: [("oT", 1, 0)], 7: [("oT", 1, 1)]}


def next_chunks(i, s16):
    if i + 1 == PAIRS:
        return list(TRANSPOSE_AT.get(s16, []))
    return [(n[0], i + 1) + n[1:] for n in NEXT_AT[s16]]


START_LINKS, BATCH_LINKS = 6, 20
PER_LINKS = START_LINKS + BATCH_LINKS
FIRST_SEGS = 1
COLUMN_SEGS = sum(n[0] == "hy" for n, _ in COLUMN)
PER_SEGS = FIRST_SEGS + (KX - 1) * COLUMN_SEGS + sum(n[0] == "hy" for n, _ in LAST_COLUMN)
PER_SAMPLED = TAP_STEPS + 1
PER_HATS, PER_SPLIT_HATS = 2 * TAPS, 2 * (TAPS - 1)
BOTH = HEAD_B + OFF_CH


def build(nc, x, wqk, wv, wp, wd, wc, bias_p, bias_c, bias_d, gamma, beta, c16, grid, c32, out, x1_d, y_d):
    fp32, fp16, bf16 = mybir.dt.float32, mybir.dt.float16, mybir.dt.bfloat16
    ALU, ACT, AX = mybir.AluOpType, mybir.ActivationFunctionType, mybir.AxisListType
    ctx = ExitStack()
    with ctx:
        def sb(name, shape, dt):
            return ctx.enter_context(nc.sbuf_tensor(name, shape, dt))

        def sem(name):
            return ctx.enter_context(nc.semaphore(name))

        X1 = sb("X1", [128, CT, PIX], fp32)
        XN = sb("XN", [128, CT, PIX], fp32)
        XA = sb("XA", [128, 2, CT, PIX], fp16)
        XB = sb("XB", [128, 2, CT, PIX], fp16)
        XP = sb("XP", [128, 2, CT, PAD, PAD], fp16)
        QS = sb("QS", [128, 2, 2, PIX], fp16)
        KS = sb("KS", [128, 2, 2, PIX], fp16)
        KL = sb("KL", [128, 2, 2, PIX], fp16)
        VS = sb("VS", [128, QT, HEADS, VCOL + 1], fp16)
        P32 = sb("P32", [128, 3, PIX], fp32)
        PL = sb("PL", [128, 3, PIX], fp16)
        TAPW = CT * CH
        WALL = sb("WALL", [128, (2 * TAPS + 2) * TAPW], fp16)
        WQK = sb("WQK", [128, 2, CT, 2 * PAIRS, PAIR_ROWS], fp16)
        WP = sb("WP", [128, 2, CT, CH], fp16)
        WC = sb("WC", [128, CT * TAPS, 2 * OFF_CH], fp16)
        SEL = sb("SEL", [128, 2 * TAPS + QT + 2, 128], fp16)
        C32 = sb("C32", [128, 128 + 128 + HEAD_B + 5], fp32)
        BIAS = sb("BIAS", [128, 4, CT], fp32)
        CBIAS = sb("CBIAS", [128, 2], fp32)
        MXP = sb("MXP", [128, 2 * QT, 2], fp32)
        MX = sb("MX", [128, 2 * QT], fp32)
        MR = sb("MR", [2 * QT, 128], fp16)
        ORS = sb("ORS", [128, QT], fp32)
        ST6 = sb("ST6", [128, 6, 6], fp32)
        MV = sb("MV", [128, 2], fp32)
        GM = sb("GM", [128, 8], fp32)
        BST = sb("BST", [128, CT, 2 * BATCH, 6], fp32)
        BMV = sb("BMV", [128, CT, 2], fp32)
        BSC = sb("BSC", [128, 4, CT], fp32)
        CV = P32[:, 0, :]
        POSS = sb("POSS", [128, PIX], fp16)
        RMX = sb("RMX", [128, 1], fp32)
        FAR = sb("FAR", [1, 2], mybir.dt.int32)
        FMX = sb("FMX", [1, 2], fp32)
        TV = P32
        H16 = PL[:, 0, :]
        HL = sb("HL", [128, 3, PIX], fp16)
        XPF = XP[:, :, :, :, :].rearrange("p a t h w -> p (a t h w)")[:, 0:2 * CT * PIX].bitcast(fp32)
        HX = XPF.rearrange("p (k n) -> p k n", k=3)
        YS = XPF.rearrange("p (t n) -> p t n", t=CT)
        M32 = sb("M32", [128, 2, MCOLS], fp32)
        CLIP, MSK = M32[0:BOTH, 0, 0:HALF], M32[0:BOTH, 1, 0:HALF]
        MHL = sb("MHL", [128, 2, 2, MCOLS], fp16)
        ZHL = PL[:, 1:3, :].rearrange("p a n -> p (a n)")[:, 0:4 * CH].rearrange("p (a b n) -> p a b n", a=2, b=2)

        WDH, WDL, WVO = 0, TAPS * TAPW, 2 * TAPS * TAPW
        SELP, SELM, SELY, SELX, ZERO = 0, TAPS, 2 * TAPS, 2 * TAPS + QT, 2 * TAPS + QT + 1
        IDENT, GMAT, CMB, COL = C32[:, 0:128], C32[:, 128:256], C32[:, 256:256 + HEAD_B], 256 + HEAD_B
        IS_POS, IS_MASK, NEG_POS, IS_LO, MHALF = [C32[:, COL + n:COL + n + 1] for n in range(5)]

        G = [ctx.enter_context(nc.psum_tensor(f"G{n}", [128, HALF], fp32)) for n in range(2)]
        R6 = ctx.enter_context(nc.psum_tensor("R6", [128, 6, HALF], fp32))
        ST = [R6[:, 2 * n:2 * n + 2, :].rearrange("p a n -> p (a n)") for n in range(2)]
        O = [R6[:, 4 + n, 0:QT * (HD + 1)].rearrange("p (q d) -> p q d", q=QT) for n in range(2)]

        consts_in = sem("consts_in")
        maxunit_in = sem("maxunit_in")
        stage_in = [sem(f"stage_in{n}") for n in range(3)]
        cleared = sem("cleared")
        half_bias = sem("half_bias")
        border_zero = sem("border_zero")
        w_high = sem("w_high")
        w_low = sem("w_low")
        x_in = sem("x_in")
        chunk_full = sem("chunk_full")
        act_read = sem("act_read")
        dve_read = sem("dve_read")
        gn_stats = sem("gn_stats")
        gn_var = sem("gn_var")
        gn_rstd = sem("gn_rstd")
        gn_shift = sem("gn_shift")
        xn_ready = sem("xn_ready")
        x_split = sem("x_split")
        x_biased = sem("x_biased")
        xph_ready = sem("xph_ready")
        xpl_ready = sem("xpl_ready")
        max_ready = sem("max_ready")
        maxrow_in = sem("maxrow_in")
        scores_full = sem("scores_full")
        p_exp = sem("p_exp")
        p_low_dve = sem("p_low_dve")
        p_low_pool = sem("p_low_pool")
        pv_done = sem("pv_done")
        o_norm = sem("o_norm")
        x1_out = sem("x1_out")
        pos_ready = sem("pos_ready")
        rows_max = sem("rows_max")
        reach_known = sem("reach_known")
        hat_ready = sem("hat_ready")
        hl_ready = sem("hl_ready")
        m_high = sem("m_high")
        m_low = sem("m_low")
        sampled = sem("sampled")
        y_act = sem("y_act")
        y_dve = sem("y_dve")
        y_stats = sem("y_stats")
        y_out = sem("y_out")
        dve_chain = sem("dve_chain")
        hats_scaled = sem("hats_scaled")
        first_hats = sem("first_hats")
        bn_var = sem("bn_var")
        bn_rstd = sem("bn_rstd")
        bn_ready = sem("bn_ready")
        yf_in = [sem(f"yf_in{n}") for n in range(4)]
        xf_in = [sem(f"xf_in{n}") for n in range(3)]
        gelu_done = sem("gelu_done")
        added = sem("added")
        out_done = [sem(f"out_done{n}") for n in range(4)]
        count_of = {"F": chunk_full, "A": act_read, "D": dve_read}

        stage = [P32[:, :, :].rearrange("p a n -> p (a n)")[:, n * TAPW:(n + 1) * TAPW] for n in range(2)]
        stage.append(M32[:, :, :].rearrange("p a n -> p (a n)")[:, 0:TAPW])
        pieces = []
        for t in range(CT):
            n = 2 * PAIRS * 2 * HD
            dst = [[WQK[:, hl, t, :, half * HEAD_B:half * HEAD_B + HD] for hl in range(2)] for half in range(2)]
            pieces.append((wqk[:, t * n:(t + 1) * n], n, dst))
        pieces.append((wv, TAPW, [[WALL[:, WVO + hl * TAPW:WVO + (hl + 1) * TAPW] for hl in range(2)]]))
        pieces.append((wp, TAPW, [[WP[:, hl, :, :].rearrange("p t n -> p (t n)") for hl in range(2)]]))
        pieces.append((wc, CT * TAPS * OFF_CH, [[WC[:, :, hl * OFF_CH:(hl + 1) * OFF_CH] for hl in range(2)]]))
        START_PIECES = CT + 1
        for n in range(TAPS):
            pieces.append((wd[:, n * TAPW:(n + 1) * TAPW], TAPW,
                           [[WALL[:, o + n * TAPW:o + (n + 1) * TAPW] for o in (WDH, WDL)]]))

        def staged(n, k):
            src, cols, dst = pieces[n]
            s = stage[n % 3][:, 0:cols]
            if len(dst) == 2:
                return s.rearrange("p (m a d) -> p m a d", a=2, d=HD)[:, :, k, :]
            if dst[0][0].shape[1:] != s.shape[1:]:
                return s.rearrange("p (m d) -> p m d", d=OFF_CH)
            return s

        NP = len(pieces)
        ring = [X1[:, :, :].rearrange("p t n -> p (t n)"), XN[:, :, :].rearrange("p t n -> p (t n)"),
                XA[:, :, :, :].rearrange("p a t n -> p (a t n)").bitcast(fp32)]

        FINAL = [BATCH - 1] + list(range(BATCH - 1))

        def YF(k):
            if k % 4 == 0:
                return YS[:, :, :].rearrange("p t n -> p (t n)")
            return WALL[:, (k % 4 - 1) * 2 * CT * PIX:k % 4 * 2 * CT * PIX].bitcast(fp32)

        def XF(k):
            return ring[k % 3]

        ON = XN[:, :, :].rearrange("p t n -> p (t n)").rearrange("p (q c) -> p q c", q=QT)
        X1F, YSF = ring[0], YS[:, :, :].rearrange("p t n -> p (t n)")
        SELF = SEL[:, :, :].rearrange("p a n -> p (a n)")
        START_NAMES = [n for n, _ in START]

        def cols_of(h):
            return slice(h * HALF, (h + 1) * HALF)

        def high_view(s):
            return P32[:, s % 3, :].bitcast(bf16).rearrange("p (n two) -> p n two", two=2)[:, :, 1]

        def columns(n, first):
            return bass.ds(n + first, 128)

        def snapped(eng, sec):
            sec.base = {w: eng.snap(v) for w, v in sec.base.items()}
            return sec

        def next_step(ky, j):
            return (j + 1, ky) if j < QT - 1 else (0, (ky + 1) % KY)

        def by_reach(eng, far, taps):
            with eng.If(far < 1):
                taps(NEAR_OFF)
            with eng.Else():
                taps(MAX_OFF)

        block = ctx.enter_context(nc.Block())

        @block.sync
        def _(sp):
            def load_x(b):
                sp.dma_start(X1F, x[bass.ds(b, 1), :, :].rearrange("a p n -> (a p) n")).then_inc(x_in, 16)

            def maxima_row(i):
                for hd in range(2):
                    sp.dma_start(QS[MAX_ROW:MAX_ROW + 1, i % 2, hd, :],
                                 MR[hd * QT:(hd + 1) * QT, :]).then_inc(maxrow_in, 16)

            def load_piece(n):
                if n >= 3:
                    sp.wait_ge(w_low, n - 2)
                sp.dma_start(stage[n % 3][:, 0:pieces[n][1]], pieces[n][0]).then_inc(stage_in[n % 3], 16)

            for n in range(3):
                load_piece(n)
            load_x(0)
            sp.dma_start(C32[:, :], c32).then_inc(consts_in, 16)
            load_piece(3)
            sp.dma_start(SELF, c16).then_inc(consts_in, 16)
            for n, a in enumerate((bias_p, bias_d, gamma, beta)):
                sp.dma_start(BIAS[:, n, :], a).then_inc(consts_in, 16)
            sp.wait_ge(cleared, 1)
            for r in (0, HEAD_B):
                sp.dma_start(CBIAS[r:r + OFF_CH, 0:1], bias_c).then_inc(consts_in, 16)
            sp.dma_start(POSS[GRID_ROW:ONES_ROW + 1, :], grid[0:2 * TAPS + 1, :]).then_inc(consts_in, 16)
            for pp in range(2):
                for hd in range(2):
                    sp.dma_start(KL[MAX_ROW:MAX_ROW + 1, pp, hd, :],
                                 grid[2 * TAPS + 1:2 * TAPS + 2, :]).then_inc(maxunit_in, 16)
            for n in range(START_PIECES, NP):
                load_piece(n)

            def batch(b):
                sec = before_taps(b)
                for i in range(1, PAIRS):
                    sp.wait_ge(act_read, sec.at(("maxT", i), "A"))
                    maxima_row(i)
                sp.wait_ge(dve_read, sec.at(("proj", CT - 1, 1), "D"))

            sp.wait_ge(act_read, start_section().at(("maxT", 0), "A"))
            maxima_row(0)
            if BATCH > 1:
                with sp.Fori(0, BATCH - 1) as b:
                    batch(b)
                    sp.dma_start(x1_d[bass.ds(b, 1), :, :].rearrange("a p n -> (a p) n"), X1F).then_inc(x1_out, 16)
                    sp.wait_ge(xn_ready, b * 6 + 6)
                    sp.wait_ge(x1_out, b * 16 + 16)
                    load_x(b + 1)
                    sp.wait_ge(act_read, last_column(b).at(("maxT", 0), "A"))
                    maxima_row(0)
            batch(BATCH - 1)
            sp.wait_ge(xph_ready, BATCH * 3)
            sp.wait_ge(xpl_ready, BATCH * 3)
            for k in range(1, min(3, BATCH)):
                sp.dma_start(XF(k), x1_d[FINAL[k], :, :]).then_inc(xf_in[k % 3], 16)
            sp.wait_ge(y_stats, BATCH)
            if BATCH > 1:
                sp.wait_ge(y_out, (BATCH - 1) * 16)
            for k in range(1, BATCH):
                if k >= 4:
                    sp.wait_ge(out_done[k % 4], 16 * (k // 4))
                sp.dma_start(YF(k), y_d[FINAL[k], :, :]).then_inc(yf_in[k % 4], 16)
                if k >= 3:
                    sp.wait_ge(added, k - 2)
                    sp.dma_start(XF(k), x1_d[FINAL[k], :, :]).then_inc(xf_in[k % 3], 16)

        @block.gpsimd
        def _(pool):
            XPV = XP[:, :, :, :, :].rearrange("p a t h w -> p (a t) h w")

            def group_rstd(count):
                pool.wait_ge(gn_var, count)
                pool.tensor_tensor(GM[:, 4:5], GM[:, 3:4], MHALF, ALU.pow).then_inc(gn_rstd, 1)

            pool.memset(WQK[:, :, :, :, :].rearrange("p a t m n -> p (a t m) n")[:, :, HD:HEAD_B], 0.0)
            for t in (QS, KS, KL):
                pool.memset(t[:, :, :, :].rearrange("p a b n -> p (a b n)"), 0.0)
            pool.memset(POSS[:, :], 0.0)
            pool.memset(CBIAS[:, :], 0.0)
            pool.memset(RMX[:, :], 0.0)
            pool.memset(VS[:, :, :, 2 * HD:2 * HD + 1], 1.0).then_inc(cleared, 1)
            for a in range(2 * CT):
                last = pool.memset(XPV[:, a, :, :], 0.0)
            last.then_inc(border_zero, 1)
            pool.memset(FAR[:, 1:2], 0).then_inc(hl_ready, 2)
            pool.wait_ge(consts_in, 16 * 9)
            group_rstd(1)
            def batch(b, final):
                for s in POOL_STEPS:
                    pool.wait_ge(p_exp, b * STEPS + s + 1)
                    pool.tensor_tensor(PL[:, s % 3, :], P32[:, s % 3, :], high_view(s),
                                       ALU.subtract).then_inc(p_low_pool, 1)
                group_rstd(b * 2 + 2)
                def hat_halves(h, buf, count, read_count):
                    v, low = TV[:, 1, cols_of(h)], H16[:, cols_of(h)]
                    pool.wait_ge(dve_read, read_count)
                    pool.tensor_tensor(low, v, IS_LO.to_broadcast([128, HALF]), ALU.mult).then_inc(hats_scaled, 1)
                    pool.wait_ge(hats_scaled, count)
                    pool.tensor_tensor(HL[:, buf, cols_of(h)], v, low, ALU.subtract).then_inc(hl_ready, 1)

                def split_m(buf, segs, count):
                    for n, (lo, hi) in enumerate(segs):
                        o = lo - segs[0][0]
                        pool.wait_ge(m_high, count + n)
                        pool.tensor_tensor(MHL[:, buf, 1, o:o + hi - lo], M32[:, buf, o:o + hi - lo],
                                           MHL[:, buf, 0, o:o + hi - lo], ALU.subtract).then_inc(m_low, 1)

                pool.wait_ge(reach_known, b + 1)
                split_m(0, made_segments(0, 0), b * PER_SEGS + 1)
                far = pool.value_load(FAR[0:1, 0:1])

                def taps(sec, end, start, seg, hats_0, reach):
                    made = 0
                    for ky in range(KY):
                        for j in range(QT):
                            nj, nky = next_step(ky, j)
                            last_tap = end and ky == KY - 1
                            if not (last_tap and j == QT - 1):
                                segs = made_segments(nj, nky, reach)
                                split_m(nj % 2, segs, seg + (made + 1))
                                made += len(segs)
                            kind, h = PREP_AT.get(j, ("", 0))
                            if kind == "mask" and not last_tap:
                                hat_halves(h, (ky + 1) % KY, hats_0 + (2 * ky + h + 1),
                                           sec.at(("prep", ky, kind, h), "D"))
                            if start and ky * QT + j == GROUPS_AT:
                                group_rstd(b * 2 + 3)

                def column(sec, kx, end, start):
                    sec = snapped(pool, sec)
                    seg = pool.snap(b * PER_SEGS + kx * COLUMN_SEGS + FIRST_SEGS)
                    hats_0 = pool.snap(b * PER_SPLIT_HATS + kx * (2 * KY))
                    by_reach(pool, far, lambda reach: taps(sec, end, start, seg, hats_0, reach))

                with pool.Fori(0, KX - 1) as kx:
                    column(column_section(b, kx), kx, False, False)
                column(last_column(b, final), KX - 1, True, not final)
                if final:
                    return
                pool.wait_ge(y_stats, b + 1)
                pool.wait_ge(y_out, b * 16 + 16)
                zeros = SEL[:, ZERO, 0:PAD].unsqueeze(1).to_broadcast([128, 2 * CT, PAD])
                pool.tensor_tensor(XPV[:, :, 0, :], zeros, zeros, ALU.add)
                pool.memset(XPV[:, :, PAD - 1, :], 0.0)
                for e in (0, PAD - 1):
                    last = pool.memset(XPV[:, :, 1:HW + 1, e], 0.0)
                last.then_inc(border_zero, 1)

            if BATCH > 1:
                with pool.Fori(0, BATCH - 1) as b:
                    batch(b, False)
            batch(BATCH - 1, True)
            pool.wait_ge(bn_var, 1)
            for t in range(CT):
                last = pool.tensor_tensor(BSC[:, 1, t:t + 1], BSC[:, 0, t:t + 1], MHALF, ALU.pow)
            last.then_inc(bn_rstd, 1)
            for k in range(BATCH):
                pool.wait_ge(added, k + 1)
                pool.dma_start(out[FINAL[k], :, :], YF(k)).then_inc(out_done[k % 4], 16)
            for k in range(min(4, BATCH)):
                pool.wait_ge(out_done[k], 16 * len(range(k, BATCH, 4)))

        @block.scalar
        def _(act):
            def chunk(sec, name):
                act.wait_ge(chunk_full, sec.at(name, "F"))
                return G[sec.bank(name)]

            def split_piece(n):
                act.wait_ge(stage_in[n % 3], 16 * (n // 3 + 1))
                for k, (hi, lo) in enumerate(pieces[n][2]):
                    last = act.activation(hi, staged(n, k), ACT.Copy, scale=W_SCALE)
                last.then_inc(w_high, 1)

            def normalise(t):
                act.activation(XN[:, t, :], X1[:, t, :], ACT.Identity, bias=GM[:, 5:6],
                               scale=GM[:, 4:5]).then_inc(xn_ready, 1)

            def bias_residual(t, b):
                act.wait_ge(xn_ready, b * 6 + t + 1)
                act.activation(X1[:, t, :], X1[:, t, :], ACT.Identity, bias=BIAS[:, 0, t:t + 1]).then_inc(x_biased, 1)

            def read_chunk(name, sec, b):
                if name[0] == "v":
                    act.activation(VS[:, name[1], :, HD:2 * HD],
                                   chunk(sec, name)[:, 0:CH].rearrange("p (h d) -> p h d", d=HD),
                                   ACT.Copy, scale=W_UN).then_inc(act_read, 1)
                if name[0] == "qk":
                    _, i, w, h = name
                    ps = chunk(sec, name)
                    for hd in range(2):
                        r = hd * HEAD_B
                        last = act.activation((QS, KS)[w][r:r + HD, i % 2, hd, cols_of(h)], ps[r:r + HD, :],
                                              ACT.Copy, scale=W_UN)
                    last.then_inc(act_read, 1)
                if name[0] == "oT":
                    act.activation(XB[:, 0, name[1], cols_of(name[2])], chunk(sec, name)[:, :],
                                   ACT.Copy).then_inc(act_read, 1)
                if name[0] == "maxT":
                    ps = chunk(sec, name)
                    if not (isinstance(b, int) and b == 0 and name[1] == 0):
                        act.wait_ge(maxrow_in, b * 32 * PAIRS + 32 * name[1])
                    act.activation(MR[:, :], ps[0:2 * QT, 0:128], ACT.Copy,
                                   scale=-1.0 / MAX_UNIT).then_inc(act_read, 1)

            act.wait_ge(cleared, 1)
            for n in range(START_PIECES):
                split_piece(n)
            act.wait_ge(consts_in, 16 * 9)
            act.wait_ge(half_bias, 1)
            act.wait_ge(gn_shift, 1)
            for t in range(CT):
                normalise(t)
            for t in range(CT):
                bias_residual(t, 0)
            sec, n = start_section(), START_PIECES
            for name in START_NAMES:
                read_chunk(name, sec, 0)
                if name[0] in ("v", "qk") and n < NP:
                    split_piece(n)
                    n += 1

            def batch(b, final):
                sec = before_taps(b)
                for s in range(STEPS):
                    act.wait_ge(scores_full, b * STEPS + s + 1)
                    if s >= 3:
                        act.wait_ge(pv_done, b * STEPS + s - 2)
                    act.activation(P32[:, s % 3, :], ST[s % 2], ACT.Exp, scale=SCALE).then_inc(p_exp, 1)
                    i, s16 = divmod(s, 2 * QT)
                    for name in next_chunks(i, s16):
                        read_chunk(name, sec, b)
                for h in range(2):
                    read_chunk(("oT", CT - 1, h), sec, b)
                act.wait_ge(gn_shift, b * 2 + 2)
                act.wait_ge(border_zero, b + 1)
                for t in range(CT):
                    normalise(t)
                    act.wait_ge(xn_ready, b * 6 + 3 + t + 1)
                    act.activation(XP[:, 0, t, 1:HW + 1, 1:HW + 1],
                                   XN[:, t, :].rearrange("p (h w) -> p h w", w=HW),
                                   ACT.Copy).then_inc(xph_ready, 1)
                for h in range(2):
                    ps = chunk(sec, ("conv", h))
                    act.activation(CV[:, cols_of(h)], ps[:, :], ACT.Copy).then_inc(act_read, 1)
                act.activation(ZHL[:, 0, 0, :], chunk(sec, ("first", "z"))[:, 0:CH], ACT.Copy,
                               scale=W_UN).then_inc(act_read, 1)
                act.wait_ge(dve_read, sec.at(("comb",), "D"))
                act.activation(MSK, chunk(sec, ("comb",))[0:BOTH, :], ACT.Tanh, bias=CBIAS[0:BOTH, 1:2],
                               scale=0.5).then_inc(act_read, 1)

                def hats(ps, h, read_count):
                    d, v = TV[:, 0, cols_of(h)], TV[:, 1, cols_of(h)]
                    act.activation(d, ps[:, :], ACT.Abs, bias=NEG_POS).then_inc(act_read, 1)
                    act.wait_ge(act_read, read_count)
                    act.activation(v, d, ACT.Relu, bias=1.0, scale=-1.0).then_inc(hat_ready, 1)

                for h in range(2):
                    name = ("first", "pos", h)
                    hats(chunk(sec, name), h, sec.at(name, "A"))
                act.wait_ge(reach_known, b + 1)
                for h in range(2):
                    act.activation(HX[:, 0, cols_of(h)], chunk(sec, ("first", "hx", h))[:, :],
                                   ACT.Copy).then_inc(act_read, 1)
                lo, hi = tap_segments(0, 0)[0]
                act.wait_ge(dve_read, sec.at(("first", "hy"), "D"))
                act.activation(MHL[:, 0, 0, 0:hi - lo], M32[:, 0, 0:hi - lo], ACT.Copy).then_inc(m_high, 1)

                far = act.value_load(FAR[0:1, 0:1])

                def taps(sec, end, start, sampled_0, hats_0, reach):
                    for ky in range(KY):
                        for j in range(QT):
                            step = ky * QT + j
                            nj, nky = next_step(ky, j)
                            buf = nj % 2
                            last_tap = end and ky == KY - 1
                            if not (last_tap and j == QT - 1):
                                segs = made_segments(nj, nky, reach)
                                act.wait_ge(sampled, sampled_0 + step)
                                for n, (lo, hi) in enumerate(segs):
                                    o = lo - segs[0][0]
                                    act.wait_ge(dve_read, sec.at(("hy", ky, j, n), "D"))
                                    act.activation(MHL[:, buf, 0, o:o + hi - lo], M32[:, buf, o:o + hi - lo],
                                                   ACT.Copy).then_inc(m_high, 1)
                            kind, h = PREP_AT.get(j, ("", 0))
                            if PREP_READER.get(kind) == "A" and not last_tap:
                                name = ("prep", ky, kind, h)
                                ps = chunk(sec, name)
                                if kind == "pos":
                                    if h == 0:
                                        act.wait_ge(hl_ready, hats_0 + (2 * ky + 2))
                                    hats(ps, h, sec.at(name, "A"))
                                else:
                                    act.activation(HX[:, (ky + 1) % KY, cols_of(h)], ps[:, :],
                                                   ACT.Copy).then_inc(act_read, 1)
                            if not (last_tap and j == QT - 1):
                                act.activation(ZHL[:, buf, 0, :], chunk(sec, ("z", ky, j))[:, 0:CH], ACT.Copy,
                                               scale=W_UN).then_inc(act_read, 1)
                            if start:
                                if step in NORM_AT and NORM_AT[step][0] == 0:
                                    act.wait_ge(gn_shift, b * 2 + 3)
                                for t in NORM_AT.get(step, ()):
                                    normalise(t)
                                for name, _ in start_at(step):
                                    read_chunk(name, sec, b + 1)
                                for t in BIAS_AT.get(step, ()):
                                    bias_residual(t, b + 1)

                def column(sec, kx, end, start):
                    sec = snapped(act, sec)
                    sampled_0 = act.snap(b * PER_SAMPLED + kx * (KY * QT) + 1)
                    hats_0 = act.snap(b * PER_SPLIT_HATS + kx * (2 * KY))
                    by_reach(act, far, lambda reach: taps(sec, end, start, sampled_0, hats_0, reach))
                    return sec

                with act.Fori(0, KX - 1) as kx:
                    column(column_section(b, kx), kx, False, False)
                sec = column(last_column(b, final), KX - 1, True, not final)
                act.wait_ge(sampled, b * PER_SAMPLED + PER_SAMPLED)
                for t in range(CT):
                    act.activation(YS[:, t, HALF:PIX], R6[:, 2 * t + 1, :], ACT.Identity,
                                   bias=BIAS[:, 1, t:t + 1]).then_inc(y_act, 1)
                if final:
                    return
                read_chunk(("maxT", 0), sec, b + 1)
                act.wait_ge(y_act, b * CT + CT)
                act.wait_ge(y_dve, b * CT + CT)
                act.dma_start(y_d[bass.ds(b, 1), :, :].rearrange("a p n -> (a p) n"), YSF).then_inc(y_out, 16)

            if BATCH > 1:
                with act.Fori(0, BATCH - 1) as b:
                    batch(b, False)
            batch(BATCH - 1, True)
            act.wait_ge(bn_ready, 1)
            for k in range(BATCH):
                if k > 0:
                    act.wait_ge(yf_in[k % 4], 16 * ((k - 1) // 4 + 1) if k % 4 else 16 * (k // 4))
                for t in range(CT):
                    y = YF(k)[:, t * PIX:(t + 1) * PIX]
                    act.activation(y, y, ACT.Gelu, bias=BSC[:, 3, t:t + 1], scale=BSC[:, 2, t:t + 1]).then_inc(gelu_done, 1)

        @block.vector
        def _(dve):
            chained = [0, 0]

            def chain_from(base):
                chained[:] = [base, 0]

            def link(ins):
                chained[1] += 1
                ins.then_inc(dve_chain, 1)
                dve.wait_ge(dve_chain, chained[0] + chained[1])

            def expect(name, count):
                if chained[1] != count:
                    raise ValueError(f"{name} is {chained[1]}")

            def chunk(sec, name):
                dve.wait_ge(chunk_full, sec.at(name, "F"))
                return G[sec.bank(name)]

            def split_piece(n):
                dve.wait_ge(w_high, n + 1)
                for k, (hi, lo) in enumerate(pieces[n][2]):
                    last = dve.scalar_tensor_tensor(lo, staged(n, k), W_SCALE, hi, ALU.mult, ALU.subtract)
                last.then_inc(w_low, 1)

            def half_stats(n):
                t, h = divmod(n, 2)
                return dve.bn_stats(ST6[:, n, :], X1[:, t, cols_of(h)])

            def partition_stats(last):
                link(last)
                dve.memset(GM[:, 6:7], 0.0)
                link(dve.bn_aggr(MV[:, :], ST6[:, :, :].rearrange("p a s -> p (a s)")))
                dve.scalar_tensor_tensor(MV[:, 1:2], MV[:, 0:1], MV[:, 0:1], MV[:, 1:2],
                                         ALU.mult, ALU.add).then_inc(gn_stats, 1)

            def group_var(name, sec):
                dve.tensor_copy(GM[:, 0:2], chunk(sec, name)[:, 0:2]).then_inc(dve_read, 1)
                dve.wait_ge(dve_read, sec.at(name, "D"))
                link(dve.scalar_tensor_tensor(GM[:, 2:3], GM[:, 0:1], GM[:, 0:1], GM[:, 1:2],
                                              ALU.mult, ALU.subtract))
                dve.tensor_scalar(GM[:, 3:4], GM[:, 2:3], -1.0, GN_EPS, ALU.mult, ALU.add).then_inc(gn_var, 1)

            def group_shift(count):
                dve.wait_ge(gn_rstd, count)
                dve.scalar_tensor_tensor(GM[:, 5:6], GM[:, 0:1], -1.0, GM[:, 4:5],
                                         ALU.mult, ALU.mult).then_inc(gn_shift, 1)

            def split_x(tile, t, count):
                dve.wait_ge(xn_ready, count)
                link(dve.tensor_copy(tile[:, 0, t, :], XN[:, t, :]))
                dve.tensor_tensor(tile[:, 1, t, :], XN[:, t, :], tile[:, 0, t, :], ALU.subtract).then_inc(x_split, 1)

            def read_chunk(name, sec, b):
                if name[0] == "gn":
                    group_var(name, sec)
                if name[0] == "v":
                    ps = chunk(sec, name)
                    dve.wait_ge(act_read, sec.at(name, "A"))
                    dve.scalar_tensor_tensor(VS[:, name[1], :, 0:HD], ps[:, 0:CH].rearrange("p (h d) -> p h d", d=HD),
                                             W_UN, VS[:, name[1], :, HD:2 * HD],
                                             ALU.mult, ALU.subtract).then_inc(dve_read, 1)
                if name[0] == "qk":
                    _, i, w, h = name
                    ps = chunk(sec, name)
                    dve.wait_ge(act_read, sec.at(name, "A"))

                    def repeat_k():
                        for hd in range(2):
                            r = hd * HEAD_B
                            dve.tensor_copy(KS[HEAD_B - r:HEAD_B - r + HD, i % 2, hd, cols_of(h)],
                                            KS[r:r + HD, i % 2, hd, cols_of(h)])

                    if w == 1 and h == 1:
                        repeat_k()
                    for hd in range(2):
                        r = hd * HEAD_B
                        o = (HEAD_B - r, r)[w]
                        high, low = (QS, KS)[w], (QS, KL)[w]
                        last = dve.scalar_tensor_tensor(low[o:o + HD, i % 2, hd, cols_of(h)], ps[r:r + HD, :], W_UN,
                                                        high[r:r + HD, i % 2, hd, cols_of(h)], ALU.mult, ALU.subtract)
                    last.then_inc(dve_read, 1)
                    if w == 1 and h == 0:
                        repeat_k()
                if name[0] == "oT":
                    _, t, h = name
                    ps = chunk(sec, name)
                    dve.wait_ge(act_read, sec.at(name, "A"))
                    dve.tensor_tensor(XB[:, 1, t, cols_of(h)], ps[:, :], XB[:, 0, t, cols_of(h)],
                                      ALU.subtract).then_inc(dve_read, 1)
                if name[0] == "max":
                    n = name[2]
                    dve.reduce_max(MXP[:, n // 2, n % 2:n % 2 + 1], chunk(sec, name)[:, :], AX.X).then_inc(dve_read, 1)
                    if n == 4 * QT - 1:
                        dve.wait_ge(dve_read, sec.at(name, "D"))
                        dve.reduce_max(MX[:, :], MXP[:, :, :], AX.X).then_inc(max_ready, 1)

            dve.wait_ge(cleared, 1)
            for n in range(START_PIECES):
                split_piece(n)
            dve.wait_ge(consts_in, 16 * 9)
            dve.tensor_scalar_mul(CBIAS[:, 1:2], CBIAS[:, 0:1], 0.5).then_inc(half_bias, 1)
            chain_from(0)
            dve.wait_ge(x_in, 16)
            for n in range(6):
                last = half_stats(n)
            partition_stats(last)
            sec, n = start_section(), START_PIECES
            read_chunk(("gn", 0), sec, 0)
            group_shift(1)
            for t in range(CT):
                split_x(XA, t, t + 1)
            for name in START_NAMES[1:]:
                read_chunk(name, sec, 0)
                if name[0] in ("v", "qk") and n < NP:
                    split_piece(n)
                    n += 1
            expect("START_LINKS", START_LINKS)

            def batch(b, final):
                chain_from(b * PER_LINKS + START_LINKS)
                sec = before_taps(b)
                for s in range(STEPS + 2):
                    i, s16 = divmod(s, 2 * QT)
                    if s < STEPS:
                        for name in next_chunks(i, s16):
                            read_chunk(name, sec, b)
                    if s in DVE_STEPS:
                        dve.wait_ge(p_exp, b * STEPS + s + 1)
                        dve.tensor_tensor(PL[:, s % 3, :], P32[:, s % 3, :], high_view(s),
                                          ALU.subtract).then_inc(p_low_dve, 1)
                    if s >= 2 and (s - 2) % QT == QT - 1:
                        head = (s - 2) // QT
                        dve.wait_ge(pv_done, b * STEPS + s - 1)
                        link(dve.reciprocal(ORS[:, :], O[head % 2][:, :, HD]))
                        dve.tensor_tensor(ON[:, :, head * HD:(head + 1) * HD], O[head % 2][:, :, 0:HD],
                                          ORS[:, :].unsqueeze(2).to_broadcast([128, QT, HD]),
                                          ALU.mult).then_inc(o_norm, 1)
                for h in range(2):
                    read_chunk(("oT", CT - 1, h), sec, b)
                dve.wait_ge(x_biased, b * 3 + 3)
                for n in range(6):
                    t, h = divmod(n, 2)
                    dve.scalar_tensor_tensor(X1[:, t, cols_of(h)], chunk(sec, ("proj", t, h))[:, :], W_UN,
                                             X1[:, t, cols_of(h)], ALU.mult, ALU.add).then_inc(dve_read, 1)
                    dve.wait_ge(dve_read, sec.at(("proj", t, h), "D"))
                    last = half_stats(n)
                partition_stats(last)
                group_var(("gn", 1), sec)
                group_shift(b * 2 + 2)
                dve.wait_ge(border_zero, b + 1)
                for t in range(CT):
                    split_x(XB, t, b * 6 + 3 + t + 1)
                    dve.wait_ge(x_split, b * 6 + 3 + t + 1)
                    dve.tensor_copy(XP[:, 1, t, 1:HW + 1, 1:HW + 1],
                                    XB[:, 1, t, :].rearrange("p (h w) -> p h w", w=HW)).then_inc(xpl_ready, 1)

                def split_z(buf, name, sec):
                    dve.wait_ge(act_read, sec.at(name, "A"))
                    dve.scalar_tensor_tensor(ZHL[:, buf, 1, :], G[sec.bank(name)][:, 0:CH], W_UN, ZHL[:, buf, 0, :],
                                             ALU.mult, ALU.subtract).then_inc(dve_read, 1)

                split_z(0, ("first", "z"), sec)
                dve.tensor_scalar(CLIP, chunk(sec, ("comb",))[0:BOTH, :], CBIAS[0:BOTH, 0:1], -float(MAX_OFF),
                                  ALU.add, ALU.max).then_inc(dve_read, 1)
                dve.wait_ge(dve_read, sec.at(("comb",), "D"))
                link(dve.tensor_scalar(CLIP, CLIP, float(MAX_OFF), IS_POS[0:BOTH, :], ALU.min, ALU.mult))
                dve.wait_ge(act_read, sec.at(("comb",), "A"))
                link(dve.scalar_tensor_tensor(CLIP, MSK, IS_MASK[0:BOTH, :], CLIP, ALU.mult, ALU.add))
                for h in range(2):
                    half, cols = CLIP[h * HEAD_B:h * HEAD_B + OFF_CH, :], cols_of(h)
                    link(dve.tensor_copy(POSS[0:OFF_CH, cols], half))
                    dve.tensor_tensor(POSS[LO_ROW:LO_ROW + OFF_CH, cols], half, POSS[0:OFF_CH, cols],
                                      ALU.subtract).then_inc(pos_ready, 1)
                dve.tensor_reduce(RMX[0:BOTH, :], CLIP, AX.X, ALU.max,
                                  apply_absolute_value=True).then_inc(rows_max, 1)

                def mask_hats(ps, h, hat_count):
                    v = TV[:, 1, cols_of(h)]
                    dve.wait_ge(hat_ready, hat_count)
                    dve.tensor_tensor(v, ps[:, :], v, ALU.mult).then_inc(dve_read, 1)

                for h in range(2):
                    name = ("first", "mask", h)
                    mask_hats(chunk(sec, name), h, b * PER_HATS + h + 1)
                    dve.wait_ge(dve_read, sec.at(name, "D"))
                    link(dve.tensor_tensor(H16[:, cols_of(h)], TV[:, 1, cols_of(h)],
                                           IS_LO.to_broadcast([128, HALF]), ALU.mult))
                    dve.tensor_tensor(HL[:, 0, cols_of(h)], TV[:, 1, cols_of(h)], H16[:, cols_of(h)],
                                      ALU.subtract).then_inc(first_hats, 1)
                dve.reduce_max(FMX[:, 0:1], chunk(sec, ("reach",))[0:1, 0:128], AX.X).then_inc(dve_read, 1)
                dve.wait_ge(dve_read, sec.at(("reach",), "D"))
                dve.tensor_scalar(FAR[:, 0:1], FMX[:, 0:1], NEAR_OFF - 2.0 ** -6, 0.0,
                                  ALU.is_gt, ALU.add).then_inc(reach_known, 1)
                dve.wait_ge(reach_known, b + 1)
                dve.wait_ge(act_read, sec.at(("first", "hx", 1), "A"))
                lo, hi = tap_segments(0, 0)[0]
                dve.tensor_tensor(M32[:, 0, 0:hi - lo], chunk(sec, ("first", "hy"))[:, 0:hi - lo], HX[:, 0, lo:hi],
                                  ALU.mult).then_inc(dve_read, 1)
                expect("BATCH_LINKS", BATCH_LINKS)
                far = dve.value_load(FAR[0:1, 0:1])

                def taps(sec, end, start, seg, hats_0, links_0, reach):
                    chain_from(links_0)
                    before, made = 0, 0
                    for ky in range(KY):
                        for j in range(QT):
                            step = ky * QT + j
                            nj, nky = next_step(ky, j)
                            buf = nj % 2
                            last_tap = end and ky == KY - 1
                            if not (last_tap and j == QT - 1):
                                if j == QT - 1:
                                    dve.wait_ge(act_read, sec.at(("prep", ky, "hx", 1), "A"))
                                segs = made_segments(nj, nky, reach)
                                if (ky, j) != (0, 0):
                                    dve.wait_ge(m_low, seg + before)
                                before, made = made, made + len(segs)
                                for n, (lo, hi) in enumerate(segs):
                                    o = lo - segs[0][0]
                                    dve.tensor_tensor(M32[:, buf, o:o + hi - lo],
                                                      chunk(sec, ("hy", ky, j, n))[:, 0:hi - lo],
                                                      HX[:, nky, lo:hi], ALU.mult).then_inc(dve_read, 1)
                            kind, h = PREP_AT.get(j, ("", 0))
                            if PREP_READER.get(kind) == "D" and not last_tap:
                                name = ("prep", ky, kind, h)
                                mask_hats(chunk(sec, name), h, hats_0 + (2 * ky + h + 1))
                            if not (last_tap and j == QT - 1):
                                split_z(buf, ("z", ky, j), sec)
                            if start:
                                if step == 0:
                                    dve.wait_ge(x_in, b * 16 + 32)
                                for n in STATS_AT.get(step, ()):
                                    last = half_stats(n)
                                    if n == 5:
                                        partition_stats(last)
                                if step == SHIFT_AT:
                                    group_shift(b * 2 + 3)
                                for t in SPLIT_AT.get(step, ()):
                                    split_x(XA, t, b * 6 + 6 + t + 1)
                                for name, _ in start_at(step):
                                    read_chunk(name, sec, b + 1)

                def column(sec, kx, end, start):
                    sec = snapped(dve, sec)
                    seg = dve.snap(b * PER_SEGS + kx * COLUMN_SEGS + FIRST_SEGS)
                    hats_0 = dve.snap(b * PER_HATS + kx * (2 * KY) + 2)
                    links_0 = dve.snap(b * PER_LINKS + (START_LINKS + BATCH_LINKS))
                    by_reach(dve, far, lambda reach: taps(sec, end, start, seg, hats_0, links_0, reach))

                with dve.Fori(0, KX - 1) as kx:
                    column(column_section(b, kx), kx, False, False)
                column(last_column(b, final), KX - 1, True, not final)
                expect("START_LINKS", 0 if final else START_LINKS)

                dve.wait_ge(sampled, b * PER_SAMPLED + PER_SAMPLED)
                for t in range(CT):
                    dve.tensor_scalar_add(YS[:, t, 0:HALF], R6[:, 2 * t, :], BIAS[:, 1, t:t + 1]).then_inc(y_dve, 1)
                for h in range(2):
                    for t in range(CT):
                        dve.wait_ge((y_dve, y_act)[h], b * CT + (t + 1))
                        last = dve.bn_stats(BST[:, t, bass.ds(b * 2 + h, 1), :].rearrange("p a s -> p (a s)"),
                                            YS[:, t, cols_of(h)])
                last.then_inc(y_stats, 1)


            if BATCH > 1:
                with dve.Fori(0, BATCH - 1) as b:
                    batch(b, False)
            batch(BATCH - 1, True)
            dve.wait_ge(y_stats, BATCH)
            chain_from(BATCH * PER_LINKS)
            for t in range(CT):
                last = dve.bn_aggr(BMV[:, t, :], BST[:, t, :, :].rearrange("p a s -> p (a s)"))
            link(last)
            dve.tensor_scalar_add(BSC[:, 0, :], BMV[:, :, 1], BN_EPS).then_inc(bn_var, 1)
            dve.wait_ge(bn_rstd, 1)
            link(dve.tensor_tensor(BSC[:, 2, :], BSC[:, 1, :], BIAS[:, 2, :], ALU.mult))
            link(dve.tensor_tensor(BSC[:, 0, :], BMV[:, :, 0], BSC[:, 2, :], ALU.mult))
            dve.tensor_tensor(BSC[:, 3, :], BIAS[:, 3, :], BSC[:, 0, :], ALU.subtract).then_inc(bn_ready, 1)
            for k in range(BATCH):
                if k > 0:
                    dve.wait_ge(xf_in[k % 3], 16 * ((k - 1) // 3 + 1) if k % 3 else 16 * (k // 3))
                for t in range(CT):
                    y = YF(k)[:, t * PIX:(t + 1) * PIX]
                    dve.wait_ge(gelu_done, k * CT + t + 1)
                    last = dve.tensor_tensor(y, y, XF(k)[:, t * PIX:(t + 1) * PIX], ALU.add)
                last.then_inc(added, 1)

        @block.tensor
        def _(pe):
            def bank(sec, name):
                for w, count in sec.replaced(name):
                    pe.wait_ge(count_of[w], count)
                return G[sec.bank(name)]

            def products(out, operands):
                for n, (l, r) in enumerate(operands):
                    last = pe.matmul(out, l, r, start=(n == 0), stop=(n == len(operands) - 1))
                return last

            def group_mean(name, sec, count):
                pe.wait_ge(gn_stats, count)
                pe.matmul(bank(sec, name)[:, 0:2], GMAT, MV[:, :], start=True, stop=True).then_inc(chunk_full, 1)

            def z_products(out, j, high, low):
                products(out[:, 0:CH],
                         [(XB[:, xp_, t, j * 128:(j + 1) * 128], (high, low)[wp_](t))
                          for t in range(CT) for xp_, wp_ in ((0, 0), (0, 1), (1, 0))]).then_inc(chunk_full, 1)

            def fill_chunk(name, sec, b):
                if name in (("v", 0), ("qk", 0, 0, 0)):
                    pe.wait_ge(x_split, b * 6 + 3)
                if name[0] == "gn":
                    group_mean(name, sec, b * 2 + 1)
                if name[0] == "v":
                    n = name[1]
                    v_w = [WALL[:, WVO + a * TAPW:WVO + (a + 1) * TAPW].rearrange("p (t c) -> p t c", t=CT)
                           for a in range(2)]
                    products(bank(sec, name)[:, 0:CH],
                             [(XA[:, xp_, t, n * 128:(n + 1) * 128], v_w[wp_][:, t, :])
                              for t in range(CT) for xp_, wp_ in ((0, 0), (0, 1), (1, 0))]).then_inc(chunk_full, 1)
                if name[0] == "qk":
                    _, i, w, h = name
                    products(bank(sec, name)[0:PAIR_ROWS, :],
                             [(WQK[:, wp_, t, 2 * i + w, :], XA[:, xp_, t, cols_of(h)])
                              for t in range(CT) for wp_, xp_ in ((0, 0), (0, 1), (1, 0))]).then_inc(chunk_full, 1)
                if name[0] == "max":
                    _, i, n = name
                    hd, q, h = n // (2 * QT), n // 2 % QT, n % 2
                    if n == 0:
                        pe.wait_ge(dve_read, sec.at(("qk", i, 1, 1), "D"))
                    pe.matmul(bank(sec, name)[:, :], QS[0:PAIR_ROWS, i % 2, hd, q * 128:(q + 1) * 128],
                              KS[0:PAIR_ROWS, i % 2, hd, cols_of(h)], start=True, stop=True).then_inc(chunk_full, 1)
                if name[0] == "oT":
                    _, t, h = name
                    if h == 0:
                        pe.wait_ge(o_norm, b * HEADS + ((t + 1) * 128 + HD - 1) // HD)
                    out = bank(sec, name)
                    for q in range(4):
                        last = pe.transpose(out[:, q * 128:(q + 1) * 128], ON[:, 4 * h + q, t * 128:(t + 1) * 128],
                                            IDENT)
                    last.then_inc(chunk_full, 1)
                if name[0] == "maxT":
                    pe.wait_ge(max_ready, b * PAIRS + name[1] + 1)
                    pe.transpose(bank(sec, name)[0:2 * QT, 0:128], MX[:, :], IDENT).then_inc(chunk_full, 1)

            pe.wait_ge(cleared, 1)
            pe.wait_ge(w_low, START_PIECES)
            pe.wait_ge(consts_in, 16 * 9)
            pe.wait_ge(maxunit_in, 16 * 4)
            sec = start_section()
            for name in START_NAMES:
                fill_chunk(name, sec, 0)
            pe.wait_ge(w_low, NP)

            def batch(b, final):
                sec = before_taps(b)

                def pv(s, first, count):
                    head, kt = divmod(s, QT)
                    if first == 0:
                        if s in POOL_STEPS:
                            pe.wait_ge(p_low_pool, b * len(POOL_STEPS) + POOL_STEPS.index(s) + 1)
                        else:
                            pe.wait_ge(p_low_dve, b * len(DVE_STEPS) + DVE_STEPS.index(s) + 1)
                        if kt == 0 and head > 1:
                            pe.wait_ge(o_norm, b * HEADS + head - 1)
                    for q in range(first, first + count):
                        out, pixels = O[head % 2][:, q, :], slice(q * 128, (q + 1) * 128)
                        pe.matmul(out, high_view(s)[:, pixels], VS[:, kt, head, HD:VCOL],
                                  start=(kt == 0 and q == 0), stop=False, skip_group_check=True)
                        pe.matmul(out[:, 0:HD], high_view(s)[:, pixels], VS[:, kt, head, 0:HD],
                                  start=False, stop=False, skip_group_check=True)
                        last = pe.matmul(out, PL[:, s % 3, pixels], VS[:, kt, head, HD:VCOL],
                                         start=False, stop=(kt == QT - 1), skip_group_check=True)
                    if first + count == QT:
                        last.then_inc(pv_done, 1)

                for s in range(STEPS + 2):
                    i, s16 = divmod(s, 2 * QT)
                    chunks = []
                    if s < STEPS:
                        hd, kt = divmod(s16, QT)
                        chunks = next_chunks(i, s16)
                        if s16 == 0:
                            pe.wait_ge(maxrow_in, b * 32 * PAIRS + 32 * (i + 1))
                        if s >= 2:
                            pe.wait_ge(p_exp, b * STEPS + s - 1)
                        for h in range(2):
                            if h == 1 and chunks and chunks[0][0] == "max":
                                fill_chunk(chunks.pop(0), sec, b)
                            out = ST[s % 2][:, cols_of(h)]
                            pe.matmul(out, KS[0:PAIR_ROWS, i % 2, hd, kt * 128:(kt + 1) * 128],
                                      QS[0:PAIR_ROWS, i % 2, hd, cols_of(h)], start=True, stop=False)
                            last = pe.matmul(out, KL[0:PAIR_ROWS, i % 2, hd, kt * 128:(kt + 1) * 128],
                                             QS[0:PAIR_ROWS, i % 2, hd, cols_of(h)], start=False, stop=True)
                        last.then_inc(scores_full, 1)
                    for k in range(4):
                        if k % 2 == 0 and chunks:
                            fill_chunk(chunks.pop(0), sec, b)
                        if s >= 2:
                            pv(s - 2, 2 * k, 2)
                    for name in chunks:
                        fill_chunk(name, sec, b)

                for h in range(2):
                    fill_chunk(("oT", CT - 1, h), sec, b)
                pe.wait_ge(dve_read, sec.at(("oT", CT - 1, 1), "D"))
                for t in range(CT):
                    for h in range(2):
                        products(bank(sec, ("proj", t, h))[:, :],
                                 [(WP[:, wp_, k, t * 128:(t + 1) * 128], XB[:, xp_, k, cols_of(h)])
                                  for k in range(CT) for wp_, xp_ in ((0, 0), (0, 1), (1, 0))]).then_inc(chunk_full, 1)
                group_mean(("gn", 1), sec, b * 2 + 2)

                outs = [bank(sec, ("conv", h)) for h in range(2)]
                shifts = [(t, kx, ky) for t in range(CT) for kx in range(KX) for ky in range(KY)]
                for a, ready, w_parts in ((0, xph_ready, 2), (1, xpl_ready, 1)):
                    for h in range(2):
                        m = a * 2 * len(shifts)
                        for t, kx, ky in shifts:
                            if h == 0 and (kx, ky) == (0, 0):
                                pe.wait_ge(ready, b * 3 + t + 1)
                            for part in range(w_parts):
                                row, r = h * (HW // 2) + ky, m % CONV_TILES * LO_ROW
                                last = pe.matmul(outs[h][r:r + OFF_CH, :],
                                                 WC[:, t * TAPS + kx * KY + ky, part * OFF_CH:(part + 1) * OFF_CH],
                                                 XP[:, a, t, row:row + HW // 2, kx:kx + HW],
                                                 start=(m < CONV_TILES), stop=(m >= 3 * len(shifts) - CONV_TILES))
                                m += 1
                        if a == 1:
                            last.then_inc(chunk_full, 1)
                z_products(bank(sec, ("first", "z")), 0, lambda t: WALL[:, WDH + t * CH:WDH + (t + 1) * CH],
                           lambda t: WALL[:, WDL + t * CH:WDL + (t + 1) * CH])
                out = bank(sec, ("comb",))
                for h, (lo, hi) in enumerate(((0, HEAD_B), (HEAD_B, BOTH))):
                    pe.wait_ge(act_read, sec.at(("conv", h), "A"))
                    last = pe.matmul(out[lo:hi, :], CMB[:, 0:hi - lo], CV[:, cols_of(h)], start=True, stop=True)
                last.then_inc(chunk_full, 1)

                for k in range(6):
                    last = pe.matmul(R6[:, k, :], SEL[:, ZERO, :], SELF[:, 0:HALF], start=True, stop=False,
                                     skip_group_check=True)
                last.then_inc(sampled, 1)

                for kind, sel in (("pos", SELP), ("mask", SELM)):
                    for h in range(2):
                        if kind == "pos":
                            pe.wait_ge(pos_ready, b * 2 + h + 1)
                        pe.matmul(bank(sec, ("first", kind, h))[:, :], SEL[:, sel, :], POSS[:, cols_of(h)],
                                  start=True, stop=True).then_inc(chunk_full, 1)
                pe.wait_ge(rows_max, b + 1)
                pe.transpose(bank(sec, ("reach",))[0:1, 0:128], RMX[:, :], IDENT).then_inc(chunk_full, 1)
                for h in range(2):
                    pe.wait_ge(first_hats, b * 2 + h + 1)
                    pe.matmul(bank(sec, ("first", "hx", h))[:, :], SEL[:, SELX, :], HL[:, 0, cols_of(h)],
                              start=True, stop=True).then_inc(chunk_full, 1)
                lo, hi = tap_segments(0, 0)[0]
                pe.wait_ge(reach_known, b + 1)
                pe.matmul(bank(sec, ("first", "hy"))[:, 0:hi - lo], SEL[:, SELY, :], HL[:, 0, lo:hi],
                          start=True, stop=True).then_inc(chunk_full, 1)
                far = pe.value_load(FAR[0:1, 0:1])

                def taps(sec, kx, end, start, seg, hats_0, reach):
                    made = 0
                    z_high, z_low = sec.base["A"], sec.base["D"]
                    for ky in range(KY):
                        for j in range(QT):
                            step = ky * QT + j
                            nj, nky = next_step(ky, j)
                            buf = j % 2
                            last_tap = end and ky == KY - 1
                            has_next = not (last_tap and j == QT - 1)
                            now = tap_segments(j, ky, reach)
                            segs = made_segments(nj, nky, reach) if has_next else []

                            def y_hats(n):
                                lo, hi = segs[n]
                                pe.matmul(bank(sec, ("hy", ky, j, n))[:, 0:hi - lo], SEL[:, SELY + nj, :],
                                          HL[:, nky, lo:hi], start=True, stop=True).then_inc(chunk_full, 1)

                            def sample(z_part, m_part, tiles=range(CT)):
                                for t in tiles:
                                    for lo, hi in now:
                                        o = lo - now[0][0]
                                        bk = 2 * t + lo // HALF
                                        last = pe.matmul(R6[:, bk, lo % HALF:lo % HALF + hi - lo],
                                                         ZHL[:, buf, z_part, t * 128:(t + 1) * 128],
                                                         MHL[:, buf, m_part, o:o + hi - lo],
                                                         start=False, stop=False, skip_group_check=True)
                                return last

                            if j == QT - 1 and has_next:
                                pe.wait_ge(hl_ready, hats_0 + (2 * ky + 2))
                            if segs:
                                y_hats(0)
                            pe.wait_ge(m_high, seg + made)
                            pe.wait_ge(act_read, z_high)
                            sample(0, 0)
                            if len(segs) == 2:
                                y_hats(1)
                            early = range(0)
                            if j in PREP_AT and not last_tap:
                                if len(segs) == 2:
                                    pe.wait_ge(m_low, seg + made)
                                    early = range(CT - 1)
                                    sample(0, 1, early)
                                kind, h = PREP_AT[j]
                                if kind == "hx":
                                    pe.wait_ge(hl_ready, hats_0 + (2 * ky + h + 1))
                                    lhs, rhs = SEL[:, SELX, :], HL[:, (ky + 1) % KY, cols_of(h)]
                                else:
                                    sel = (SELP if kind == "pos" else SELM) + ky + 1
                                    lhs, rhs = SELF[:, bass.ds(kx * (KY * 128) + sel * 128, 128)], POSS[:, cols_of(h)]
                                pe.matmul(bank(sec, ("prep", ky, kind, h))[:, :], lhs, rhs,
                                          start=True, stop=True).then_inc(chunk_full, 1)
                            z_before = z_low
                            if has_next:
                                name = ("z", ky, j)
                                tap = kx * (KY * TAPW) + (ky + (j == QT - 1)) * TAPW
                                z_products(bank(sec, name), nj,
                                           lambda t: WALL[:, bass.ds(tap + (WDH + t * CH), CH)],
                                           lambda t: WALL[:, bass.ds(tap + (WDL + t * CH), CH)])
                                z_high, z_low = sec.at(name, "A"), sec.at(name, "D")
                            if not early:
                                pe.wait_ge(m_low, seg + made)
                            sample(0, 1, range(len(early), CT))
                            pe.wait_ge(dve_read, z_before)
                            beside = [name for name, _ in start_at(step)] if start else []
                            for t in range(CT):
                                last = sample(1, 0, [t])
                                if t < CT - 1 and t < len(beside):
                                    fill_chunk(beside[t], sec, b + 1)
                            for name in beside[CT - 1:]:
                                fill_chunk(name, sec, b + 1)
                            last.then_inc(sampled, 1)
                            made += len(segs)

                def column(sec, kx, end, start):
                    sec = snapped(pe, sec)
                    seg = pe.snap(b * PER_SEGS + kx * COLUMN_SEGS + FIRST_SEGS)
                    hats_0 = pe.snap(b * PER_SPLIT_HATS + kx * (2 * KY) + 2)
                    by_reach(pe, far, lambda reach: taps(sec, kx, end, start, seg, hats_0, reach))
                    return sec

                with pe.Fori(0, KX - 1) as kx:
                    column(column_section(b, kx), kx, False, False)
                sec = column(last_column(b, final), KX - 1, True, not final)
                if final:
                    return
                fill_chunk(("maxT", 0), sec, b + 1)
                pe.wait_ge(y_act, b * CT + CT)
                pe.wait_ge(y_dve, b * CT + CT)

            if BATCH > 1:
                with pe.Fori(0, BATCH - 1) as b:
                    batch(b, False)
            batch(BATCH - 1, True)


def shape_constants():
    m = np.arange(128)
    sel = np.zeros((128, 2 * TAPS + QT + 2, 128), np.float16)
    for i in range(TAPS):
        for r in (0, LO_ROW, GRID_ROW):
            sel[r + i, i, 0:64] = 1
            sel[r + TAPS + i, i, 64:128] = 1
            if r < GRID_ROW:
                sel[r + 2 * TAPS + i, TAPS + i, 64:128] = 1
        sel[ONES_ROW, TAPS + i, :] = 1
    for j in range(QT):
        y = TILE_ROWS * j + m // HW
        sel[y, 2 * TAPS + j, m] = 1
        sel[32 + y, 2 * TAPS + j, m] = 1
    for r in (64, 96):
        sel[r + m % HW, 2 * TAPS + QT, m] = 1
    grid = np.zeros((2 * TAPS + 2, HW, HW), np.float16)
    for i in range(TAPS):
        kx, ky = divmod(i, KY)
        grid[i] = (np.arange(HW) - 1 + ky)[:, None]
        grid[TAPS + i] = (np.arange(HW) - 1 + kx)[None, :]
    grid[2 * TAPS] = 1
    grid[2 * TAPS + 1] = MAX_UNIT
    c32 = np.zeros((128, 128 + 128 + HEAD_B + 5), np.float32)
    c32[:, 0:128] = np.eye(128)
    per = 128 // GN_GROUPS
    c32[:, 128:256] = np.kron(np.eye(GN_GROUPS), np.full((per, per), 1.0 / per))
    for r in range(OFF_CH):
        c32[[n * LO_ROW + r for n in range(CONV_TILES)], 256 + r] = W_UN
    col = 256 + HEAD_B
    c32[:, col] = m % HEAD_B < 2 * TAPS
    c32[:, col + 1] = (m % HEAD_B >= 2 * TAPS) & (m % HEAD_B < OFF_CH)
    c32[:, col + 2] = -(m % 32)
    c32[:, col + 3] = m // 32 % 2
    c32[:, col + 4] = -0.5
    return sel.reshape(128, -1), grid.reshape(2 * TAPS + 2, -1), c32


def kernel(x, L0_conv_w_qkv, L0_conv_w_proj, L0_conv_b_proj, L1_conv_proj_w, L1_conv_proj_b, L1_conv_off_w,
           L1_conv_off_b, L1_conv_mask_w, L1_conv_mask_b, L1_conv_gamma, L1_conv_beta):
    import concourse.bacc as bacc
    from concourse.bass_utils import run_bass_kernel_spmd

    x = np.asarray(x)
    qkv = np.asarray(L0_conv_w_qkv).reshape(3, PAIRS, 2, HD, PART, CT)
    per_channel = lambda a: np.asarray(a).reshape(PART, CT)
    off = np.asarray(L1_conv_off_w).reshape(3, 3, 2, CH, 3, 3).transpose(2, 1, 0, 3, 4, 5).reshape(2 * TAPS, CH, 3, 3)
    mask = np.asarray(L1_conv_mask_w).reshape(3, 3, CH, 3, 3).transpose(1, 0, 2, 3, 4).reshape(TAPS, CH, 3, 3)
    wc = np.concatenate([off, mask], 0).reshape(OFF_CH, PART, CT, 3, 3).transpose(1, 2, 4, 3, 0)
    off_b = np.asarray(L1_conv_off_b).reshape(3, 3, 2).transpose(2, 1, 0).reshape(-1)
    mask_b = np.asarray(L1_conv_mask_b).reshape(3, 3).T.reshape(-1)
    c16, grid, c32 = shape_constants()
    arrays = {
        "x": x.reshape(BATCH, PART, CT * PIX),
        "wqk": qkv[0:2].transpose(4, 5, 1, 0, 2, 3).reshape(PART, -1),
        "wv": np.asarray(L0_conv_w_qkv).reshape(3, CH, PART, CT)[2].transpose(1, 2, 0).reshape(PART, -1),
        "wp": np.asarray(L0_conv_w_proj).reshape(PART, CT, CT, PART).transpose(3, 2, 1, 0).reshape(PART, -1),
        "wd": np.asarray(L1_conv_proj_w).reshape(PART, CT, PART, CT, 3, 3).transpose(2, 5, 4, 3, 1, 0).reshape(PART, -1),
        "wc": wc.reshape(PART, -1),
        "bias_p": per_channel(L0_conv_b_proj),
        "bias_c": np.concatenate([off_b, mask_b])[:, None],
        "bias_d": per_channel(L1_conv_proj_b),
        "gamma": per_channel(L1_conv_gamma),
        "beta": per_channel(L1_conv_beta),
        "c16": c16,
        "grid": grid,
        "c32": c32,
    }
    arrays = {k: np.ascontiguousarray(v) for k, v in arrays.items()}
    nc = bacc.Bacc("TRN2", target_bir_lowering=False, num_devices=1)
    args = [nc.dram_tensor(k, v.shape, mybir.dt.from_np(v.dtype), kind="ExternalInput").ap() for k, v in arrays.items()]
    shape = [BATCH, PART, CT * PIX]
    out = nc.dram_tensor("out", shape, mybir.dt.float32, kind="ExternalOutput").ap()
    x1_d = nc.dram_tensor("x1_scratch", shape, mybir.dt.float32, kind="Internal").ap()
    y_d = nc.dram_tensor("y_scratch", shape, mybir.dt.float32, kind="Internal").ap()
    build(nc, *args, out, x1_d, y_d)
    r = run_bass_kernel_spmd(nc, [arrays], core_ids=[0])
    return r.results[0]["out"].reshape(BATCH, CH, HW, HW)
```
